# Optimizing a Trainium2 kernel written in Bass

```python
import numpy as np
import jax
import jax.numpy as jnp

def _softmax(x, axis=-1):
    return jax.nn.softmax(x, axis=axis)

def _gelu(x):
    return jax.nn.gelu(x, approximate=True)

def _silu(x):
    return jax.nn.silu(x)

def _sigmoid(x):
    return jax.nn.sigmoid(x)

def _layernorm(x, axis=-1, eps=1e-05):
    m = jnp.mean(x, axis=axis, keepdims=True)
    v = jnp.var(x, axis=axis, keepdims=True)
    return (x - m) / jnp.sqrt(v + eps)

def _scatter_add(tgt, idx, src, axis=0):
    return tgt.at[idx].add(src)

def _segment_sum(src, seg, n):
    return jax.ops.segment_sum(src, seg, n)
kernel_name = 'mk_flamingo_gated_d4_seqx_r4_60af94'

def setup_inputs(seed: int=0):
    np.random.seed(seed)
    _w = jnp.asarray

    def _rec_inputs():
        import jax
        import jax.numpy as jnp
        _rk = jax.random.key(seed)
        x = 7.22e-05 + 1 * jax.random.normal(jax.random.fold_in(_rk, 1), (8, 256, 256), jnp.float32)
        _lenS = 256 - jax.random.randint(jax.random.fold_in(_rk, 7), (8,), 0, max(1, 256 // 4) + 1, jnp.int32)
        _lenS2 = 256 - jax.random.randint(jax.random.fold_in(_rk, 8), (8,), 0, max(1, 256 // 4) + 1, jnp.int32)
        _ctx_1024P = jax.random.normal(jax.random.fold_in(_rk, 11), (8, 16, 256), jnp.float32)
        _ctx_1024c = jax.random.dirichlet(jax.random.fold_in(_rk, 511), 0.3 * jnp.ones((16,), jnp.float32), (8, 256))
        _ctx_1024t = jnp.einsum('bsk,bkd->bsd', _ctx_1024c, _ctx_1024P)
        _ctx_1024t = _ctx_1024t * jax.lax.rsqrt(jnp.mean(jnp.square(_ctx_1024t)) + 1e-12) * 0.953939
        ctx_1024 = 4.13588e-05 + 0.999923 * (_ctx_1024t + 0.3 * jax.random.normal(jax.random.fold_in(_rk, 611), (8, 256, 256), jnp.float32))
        _validS = jnp.arange(256)[None, :] < _lenS[:, None]
        _validS2 = jnp.arange(256)[None, :] < _lenS2[:, None]
        _causal = jnp.tril(jnp.ones((256, 256), dtype=bool))
        mask_Bx1xSxS2_bf0 = jnp.logical_not(jnp.ones((8, 1, 256, 256), dtype=bool))
        mask_Bx1xS2_ik1 = jnp.where(jnp.broadcast_to(_validS2[:, None, :], (8, 1, 256)), 1, 0).astype(jnp.int32)
        _g = jax.random.normal(jax.random.fold_in(_rk, 9001), (2, 4), jnp.float32)
        _g = jnp.sign(_g) * jnp.maximum(jnp.abs(_g), 1.0) + (_g == 0) * 1.0
        g_xattn = _g[0]
        g_ffn = _g[1]
        return (x, ctx_1024, mask_Bx1xSxS2_bf0, mask_Bx1xS2_ik1, g_xattn, g_ffn)
    x, ctx_1024, mask_Bx1xSxS2_bf0, mask_Bx1xS2_ik1, g_xattn, g_ffn = _rec_inputs()

    def _L0_xattn_setup():
        import jax, jax.numpy as jnp
        import numpy as np
        D = 256
        H = 16
        HD = D // H

        def _split_heads(x):
            B, S, _ = x.shape
            return x.reshape(B, S, H, HD).transpose(0, 2, 1, 3)
        key = jax.random.key(seed)
        ks = jax.random.split(key, 11)
        B, S = (4, 512)
        scale = 1.0 / np.sqrt(D)
        inp = {'query': jax.random.normal(ks[0], (B, S, D), jnp.float32), 'key': jax.random.normal(ks[1], (B, S, D), jnp.float32), 'value': jax.random.normal(ks[2], (B, S, D), jnp.float32), 'Wq': jax.random.normal(ks[3], (D, D), jnp.float32) * scale, 'bq': jnp.zeros((D,), jnp.float32), 'Wk': jax.random.normal(ks[4], (D, D), jnp.float32) * scale, 'bk': jnp.zeros((D,), jnp.float32), 'Wv': jax.random.normal(ks[5], (D, D), jnp.float32) * scale, 'bv': jnp.zeros((D,), jnp.float32), 'Wo': jax.random.normal(ks[6], (D, D), jnp.float32) * scale, 'bo': jnp.zeros((D,), jnp.float32)}
        return inp
    _L0_xattn_all = _L0_xattn_setup()
    _L0_xattn_in = {k: v for k, v in _L0_xattn_all.items() if k in ('Wq', 'bq', 'Wk', 'bk', 'Wv', 'bv', 'Wo', 'bo')}
    del _L0_xattn_all

    def _L0_ffn_setup():
        import jax, jax.numpy as jnp
        import numpy as np
        D_MODEL, D_FF, N_EXPERTS, TOP_K = (256, 1024, 8, 2)
        BATCH, SEQ = (2, 512)
        key = jax.random.key(seed)
        ks = jax.random.split(key, 10)
        s = 0.02
        return {'x': jax.random.normal(ks[0], (BATCH, SEQ, D_MODEL), jnp.float32), 'Wg': jax.random.normal(ks[1], (D_MODEL, N_EXPERTS), jnp.float32) * s, 'W1': jax.random.normal(ks[2], (N_EXPERTS, D_MODEL, D_FF), jnp.float32) * s, 'b1': jnp.zeros((N_EXPERTS, D_FF), jnp.float32), 'W2': jax.random.normal(ks[3], (N_EXPERTS, D_FF, D_MODEL), jnp.float32) * s, 'b2': jnp.zeros((N_EXPERTS, D_MODEL), jnp.float32), 'Ws1': jax.random.normal(ks[4], (D_MODEL, D_FF), jnp.float32) * s, 'bs1': jnp.zeros((D_FF,), jnp.float32), 'Ws2': jax.random.normal(ks[5], (D_FF, D_MODEL), jnp.float32) * s, 'bs2': jnp.zeros((D_MODEL,), jnp.float32)}
    _L0_ffn_all = _L0_ffn_setup()
    _L0_ffn_in = {k: v for k, v in _L0_ffn_all.items() if k in ('Wg', 'W1', 'b1', 'W2', 'b2', 'Ws1', 'bs1', 'Ws2', 'bs2')}
    del _L0_ffn_all

    def _L1_xattn_setup():
        import jax, jax.numpy as jnp
        import numpy as np
        EMBED = 256
        HEADS = 16
        HEAD_DIM = EMBED // HEADS
        key = jax.random.key(seed)
        ks = jax.random.split(key, 8)
        N, L = (2, 1024)
        return {'value': jax.random.normal(ks[0], (N, L, EMBED), dtype=jnp.float32), 'key': jax.random.normal(ks[1], (N, L, EMBED), dtype=jnp.float32), 'query': jax.random.normal(ks[2], (N, L, EMBED), dtype=jnp.float32), 'Wv': jax.random.normal(ks[3], (HEAD_DIM, HEAD_DIM), dtype=jnp.float32) * HEAD_DIM ** (-0.5), 'Wk': jax.random.normal(ks[4], (HEAD_DIM, HEAD_DIM), dtype=jnp.float32) * HEAD_DIM ** (-0.5), 'Wq': jax.random.normal(ks[5], (HEAD_DIM, HEAD_DIM), dtype=jnp.float32) * HEAD_DIM ** (-0.5), 'Wo': jax.random.normal(ks[6], (EMBED, EMBED), dtype=jnp.float32) * EMBED ** (-0.5), 'bo': jnp.zeros((EMBED,), dtype=jnp.float32)}
    _L1_xattn_all = _L1_xattn_setup()
    _L1_xattn_in = {k: v for k, v in _L1_xattn_all.items() if k in ('Wv', 'Wk', 'Wq', 'Wo', 'bo')}
    del _L1_xattn_all

    def _L1_ffn_setup():
        import jax, jax.numpy as jnp
        import numpy as np
        D_MODEL = 256
        D_FF = 1024
        N_EXPERTS = 4
        key = jax.random.key(seed)
        ks = jax.random.split(key, 8)
        s_in = 1.0 / np.sqrt(D_MODEL)
        s_ff = 1.0 / np.sqrt(D_FF)
        x = jax.random.normal(ks[0], (4, 512, D_MODEL), dtype=jnp.float32)
        W1 = jax.random.uniform(ks[1], (N_EXPERTS, D_MODEL, D_FF), jnp.float32, -s_in, s_in)
        b1 = jax.random.uniform(ks[2], (N_EXPERTS, D_FF), jnp.float32, -s_in, s_in)
        W2 = jax.random.uniform(ks[3], (N_EXPERTS, D_FF, D_MODEL), jnp.float32, -s_ff, s_ff)
        b2 = jax.random.uniform(ks[4], (N_EXPERTS, D_MODEL), jnp.float32, -s_ff, s_ff)
        Wg = jax.random.uniform(ks[5], (D_MODEL, N_EXPERTS), jnp.float32, -s_in, s_in)
        bg = jax.random.uniform(ks[6], (N_EXPERTS,), jnp.float32, -s_in, s_in)
        return {'x': x, 'W1': W1, 'b1': b1, 'W2': W2, 'b2': b2, 'Wg': Wg, 'bg': bg}
    _L1_ffn_all = _L1_ffn_setup()
    _L1_ffn_in = {k: v for k, v in _L1_ffn_all.items() if k in ('W1', 'b1', 'W2', 'b2', 'Wg', 'bg')}
    del _L1_ffn_all

    def _L2_xattn_setup():
        import jax, jax.numpy as jnp
        import numpy as np
        B, S, D, H = (2, 512, 256, 16)
        HD = D // H
        LN_EPS = 1e-05

        def _linear(x, w, b):
            return jnp.einsum('bsd,od->bso', x, w) + b

        def _split_heads(x):
            b, s, _ = x.shape
            return x.reshape(b, s, H, HD).transpose(0, 2, 1, 3)
        key = jax.random.key(seed)
        ks = jax.random.split(key, 14)
        w = 0.02
        return {'q': jax.random.normal(ks[0], (B, S, D), jnp.float32), 'k': jax.random.normal(ks[1], (B, S, D), jnp.float32), 'v': jax.random.normal(ks[2], (B, S, D), jnp.float32), 'mask': jnp.zeros((B, 1, S, S), dtype=bool), 'training': 0, 'wq_w': jax.random.normal(ks[3], (D, D), jnp.float32) * w, 'wq_b': jnp.zeros((D,), jnp.float32), 'wk_w': jax.random.normal(ks[4], (D, D), jnp.float32) * w, 'wk_b': jnp.zeros((D,), jnp.float32), 'wv_w': jax.random.normal(ks[5], (D, D), jnp.float32) * w, 'wv_b': jnp.zeros((D,), jnp.float32), 'wo_w': jax.random.normal(ks[6], (D, D), jnp.float32) * w, 'wo_b': jnp.zeros((D,), jnp.float32), 'ln_g': jnp.ones((D,), jnp.float32), 'ln_b': jnp.zeros((D,), jnp.float32)}
    _L2_xattn_all = _L2_xattn_setup()
    _L2_xattn_in = {k: v for k, v in _L2_xattn_all.items() if k in ('wq_w', 'wq_b', 'wk_w', 'wk_b', 'wv_w', 'wv_b', 'wo_w', 'wo_b', 'ln_g', 'ln_b')}
    del _L2_xattn_all

    def _L2_ffn_setup():
        import jax, jax.numpy as jnp
        import numpy as np
        LATENT = 256
        LEAF_W = 64
        DEPTH = 4
        N_LEAVES = 2 ** DEPTH
        N_NODES = 2 ** DEPTH - 1
        B, S = (4, 512)

        def _fff_params(key, prefix):
            ks = jax.random.split(key, 4)
            d, h, l, n = (LATENT, LEAF_W, N_LEAVES, N_NODES)
            s_in = 1.0 / np.sqrt(d).astype(np.float32)
            s_h = 1.0 / np.sqrt(h).astype(np.float32)
            return {f'{prefix}_node_w': jax.random.normal(ks[0], (n, d), jnp.float32) * s_in, f'{prefix}_node_b': jax.random.normal(ks[1], (n,), jnp.float32) * s_in, f'{prefix}_w1': jax.random.normal(ks[2], (l, d, h), jnp.float32) * s_in, f'{prefix}_b1': jnp.zeros((l, h), jnp.float32), f'{prefix}_w2': jax.random.normal(ks[3], (l, h, d), jnp.float32) * s_h, f'{prefix}_b2': jnp.zeros((l, d), jnp.float32)}

        def _fff(x, node_w, node_b, w1, b1, w2, b2):
            Bx, Sx, D = x.shape
            xf = x.reshape(-1, D)
            N = xf.shape[0]
            cur = jnp.zeros((N,), jnp.int32)
            for _ in range(DEPTH):
                pw = node_w[cur]
                score = jnp.einsum('nd,nd->n', xf, pw) + node_b[cur]
                cur = 2 * cur + 1 + (score >= 0).astype(jnp.int32)
            leaf = cur - N_NODES
            sel = jax.nn.one_hot(leaf, N_LEAVES, dtype=xf.dtype)
            hidden_all = jax.nn.relu(jnp.einsum('nd,ldh->lnh', xf, w1) + b1[:, None, :])
            hidden = hidden_all * sel.T[:, :, None]
            out = jnp.einsum('lnh,lho->no', hidden, w2) + sel @ b2
            return out.reshape(Bx, Sx, D)
        key = jax.random.key(seed)
        kx, kq, kk, kv = jax.random.split(key, 4)
        inp = {'x': jax.random.normal(kx, (B, S, LATENT), jnp.float32)}
        inp.update(_fff_params(kq, 'q'))
        inp.update(_fff_params(kk, 'k'))
        inp.update(_fff_params(kv, 'v'))
        return inp
    _L2_ffn_all = _L2_ffn_setup()
    _L2_ffn_in = {k: v for k, v in _L2_ffn_all.items() if k in ('q_node_w', 'q_node_b', 'q_w1', 'q_b1', 'q_w2', 'q_b2', 'k_node_w', 'k_node_b', 'k_w1', 'k_b1', 'k_w2', 'k_b2', 'v_node_w', 'v_node_b', 'v_w1', 'v_b1', 'v_w2', 'v_b2')}
    del _L2_ffn_all

    def _L3_xattn_setup():
        import jax, jax.numpy as jnp
        import numpy as np
        B, NQ, NK = (8, 512, 512)
        DQ = DK = DV = 256
        EPS = 1e-05

        def _xavier(key, shape):
            fan_in, fan_out = (shape[0], shape[1])
            lim = float(np.sqrt(6.0 / (fan_in + fan_out)))
            return jax.random.uniform(key, shape, jnp.float32, -lim, lim)

        def _layernorm(x, g, b):
            mu = jnp.mean(x, axis=-1, keepdims=True)
            var = jnp.mean(jnp.square(x - mu), axis=-1, keepdims=True)
            return (x - mu) * jax.lax.rsqrt(var + EPS) * g + b
        key = jax.random.key(seed)
        ks = jax.random.split(key, 12)
        return {'Q': jax.random.normal(ks[0], (B, NQ, DQ), jnp.float32), 'K': jax.random.normal(ks[1], (B, NK, DK), jnp.float32), 'V': jax.random.normal(ks[2], (B, NK, DK), jnp.float32), 'pad_mask': jax.random.randint(ks[3], (B, 1, NK), 0, 2, jnp.int32), 'Wq': _xavier(ks[4], (DQ, DV)), 'bq': jnp.zeros((DV,), jnp.float32), 'Wk': _xavier(ks[5], (DK, DV)), 'bk': jnp.zeros((DV,), jnp.float32), 'Wv': _xavier(ks[6], (DK, DV)), 'bv': jnp.zeros((DV,), jnp.float32), 'Wo': _xavier(ks[7], (DV, DV)), 'bo': jnp.zeros((DV,), jnp.float32), 'g0': jnp.ones((DV,), jnp.float32), 'beta0': jnp.zeros((DV,), jnp.float32)}
    _L3_xattn_all = _L3_xattn_setup()
    _L3_xattn_in = {k: v for k, v in _L3_xattn_all.items() if k in ('Wq', 'bq', 'Wk', 'bk', 'Wv', 'bv', 'Wo', 'bo', 'g0', 'beta0')}
    del _L3_xattn_all

    def _L3_ffn_setup():
        import jax, jax.numpy as jnp
        import numpy as np
        B, S, D, F, E = (2, 512, 256, 1024, 8)
        LN_EPS = 1e-05

        def _xavier(key, shape, fan_in, fan_out):
            a = np.sqrt(6.0 / (fan_in + fan_out))
            return jax.random.uniform(key, shape, jnp.float32, -a, a)
        key = jax.random.key(seed)
        ks = jax.random.split(key, 8)
        tgt = jax.random.normal(ks[0], (B, S, D), jnp.float32)
        router_w = _xavier(ks[1], (E, D), D, E)
        router_b = jnp.zeros((E,), jnp.float32)
        w1 = _xavier(ks[2], (E, D, F), D, F)
        b1 = jnp.zeros((E, F), jnp.float32)
        w2 = _xavier(ks[3], (E, F, D), F, D)
        b2 = jnp.zeros((E, D), jnp.float32)
        gamma = jnp.ones((D,), jnp.float32)
        beta = jnp.zeros((D,), jnp.float32)
        return {'tgt': tgt, 'router_w': router_w, 'router_b': router_b, 'w1': w1, 'b1': b1, 'w2': w2, 'b2': b2, 'gamma': gamma, 'beta': beta}
    _L3_ffn_all = _L3_ffn_setup()
    _L3_ffn_in = {k: v for k, v in _L3_ffn_all.items() if k in ('router_w', 'router_b', 'w1', 'b1', 'w2', 'b2', 'gamma', 'beta')}
    del _L3_ffn_all
    return {'x': x, 'ctx_1024': ctx_1024, 'mask_Bx1xSxS2_bf0': mask_Bx1xSxS2_bf0, 'mask_Bx1xS2_ik1': mask_Bx1xS2_ik1, 'g_xattn': g_xattn, 'g_ffn': g_ffn, 'L0_xattn_Wq': _L0_xattn_in['Wq'], 'L0_xattn_bq': _L0_xattn_in['bq'], 'L0_xattn_Wk': _L0_xattn_in['Wk'], 'L0_xattn_bk': _L0_xattn_in['bk'], 'L0_xattn_Wv': _L0_xattn_in['Wv'], 'L0_xattn_bv': _L0_xattn_in['bv'], 'L0_xattn_Wo': _L0_xattn_in['Wo'], 'L0_xattn_bo': _L0_xattn_in['bo'], 'L0_ffn_Wg': _L0_ffn_in['Wg'], 'L0_ffn_W1': _L0_ffn_in['W1'], 'L0_ffn_b1': _L0_ffn_in['b1'], 'L0_ffn_W2': _L0_ffn_in['W2'], 'L0_ffn_b2': _L0_ffn_in['b2'], 'L0_ffn_Ws1': _L0_ffn_in['Ws1'], 'L0_ffn_bs1': _L0_ffn_in['bs1'], 'L0_ffn_Ws2': _L0_ffn_in['Ws2'], 'L0_ffn_bs2': _L0_ffn_in['bs2'], 'L1_xattn_Wv': _L1_xattn_in['Wv'], 'L1_xattn_Wk': _L1_xattn_in['Wk'], 'L1_xattn_Wq': _L1_xattn_in['Wq'], 'L1_xattn_Wo': _L1_xattn_in['Wo'], 'L1_xattn_bo': _L1_xattn_in['bo'], 'L1_ffn_W1': _L1_ffn_in['W1'], 'L1_ffn_b1': _L1_ffn_in['b1'], 'L1_ffn_W2': _L1_ffn_in['W2'], 'L1_ffn_b2': _L1_ffn_in['b2'], 'L1_ffn_Wg': _L1_ffn_in['Wg'], 'L1_ffn_bg': _L1_ffn_in['bg'], 'L2_xattn_wq_w': _L2_xattn_in['wq_w'], 'L2_xattn_wq_b': _L2_xattn_in['wq_b'], 'L2_xattn_wk_w': _L2_xattn_in['wk_w'], 'L2_xattn_wk_b': _L2_xattn_in['wk_b'], 'L2_xattn_wv_w': _L2_xattn_in['wv_w'], 'L2_xattn_wv_b': _L2_xattn_in['wv_b'], 'L2_xattn_wo_w': _L2_xattn_in['wo_w'], 'L2_xattn_wo_b': _L2_xattn_in['wo_b'], 'L2_xattn_ln_g': _L2_xattn_in['ln_g'], 'L2_xattn_ln_b': _L2_xattn_in['ln_b'], 'L2_ffn_q_node_w': _L2_ffn_in['q_node_w'], 'L2_ffn_q_node_b': _L2_ffn_in['q_node_b'], 'L2_ffn_q_w1': _L2_ffn_in['q_w1'], 'L2_ffn_q_b1': _L2_ffn_in['q_b1'], 'L2_ffn_q_w2': _L2_ffn_in['q_w2'], 'L2_ffn_q_b2': _L2_ffn_in['q_b2'], 'L2_ffn_k_node_w': _L2_ffn_in['k_node_w'], 'L2_ffn_k_node_b': _L2_ffn_in['k_node_b'], 'L2_ffn_k_w1': _L2_ffn_in['k_w1'], 'L2_ffn_k_b1': _L2_ffn_in['k_b1'], 'L2_ffn_k_w2': _L2_ffn_in['k_w2'], 'L2_ffn_k_b2': _L2_ffn_in['k_b2'], 'L2_ffn_v_node_w': _L2_ffn_in['v_node_w'], 'L2_ffn_v_node_b': _L2_ffn_in['v_node_b'], 'L2_ffn_v_w1': _L2_ffn_in['v_w1'], 'L2_ffn_v_b1': _L2_ffn_in['v_b1'], 'L2_ffn_v_w2': _L2_ffn_in['v_w2'], 'L2_ffn_v_b2': _L2_ffn_in['v_b2'], 'L3_xattn_Wq': _L3_xattn_in['Wq'], 'L3_xattn_bq': _L3_xattn_in['bq'], 'L3_xattn_Wk': _L3_xattn_in['Wk'], 'L3_xattn_bk': _L3_xattn_in['bk'], 'L3_xattn_Wv': _L3_xattn_in['Wv'], 'L3_xattn_bv': _L3_xattn_in['bv'], 'L3_xattn_Wo': _L3_xattn_in['Wo'], 'L3_xattn_bo': _L3_xattn_in['bo'], 'L3_xattn_g0': _L3_xattn_in['g0'], 'L3_xattn_beta0': _L3_xattn_in['beta0'], 'L3_ffn_router_w': _L3_ffn_in['router_w'], 'L3_ffn_router_b': _L3_ffn_in['router_b'], 'L3_ffn_w1': _L3_ffn_in['w1'], 'L3_ffn_b1': _L3_ffn_in['b1'], 'L3_ffn_w2': _L3_ffn_in['w2'], 'L3_ffn_b2': _L3_ffn_in['b2'], 'L3_ffn_gamma': _L3_ffn_in['gamma'], 'L3_ffn_beta': _L3_ffn_in['beta']}

def reference(x, ctx_1024, mask_Bx1xSxS2_bf0, mask_Bx1xS2_ik1, g_xattn, g_ffn, L0_xattn_Wq, L0_xattn_bq, L0_xattn_Wk, L0_xattn_bk, L0_xattn_Wv, L0_xattn_bv, L0_xattn_Wo, L0_xattn_bo, L0_ffn_Wg, L0_ffn_W1, L0_ffn_b1, L0_ffn_W2, L0_ffn_b2, L0_ffn_Ws1, L0_ffn_bs1, L0_ffn_Ws2, L0_ffn_bs2, L1_xattn_Wv, L1_xattn_Wk, L1_xattn_Wq, L1_xattn_Wo, L1_xattn_bo, L1_ffn_W1, L1_ffn_b1, L1_ffn_W2, L1_ffn_b2, L1_ffn_Wg, L1_ffn_bg, L2_xattn_wq_w, L2_xattn_wq_b, L2_xattn_wk_w, L2_xattn_wk_b, L2_xattn_wv_w, L2_xattn_wv_b, L2_xattn_wo_w, L2_xattn_wo_b, L2_xattn_ln_g, L2_xattn_ln_b, L2_ffn_q_node_w, L2_ffn_q_node_b, L2_ffn_q_w1, L2_ffn_q_b1, L2_ffn_q_w2, L2_ffn_q_b2, L2_ffn_k_node_w, L2_ffn_k_node_b, L2_ffn_k_w1, L2_ffn_k_b1, L2_ffn_k_w2, L2_ffn_k_b2, L2_ffn_v_node_w, L2_ffn_v_node_b, L2_ffn_v_w1, L2_ffn_v_b1, L2_ffn_v_w2, L2_ffn_v_b2, L3_xattn_Wq, L3_xattn_bq, L3_xattn_Wk, L3_xattn_bk, L3_xattn_Wv, L3_xattn_bv, L3_xattn_Wo, L3_xattn_bo, L3_xattn_g0, L3_xattn_beta0, L3_ffn_router_w, L3_ffn_router_b, L3_ffn_w1, L3_ffn_b1, L3_ffn_w2, L3_ffn_b2, L3_ffn_gamma, L3_ffn_beta):
    import jax
    import jax.numpy as jnp

    def _L0_xattn_ref(query, key, value, Wq, bq, Wk, bk, Wv, bv, Wo, bo):
        import jax, jax.numpy as jnp
        import numpy as np
        D = 256
        H = 16
        HD = D // H

        def _split_heads(x):
            B, S, _ = x.shape
            return x.reshape(B, S, H, HD).transpose(0, 2, 1, 3)
        B, S, _ = query.shape
        q = _split_heads(query @ Wq + bq)
        k = _split_heads(key @ Wk + bk)
        v = _split_heads(value @ Wv + bv)
        scaling = jnp.sqrt(jnp.asarray(HD, jnp.float32))
        attn = jnp.einsum('bhqd,bhkd->bhqk', q, k) / scaling
        causal = 1.0 - jnp.tril(jnp.ones((S, S), jnp.float32))
        attn = attn + causal * -1000000000.0
        probs = jax.nn.softmax(attn, axis=-1)
        out = jnp.einsum('bhqk,bhkd->bhqd', probs, v)
        out = out.transpose(0, 2, 1, 3).reshape(B, S, D)
        return out @ Wo + bo

    def _L0_ffn_ref(x, Wg, W1, b1, W2, b2, Ws1, bs1, Ws2, bs2):
        import jax, jax.numpy as jnp
        import numpy as np
        D_MODEL, D_FF, N_EXPERTS, TOP_K = (256, 1024, 8, 2)
        BATCH, SEQ = (2, 512)
        B, S, D = x.shape
        xf = x.reshape(B * S, D)
        T = B * S
        logits = xf @ Wg
        top_vals, top_idx = jax.lax.top_k(logits, TOP_K)
        top_w = jax.nn.softmax(top_vals, axis=-1)
        combine = jnp.zeros((T, N_EXPERTS), x.dtype).at[jnp.arange(T)[:, None], top_idx].add(top_w)
        h = jax.nn.relu(jnp.einsum('td,edf->tef', xf, W1) + b1)
        sparse = jnp.einsum('te,tef,efd->td', combine, h, W2)
        sparse = sparse + combine @ b2
        shared = jax.nn.relu(xf @ Ws1 + bs1) @ Ws2 + bs2
        out = sparse + shared
        return out.reshape(B, S, D)

    def _L1_xattn_ref(value, key, query, Wv, Wk, Wq, Wo, bo):
        import jax, jax.numpy as jnp
        import numpy as np
        EMBED = 256
        HEADS = 16
        HEAD_DIM = EMBED // HEADS
        N, Lq = (query.shape[0], query.shape[1])
        Lk, Lv = (key.shape[1], value.shape[1])
        v = value.reshape(N, Lv, HEADS, HEAD_DIM)
        k = key.reshape(N, Lk, HEADS, HEAD_DIM)
        q = query.reshape(N, Lq, HEADS, HEAD_DIM)
        v = jnp.einsum('nlhd,ed->nlhe', v, Wv)
        k = jnp.einsum('nlhd,ed->nlhe', k, Wk)
        q = jnp.einsum('nlhd,ed->nlhe', q, Wq)
        energy = jnp.einsum('nqhd,nkhd->nhqk', q, k)
        attention = jax.nn.softmax(energy * EMBED ** (-0.5), axis=3)
        out = jnp.einsum('nhqk,nkhd->nqhd', attention, v).reshape(N, Lq, EMBED)
        return out @ Wo.T + bo

    def _L1_ffn_ref(x, W1, b1, W2, b2, Wg, bg):
        import jax, jax.numpy as jnp
        import numpy as np
        D_MODEL = 256
        D_FF = 1024
        N_EXPERTS = 4
        gate_logits = jnp.einsum('bld,de->ble', x, Wg) + bg
        idx = jnp.argmax(jax.nn.softmax(gate_logits, axis=-1), axis=-1)
        h = jnp.einsum('bld,edf->belf', x, W1) + b1[None, :, None, :]
        h = jax.nn.gelu(h, approximate=False)
        y = jnp.einsum('belf,efd->beld', h, W2) + b2[None, :, None, :]
        onehot = jax.nn.one_hot(idx, N_EXPERTS, dtype=x.dtype)
        out = jnp.einsum('beld,ble->bld', y, onehot)
        return out

    def _L2_xattn_ref(q, k, v, mask, training, wq_w, wq_b, wk_w, wk_b, wv_w, wv_b, wo_w, wo_b, ln_g, ln_b):
        import jax, jax.numpy as jnp
        import numpy as np
        B, S, D, H = (2, 512, 256, 16)
        HD = D // H
        LN_EPS = 1e-05

        def _linear(x, w, b):
            return jnp.einsum('bsd,od->bso', x, w) + b

        def _split_heads(x):
            b, s, _ = x.shape
            return x.reshape(b, s, H, HD).transpose(0, 2, 1, 3)
        residual = q
        Q = _split_heads(_linear(q, wq_w, wq_b))
        K = _split_heads(_linear(k, wk_w, wk_b))
        V = _split_heads(_linear(v, wv_w, wv_b))
        dk = jnp.sqrt(jnp.asarray(HD, jnp.float16)).astype(jnp.float32) + 1e-08
        score = jnp.einsum('bhqd,bhkd->bhqk', Q, K) / dk
        attn = jnp.where(mask, -jnp.inf, score)
        ctx = jnp.einsum('bhqk,bhkd->bhqd', attn, V)
        b, _, s, _ = ctx.shape
        ctx = ctx.transpose(0, 2, 1, 3).reshape(b, s, D)
        o = _linear(ctx, wo_w, wo_b)
        x = residual + o
        mu = jnp.mean(x, axis=-1, keepdims=True)
        var = jnp.mean(jnp.square(x - mu), axis=-1, keepdims=True)
        return ln_g * (x - mu) * jax.lax.rsqrt(var + LN_EPS) + ln_b

    def _L2_ffn_ref(x, q_node_w, q_node_b, q_w1, q_b1, q_w2, q_b2, k_node_w, k_node_b, k_w1, k_b1, k_w2, k_b2, v_node_w, v_node_b, v_w1, v_b1, v_w2, v_b2):
        import jax, jax.numpy as jnp
        import numpy as np
        LATENT = 256
        LEAF_W = 64
        DEPTH = 4
        N_LEAVES = 2 ** DEPTH
        N_NODES = 2 ** DEPTH - 1
        B, S = (4, 512)

        def _fff_params(key, prefix):
            ks = jax.random.split(key, 4)
            d, h, l, n = (LATENT, LEAF_W, N_LEAVES, N_NODES)
            s_in = 1.0 / np.sqrt(d).astype(np.float32)
            s_h = 1.0 / np.sqrt(h).astype(np.float32)
            return {f'{prefix}_node_w': jax.random.normal(ks[0], (n, d), jnp.float32) * s_in, f'{prefix}_node_b': jax.random.normal(ks[1], (n,), jnp.float32) * s_in, f'{prefix}_w1': jax.random.normal(ks[2], (l, d, h), jnp.float32) * s_in, f'{prefix}_b1': jnp.zeros((l, h), jnp.float32), f'{prefix}_w2': jax.random.normal(ks[3], (l, h, d), jnp.float32) * s_h, f'{prefix}_b2': jnp.zeros((l, d), jnp.float32)}

        def _fff(x, node_w, node_b, w1, b1, w2, b2):
            Bx, Sx, D = x.shape
            xf = x.reshape(-1, D)
            N = xf.shape[0]
            cur = jnp.zeros((N,), jnp.int32)
            for _ in range(DEPTH):
                pw = node_w[cur]
                score = jnp.einsum('nd,nd->n', xf, pw) + node_b[cur]
                cur = 2 * cur + 1 + (score >= 0).astype(jnp.int32)
            leaf = cur - N_NODES
            sel = jax.nn.one_hot(leaf, N_LEAVES, dtype=xf.dtype)
            hidden_all = jax.nn.relu(jnp.einsum('nd,ldh->lnh', xf, w1) + b1[:, None, :])
            hidden = hidden_all * sel.T[:, :, None]
            out = jnp.einsum('lnh,lho->no', hidden, w2) + sel @ b2
            return out.reshape(Bx, Sx, D)
        q = _fff(x, q_node_w, q_node_b, q_w1, q_b1, q_w2, q_b2)
        k = _fff(x, k_node_w, k_node_b, k_w1, k_b1, k_w2, k_b2)
        v = _fff(x, v_node_w, v_node_b, v_w1, v_b1, v_w2, v_b2)
        scale = 1.0 / np.sqrt(LATENT).astype(np.float32)
        attn = jax.nn.softmax(jnp.einsum('bqd,bkd->bqk', q, k) * scale, axis=-1)
        return jnp.einsum('bqk,bkd->bqd', attn, v)

    def _L3_xattn_ref(Q, K, V, pad_mask, Wq, bq, Wk, bk, Wv, bv, Wo, bo, g0, beta0):
        import jax, jax.numpy as jnp
        import numpy as np
        B, NQ, NK = (8, 512, 512)
        DQ = DK = DV = 256
        EPS = 1e-05

        def _xavier(key, shape):
            fan_in, fan_out = (shape[0], shape[1])
            lim = float(np.sqrt(6.0 / (fan_in + fan_out)))
            return jax.random.uniform(key, shape, jnp.float32, -lim, lim)

        def _layernorm(x, g, b):
            mu = jnp.mean(x, axis=-1, keepdims=True)
            var = jnp.mean(jnp.square(x - mu), axis=-1, keepdims=True)
            return (x - mu) * jax.lax.rsqrt(var + EPS) * g + b
        q = Q @ Wq + bq
        k = K @ Wk + bk
        v = V @ Wv + bv
        scale = 1.0 / jnp.sqrt(jnp.float32(DV))
        scores = jnp.einsum('bqd,bkd->bqk', q, k) * scale
        scores = jnp.where(pad_mask == 0, jnp.float32(-1000000000.0), scores)
        w = jax.nn.softmax(scores, axis=-1)
        out = jnp.einsum('bqk,bkd->bqd', w, v)
        out = out @ Wo + bo
        out = _layernorm(out, g0, beta0)
        return out

    def _L3_ffn_ref(tgt, router_w, router_b, w1, b1, w2, b2, gamma, beta):
        import jax, jax.numpy as jnp
        import numpy as np
        B, S, D, F, E = (2, 512, 256, 1024, 8)
        LN_EPS = 1e-05

        def _xavier(key, shape, fan_in, fan_out):
            a = np.sqrt(6.0 / (fan_in + fan_out))
            return jax.random.uniform(key, shape, jnp.float32, -a, a)
        logits = jnp.einsum('bsd,ed->bse', tgt, router_w) + router_b
        rw = jax.nn.softmax(logits, axis=-1)
        rw = jnp.zeros_like(rw).at[..., 0].set(1.0)
        h = jax.nn.relu(jnp.einsum('bsd,edf->besf', tgt, w1) + b1[None, :, None, :])
        eo = jnp.einsum('besf,efd->besd', h, w2) + b2[None, :, None, :]
        tgt2 = jnp.einsum('besd,bse->bsd', eo, rw)
        x = tgt + tgt2
        mean = jnp.mean(x, axis=-1, keepdims=True)
        var = jnp.mean(jnp.square(x - mean), axis=-1, keepdims=True)
        return (x - mean) * jax.lax.rsqrt(var + LN_EPS) * gamma + beta
    x = x + jnp.tanh(g_xattn[0]) * _L0_xattn_ref(_layernorm(x, axis=-1), ctx_1024, ctx_1024, L0_xattn_Wq, L0_xattn_bq, L0_xattn_Wk, L0_xattn_bk, L0_xattn_Wv, L0_xattn_bv, L0_xattn_Wo, L0_xattn_bo)
    x = x + jnp.tanh(g_ffn[0]) * _L0_ffn_ref(_layernorm(x, axis=-1), L0_ffn_Wg, L0_ffn_W1, L0_ffn_b1, L0_ffn_W2, L0_ffn_b2, L0_ffn_Ws1, L0_ffn_bs1, L0_ffn_Ws2, L0_ffn_bs2)
    x = x + jnp.tanh(g_xattn[1]) * _L1_xattn_ref(ctx_1024, ctx_1024, _layernorm(x, axis=-1), L1_xattn_Wv, L1_xattn_Wk, L1_xattn_Wq, L1_xattn_Wo, L1_xattn_bo)
    x = x + jnp.tanh(g_ffn[1]) * _L1_ffn_ref(_layernorm(x, axis=-1), L1_ffn_W1, L1_ffn_b1, L1_ffn_W2, L1_ffn_b2, L1_ffn_Wg, L1_ffn_bg)
    x = x + jnp.tanh(g_xattn[2]) * _L2_xattn_ref(_layernorm(x, axis=-1), ctx_1024, ctx_1024, mask_Bx1xSxS2_bf0, 0, L2_xattn_wq_w, L2_xattn_wq_b, L2_xattn_wk_w, L2_xattn_wk_b, L2_xattn_wv_w, L2_xattn_wv_b, L2_xattn_wo_w, L2_xattn_wo_b, L2_xattn_ln_g, L2_xattn_ln_b)
    x = x + jnp.tanh(g_ffn[2]) * _L2_ffn_ref(_layernorm(x, axis=-1), L2_ffn_q_node_w, L2_ffn_q_node_b, L2_ffn_q_w1, L2_ffn_q_b1, L2_ffn_q_w2, L2_ffn_q_b2, L2_ffn_k_node_w, L2_ffn_k_node_b, L2_ffn_k_w1, L2_ffn_k_b1, L2_ffn_k_w2, L2_ffn_k_b2, L2_ffn_v_node_w, L2_ffn_v_node_b, L2_ffn_v_w1, L2_ffn_v_b1, L2_ffn_v_w2, L2_ffn_v_b2)
    x = x + jnp.tanh(g_xattn[3]) * _L3_xattn_ref(_layernorm(x, axis=-1), ctx_1024, ctx_1024, mask_Bx1xS2_ik1, L3_xattn_Wq, L3_xattn_bq, L3_xattn_Wk, L3_xattn_bk, L3_xattn_Wv, L3_xattn_bv, L3_xattn_Wo, L3_xattn_bo, L3_xattn_g0, L3_xattn_beta0)
    x = x + jnp.tanh(g_ffn[3]) * _L3_ffn_ref(_layernorm(x, axis=-1), L3_ffn_router_w, L3_ffn_router_b, L3_ffn_w1, L3_ffn_b1, L3_ffn_w2, L3_ffn_b2, L3_ffn_gamma, L3_ffn_beta)
    return x

_drawn_inputs = setup_inputs


def setup_inputs(seed=0):
    import zlib

    import numpy as np

    out = dict(_drawn_inputs(seed))
    spreads = {'L0_xattn_bq': (0.0, 0.373),
     'L0_xattn_bk': (0.0, 0.8),
     'L0_xattn_bv': (0.0, 0.1),
     'L0_xattn_bo': (0.0, 0.1),
     'L0_ffn_b1': (0.0, 0.314),
     'L0_ffn_b2': (0.0, 0.1),
     'L0_ffn_bs1': (0.0, 0.1),
     'L0_ffn_bs2': (0.0, 0.1),
     'L1_xattn_bo': (0.0, 0.1),
     'L2_xattn_wq_b': (0.0, 0.1),
     'L2_xattn_wk_b': (0.0, 0.1),
     'L2_xattn_wv_b': (0.0, 0.1),
     'L2_xattn_wo_b': (0.0, 0.1),
     'L2_xattn_ln_g': (1.0, 0.2),
     'L2_xattn_ln_b': (0.0, 0.1),
     'L2_ffn_q_b1': (0.0, 0.8),
     'L2_ffn_q_b2': (0.0, 0.8),
     'L2_ffn_k_b1': (0.0, 0.8),
     'L2_ffn_k_b2': (0.0, 0.8),
     'L2_ffn_v_b1': (0.0, 0.587),
     'L2_ffn_v_b2': (0.0, 0.344),
     'L3_xattn_bq': (0.0, 0.303),
     'L3_xattn_bk': (0.0, 0.8),
     'L3_xattn_bv': (0.0, 0.1),
     'L3_xattn_bo': (0.0, 0.1),
     'L3_xattn_g0': (1.0, 0.2),
     'L3_xattn_beta0': (0.0, 0.1),
     'L3_ffn_router_b': (0.0, 0.1),
     'L3_ffn_b1': (0.0, 0.1),
     'L3_ffn_b2': (0.0, 0.1),
     'L3_ffn_gamma': (1.0, 0.2),
     'L3_ffn_beta': (0.0, 0.1)}
    factors = {'g_ffn': 2.886,
     'L1_ffn_b1': 6.099,
     'L1_ffn_b2': 4.969,
     'L2_ffn_q_node_w': 3.721,
     'L2_ffn_q_node_b': 8.0,
     'L2_ffn_q_w1': 4.271,
     'L2_ffn_q_w2': 3.675,
     'L2_ffn_k_node_w': 3.789,
     'L2_ffn_k_node_b': 8.0,
     'L2_ffn_k_w1': 4.249,
     'L2_ffn_k_w2': 3.631,
     'L2_ffn_v_node_b': 3.077}
    for name, (base, spread) in spreads.items():
        noise = np.random.default_rng([zlib.crc32(name.encode()), seed]).standard_normal(out[name].shape)
        drawn = base * np.exp(spread * noise) if base else spread * noise
        out[name] = jnp.asarray(drawn.astype(out[name].dtype))
    for name, factor in factors.items():
        out[name] = (out[name] * factor).astype(out[name].dtype)
    return out
```

```python
from contextlib import ExitStack

import concourse.bass as bass
from concourse import mybir

P = 128
NBATCH, SEQ, D = 8, 256, 256
T = NBATCH * SEQ
NT = T // P
BLK = 512
NB = T // BLK
KD = D // P
H, HD = 16, 16
GH = P // HD
F = 1024
NF = F // P
E0, E1 = 9, 4
NLEAF, LEAFW, DEPTH, TREES = 16, 64, 4, 3
NODES = NLEAF - 1
EPS = 1e-5
NEG = -1.0e9
BIG = 1.0e30

ALU = mybir.AluOpType
ACT = mybir.ActivationFunctionType
AXX = mybir.AxisListType.X
F32 = mybir.dt.float32
BF16 = mybir.dt.bfloat16
I32 = mybir.dt.int32
U8 = mybir.dt.uint8
ds = bass.ds

COLS, ROWS = {}, {}
for _name, _n in (("L0_bq", 2), ("L0_bk", 2), ("L0_b1", E0 * NF), ("L1_b1", E1 * NF), ("L2_bq", 2),
                  ("L2_b1", TREES * NF), ("L3_bq", 2), ("L3_bk", 2), ("L3_b1", NF)):
    COLS[_name] = (sum(n for _, n in COLS.values()), _n)
for _name, _n in (("attn0", 2), ("ffn0", E0), ("attn1", 1), ("ffn1", E1), ("attn2", 5), ("attn3", 4), ("ffn3", 3)):
    ROWS[_name] = (sum(n for _, n in ROWS.values()), _n)
NCOLS = sum(n for _, n in COLS.values())
NROWS = sum(n for _, n in ROWS.values())
NSMALL = E1 + TREES * NODES
NGATEW = (E0 - 1) + E1 + TREES * NODES


def wait(eng, sem, value):
    if not isinstance(value, int) or value > 0:
        eng.wait_ge(sem, value)


def decoder_kernel(nc, a, out):
    ctx = ExitStack()
    with ctx:
        def sb(name, shape, dt=F32):
            return ctx.enter_context(nc.sbuf_tensor(name, shape, dt))

        def sem(name):
            return ctx.enter_context(nc.semaphore(name))

        phase_sems = []

        def psem(name):
            phase_sems.append(nc.alloc_semaphore(name=name))
            return phase_sems[-1]

        def end_phase():
            nc.clear_and_free_semaphores(phase_sems)
            nc.all_engine_barrier()
            phase_sems.clear()

        x_tok = sb("x_tok", [P, NT, D])
        xnT = sb("xnT", [P, KD, T])
        ctxT = sb("ctxT", [P, KD, T])
        wbuf = sb("wbuf", [P, 3, 4096])
        hbuf = sb("hbuf", [P, 4096])
        vbuf = sb("vbuf", [P, 4096])
        attw = sb("attw", [P, 2, 4, KD, D])
        rowsA = sb("rowsA", [P, 5, D])
        rowsF = sb("rowsF", [P, E0, D])
        stage = sb("stage", [P, KD, BLK])
        qT = sb("qT", [P, KD, BLK])
        kT = sb("kT", [P, KD, BLK])
        prob = sb("prob", [P, 2, 2, 2, SEQ])
        probT = sb("probT", [P, 4, 2, SEQ])
        oT = sb("oT", [P, KD, SEQ])
        xs = sb("xs", [P, 2, D])
        ts = sb("ts", [P, 2, D])
        stats = sb("stats", [P, 2, 6])
        sm = sb("sm", [P, 8, 2])
        negmax = sb("negmax", [P, 2, 2, 2])
        rowsum = sb("rowsum", [P, 2, 2, 2])
        rinv = sb("rinv", [P, 2, 2, 2])
        cols = sb("cols", [P, NCOLS])
        qbias = sb("qbias", [P, 4])
        gates = sb("gates", [P, 8])
        small = sb("small", [P, NSMALL])
        gatew = sb("gatew", [P, KD, NGATEW])
        ident = sb("ident", [P, P])
        identb = sb("identb", [P, P], BF16)
        causal = sb("causal", [P, P], BF16)
        hmask = sb("hmask", [P, GH])
        bmask = sb("bmask", [P, P])
        mhalf = sb("mhalf", [P, 2])
        rank = sb("rank", [P, E0 - 1])
        logit = sb("logit", [P, NT, E0 - 1])
        rt = sb("rt", [P, 3, NT, E0 - 1])
        r1 = sb("r1", [P, 8, NT])
        comb = sb("comb", [P, E0, NT])
        dec = sb("dec", [P, 4, TREES, NLEAF])
        path = sb("path", [P, 2, 4, TREES, NLEAF])
        spare = sb("spare", [P, 2])
        anym = sb("anym", [P, 2, NT])
        rep = sb("rep", [P, 3, HD])
        ps = ctx.enter_context(nc.psum_tensor("ps", [P, 8, 512], F32))

        km = hbuf[:, :].rearrange("p (g j s) -> p g j s", g=2, j=GH)
        hT = hbuf[:, :].rearrange("p (f t) -> p f t", f=NF)
        vm = [wbuf[:, 2, :].rearrange("p (t h c) -> p t h c", t=2, h=H),
              vbuf[:, :].rearrange("p (t h c) -> p t h c", t=2, h=H)]
        xn_tok = vbuf[:, :].rearrange("p (t d) -> p t d", t=NT)
        selpad = vbuf[:, 0:512].rearrange("p (t c) -> p t c", t=4)
        selT = vbuf[:, 512:1024]
        leafw = vbuf[:, 1024:2560].bitcast(BF16).rearrange("p (t f) -> p t f", t=TREES)
        b2pad = vbuf[:, 2560:3328].rearrange("p (t d) -> p t d", t=TREES)
        selm = vbuf[:, 3328:3584].bitcast(BF16)
        w1 = [wbuf[:, s, 0:2048].rearrange("p (k f) -> p k f", k=KD) for s in range(3)]
        w2 = [wbuf[:, s, 2048:4096].rearrange("p (f d) -> p f d", f=NF) for s in range(3)]

        def col(name, j):
            o = COLS[name][0]
            if isinstance(j, int):
                return cols[:, o + j:o + j + 1]
            return cols[:, ds(j + o, 1)]

        ld_const = sem("ld_const")
        ld_x = sem("ld_x")
        ld_att = [sem(f"ld_att{s}") for s in range(2)]
        ld_w = [sem(f"ld_w{s}") for s in range(3)]
        ld_rowsA = sem("ld_rowsA")
        ld_rowsF = sem("ld_rowsF")
        ld_pad = sem("ld_pad")
        stored = sem("stored")

        def load_rows(sp, dst, name, signal):
            o, n = ROWS[name]
            sp.dma_start(dst[:, 0:n, :], a["rows"][o:o + n, :].unsqueeze(0).broadcast_to([P, n, D])).then_inc(signal, 16)

        def load_att(sp, slot, l):
            sp.dma_start(attw[:, slot], a["attw"][l].rearrange("w (k p) n -> p w k n", p=P)).then_inc(ld_att[slot], 16)

        def load_expert(sp, slot, first, second):
            sp.dma_start(w1[slot], first.rearrange("(k p) f -> p k f", p=P)).then_inc(ld_w[slot], 16)
            sp.dma_start(w2[slot], second.rearrange("(f p) d -> p f d", p=P)).then_inc(ld_w[slot], 16)

        def gate(i):
            return gates[:, i:i + 1]

        class Norm:
            LINKS = 7

            def __init__(self, name, per):
                self.per = per
                self.link = psem(name + "_link")
                self.rstd = psem(name + "_rstd")
                self.used = psem(name + "_used")

            def statistics(self, dve, blk, j, tiles):
                base = (blk * self.per + j) * self.LINKS
                dve.memset(spare[:, 0:1], 0.0)
                for t in range(2):
                    ins = dve.bn_stats(stats[:, t, :], tiles(t))
                ins.then_inc(self.link, 1)
                me, mo = stats[:, :, 1], stats[:, :, 4]
                dve.wait_ge(self.link, base + 1)
                dve.tensor_tensor(sm[:, 0, :], me, mo, ALU.add)
                dve.tensor_tensor(sm[:, 1, :], me, mo, ALU.subtract)
                dve.tensor_tensor(sm[:, 2, :], stats[:, :, 2], stats[:, :, 5], ALU.add).then_inc(self.link, 1)
                dve.wait_ge(self.link, base + 2)
                dve.tensor_tensor(sm[:, 3, :], sm[:, 1, :], sm[:, 1, :], ALU.mult).then_inc(self.link, 1)
                dve.tensor_scalar(sm[:, 4, :], sm[:, 0, :], 0.5, None, ALU.mult).then_inc(self.link, 1)
                dve.wait_ge(self.link, base + 4)
                dve.scalar_tensor_tensor(sm[:, 5, :], sm[:, 3, :], D / 4.0, sm[:, 2, :], ALU.mult, ALU.add).then_inc(self.link, 1)
                dve.wait_ge(self.link, base + 5)
                dve.tensor_scalar(sm[:, 6, :], sm[:, 5, :], 1.0 / D, EPS, ALU.mult, ALU.add).then_inc(self.link, 1)

            def power(self, pool, blk, j):
                pool.wait_ge(self.link, (blk * self.per + j) * self.LINKS + 6)
                pool.tensor_tensor(sm[:, 7, :], sm[:, 6, :], mhalf[:, :], ALU.pow).then_inc(self.rstd, 1)

            def result(self, dve, blk, j, outs, tiles):
                dve.wait_ge(self.rstd, blk * self.per + j + 1)
                for t in range(2):
                    ins = dve.tensor_scalar(outs(t), tiles(t), sm[:, 4, t:t + 1], sm[:, 7, t:t + 1], ALU.subtract, ALU.mult)
                ins.then_inc(self.link, 1)

            def done(self, blk, j):
                return (blk * self.per + j + 1) * self.LINKS

        def x_pair(blk, u):
            return lambda t: x_tok[:, ds(blk * 4 + (2 * u + t), 1), :]

        def transpose_pair(pe, bank, src):
            for k in range(KD):
                for t in range(2):
                    ins = pe.transpose(ps[:, bank, k * SEQ + t * P:k * SEQ + (t + 1) * P], src[:, t, k * P:(k + 1) * P], ident[:, :])
            return ins

        def store_T(act, dst, bank, blk, u):
            return act.activation(dst[:, :, ds(blk * BLK + u * SEQ, SEQ)],
                                  ps[:, bank, :].rearrange("p (k t) -> p k t", k=KD), ACT.Identity)

        def phase_setup():
            cst = psem("cst")
            dcst = psem("dcst")
            got_gates = psem("got_gates")
            ctx_in = [psem(f"ctx_in{s}") for s in range(2)]
            turned = psem("setup_turned")
            kept = [psem(f"setup_kept{j}") for j in range(4)]
            nrm = Norm("setup_norm", 2)
            ctx_rows = a["ctx"].rearrange("(t p) d -> p t d", p=P)
            cst_n = 24

            with nc.Block() as block:
                @block.sync
                def _(sp):
                    sp.dma_start(x_tok[:, :, :], a["x"].rearrange("(t p) d -> p t d", p=P)).then_inc(ld_x, 16)
                    for dst, src in ((cols, "cols"), (gatew, "gatew"), (rep, "rep")):
                        sp.dma_start(dst[:], a[src]).then_inc(ld_const, 16)
                    sp.dma_start(gates[:, :], a["g"].unsqueeze(0).broadcast_to([P, 8])).then_inc(ld_const, 16)
                    sp.dma_start(small[:, :], a["small"].unsqueeze(0).broadcast_to([P, NSMALL])).then_inc(ld_const, 16)
                    with sp.Fori(0, NB) as blk:
                        for u in range(2):
                            wait(sp, turned, blk * 4)
                            dst = prob[:, u].rearrange("p a b s -> p (a b) s")[:, 0:2, :]
                            sp.dma_start(dst, ctx_rows[:, ds(blk * 4 + 2 * u, 2), :]).then_inc(ctx_in[u], 16)
                    load_att(sp, 0, 0)
                    load_rows(sp, rowsA, "attn0", ld_rowsA)
                    load_rows(sp, rowsF, "ffn0", ld_rowsF)
                    load_expert(sp, 0, a["L0_w1"][0], a["L0_w2"][0])
                    load_expert(sp, 1, a["L0_w1"][1], a["L0_w2"][1])

                @block.gpsimd
                def _(pool):
                    ones = probT[:, 0, 0, 0:P]
                    pool.memset(ones, 1.0).then_inc(cst, 1)
                    pool.memset(mhalf[:, :], -0.5).then_inc(cst, 1)
                    pool.wait_ge(cst, 2)
                    pool.affine_select(out=ident[:, :], in_=ones, pattern=[[-1, P]], compare_op=ALU.is_equal, fill=0.0,
                                       base=0, channel_multiplier=1).then_inc(cst, 1)
                    pool.affine_select(out=identb[:, :], in_=ones, pattern=[[-1, P]], compare_op=ALU.is_equal, fill=0.0,
                                       base=0, channel_multiplier=1).then_inc(cst, 1)
                    with pool.Fori(0, NB) as blk:
                        for u in range(2):
                            nrm.power(pool, blk, u)
                    pool.memset(rt[:, 0, :, :].rearrange("p a b -> p (a b)"), 0.0).then_inc(cst, 1)
                    pool.wait_ge(cst, 5)
                    zeros = rt[:, 0, :, :].rearrange("p a b -> p (a b)")
                    pool.affine_select(out=causal[:, :], in_=zeros, pattern=[[-1, P]], compare_op=ALU.is_ge, fill=NEG,
                                       base=0, channel_multiplier=1).then_inc(cst, 1)
                    pool.affine_select(out=hmask[:, :], in_=ones[:, 0:GH], pattern=[[-HD, GH]], compare_op=ALU.is_ge, fill=0.0,
                                       base=0, channel_multiplier=1).then_inc(cst, 1)
                    pool.wait_ge(cst, 7)
                    pool.affine_select(out=hmask[:, :], in_=hmask[:, :], pattern=[[HD, GH]], compare_op=ALU.is_ge, fill=0.0,
                                       base=HD - 1, channel_multiplier=-1).then_inc(cst, 1)
                    pool.wait_ge(cst, 8)
                    pool.tensor_scalar(bmask[:, :].rearrange("p (j c) -> p j c", c=HD),
                                       hmask[:, :].unsqueeze(2).broadcast_to([P, GH, HD]), 0.25, None, ALU.mult).then_inc(cst, 1)
                    for e in range(E0 - 1):
                        pool.memset(rank[:, e:e + 1], float(E0 - 1 - e))
                    pool.memset(wbuf[:, 2, :], 0.0)
                    pool.memset(vbuf[:, :], 0.0)

                @block.vector
                def _(dve):
                    dve.wait_ge(ld_x, 16)
                    with dve.Fori(0, NB) as blk:
                        for u in range(2):
                            xp = x_pair(blk, u)
                            nrm.statistics(dve, blk, u, xp)
                            wait(dve, turned, blk * 4 + 2 * u)
                            nrm.result(dve, blk, u, lambda t: xs[:, t, :], xp)

                @block.scalar
                def _(act):
                    act.wait_ge(ld_const, 80)
                    act.activation(gates[:, :], gates[:, :], ACT.Tanh).then_inc(got_gates, 1)
                    act.mul(qbias[:, 0:2], cols[:, COLS["L0_bq"][0]:COLS["L0_bq"][0] + 2], HD ** -0.5)
                    act.mul(qbias[:, 2:4], cols[:, COLS["L3_bq"][0]:COLS["L3_bq"][0] + 2], D ** -0.5)
                    with act.Fori(0, NB) as blk:
                        for u in range(2):
                            for j, dst in ((2 * u, xnT), (2 * u + 1, ctxT)):
                                act.wait_ge(turned, blk * 4 + (j + 1))
                                store_T(act, dst, j, blk, u).then_inc(kept[j], 1)

                @block.tensor
                def _(pe):
                    pe.wait_ge(cst, 4)
                    with pe.Fori(0, NB) as blk:
                        for u in range(2):
                            pe.wait_ge(nrm.link, nrm.done(blk, u))
                            wait(pe, kept[2 * u], blk)
                            transpose_pair(pe, 2 * u, xs).then_inc(turned, 1)
                            pe.wait_ge(ctx_in[u], blk * 16 + 16)
                            wait(pe, kept[2 * u + 1], blk)
                            transpose_pair(pe, 2 * u + 1, prob[:, u].rearrange("p a b s -> p (a b) s")).then_inc(turned, 1)

        def phase_heads(l, sync_tail):
            causal_l = l == 0
            slot = l % 2
            scale = HD ** -0.5 if l == 0 else D ** -0.5
            wq, wk, wv, wo = (attw[:, slot, i] for i in range(4))
            parts = (lambda m: list(range(KD))) if l == 0 else (lambda m: [m])
            n = f"L{l}a_"
            s_full = psem(n + "s_full")
            s_read = psem(n + "s_read")
            turned_s = psem(n + "turned")
            pt_in = [psem(n + f"pt_in{hh}") for hh in range(2)]
            av = psem(n + "av")
            o_in = psem(n + "o_in")
            a_full = psem(n + "a_full")
            v_in = psem(n + "v_in")
            wo_in = psem(n + "wo_in")
            xT_in = psem(n + "xT_in")
            staged = psem(n + "staged")
            km_in = psem(n + "km_in")
            maxed = psem(n + "maxed")
            inv = psem(n + "inv")
            normed = psem(n + "normed")
            xup = psem(n + "xup")
            nrm = Norm(n + "norm", 2)
            wbd = psem(n + "wbd")
            STEPS = 16
            SF, SR = 36, 68

            def tile_full(blk, i):
                return blk * SF + (4 + i + 1)

            def tile_read(blk, i):
                return blk * SR + (4 + 2 * (i + 1))

            bo = rowsA[:, 1 if l == 0 else 0, :]

            def where(st):
                return st // 8, st // 4 % 2, st % 4

            def keys(qt):
                return P if causal_l and qt == 0 else SEQ

            with nc.Block() as block:
                @block.sync
                def _(sp):
                    sync_tail(sp)

                @block.gpsimd
                def _(pool):
                    if l == 1:
                        for i in range(3):
                            for m in range(KD):
                                ins = pool.tensor_tensor(attw[:, slot, i, m, m * P:(m + 1) * P].rearrange("p (j c) -> p j c", c=HD),
                                                         rep[:, i, :].unsqueeze(1).broadcast_to([P, GH, HD]),
                                                         hmask[:, :].unsqueeze(2).broadcast_to([P, GH, HD]), ALU.mult)
                        ins.then_inc(wbd, 1)
                    with pool.Fori(0, NB) as blk:
                        pool.wait_ge(s_read, blk * SR + 1)
                        pool.tensor_copy(stage[:, :, :], ctxT[:, :, ds(blk * BLK, BLK)]).then_inc(staged, 1)
                        for u in range(2):
                            for g in range(2):
                                pool.wait_ge(s_read, blk * SR + (3 + g))
                                if u:
                                    pool.wait_ge(s_full, tile_full(blk, 8 * g + 7))
                                pool.tensor_tensor(km[:, g], kT[:, g, u * SEQ:(u + 1) * SEQ].unsqueeze(1).broadcast_to([P, GH, SEQ]),
                                                   hmask[:, :].unsqueeze(2).broadcast_to([P, GH, SEQ]), ALU.mult).then_inc(km_in, 1)
                            if u == 1:
                                nrm.power(pool, blk, 0)
                        nrm.power(pool, blk, 1)

                @block.scalar
                def _(act):
                    def exps(blk, st):
                        for qt in range(2):
                            i = 2 * st + qt
                            kk = keys(qt)
                            act.wait_ge(maxed, blk * 32 + (2 * st + qt + 1))
                            if qt == 0:
                                wait(act, turned_s, blk * 32 + max(0, 2 * st - 2))
                            for hh in range(2):
                                ins = act.activation(prob[:, st % 2, qt, hh, 0:kk], ps[:, i % 4, hh * SEQ:hh * SEQ + kk], ACT.Exp,
                                                     bias=negmax[:, st % 2, qt, hh:hh + 1], accum_out=rowsum[:, st % 2, qt, hh:hh + 1])
                                ins.then_inc(s_read, 1)

                    def turned(blk, st):
                        act.wait_ge(turned_s, blk * 32 + (2 * st + 1))
                        wait(act, av, blk * STEPS + max(0, st - 1))
                        s = (2 * st) % 4
                        if causal_l:
                            act.activation(probT[:, s, 0, :], ps[:, 4, 0:SEQ], ACT.Identity)
                            act.activation(probT[:, s, 1, P:], ps[:, 4, SEQ + P:], ACT.Identity).then_inc(pt_in[0], 1)
                        else:
                            act.activation(probT[:, s].rearrange("p a b -> p (a b)"), ps[:, 4, :], ACT.Identity).then_inc(pt_in[0], 1)

                    def context(blk, i):
                        act.wait_ge(av, blk * STEPS + 4 * (i + 1))
                        wait(act, a_full, blk * 6 + (0 if i < 2 else 3))
                        act.activation(oT[:, i % 2, :], ps[:, 6, 0:SEQ], ACT.Identity).then_inc(o_in, 1)

                    def norm_T(blk, u):
                        act.wait_ge(a_full, blk * 6 + (4 + 2 * u))
                        store_T(act, xnT, 7, blk, u).then_inc(xT_in, 1)

                    with act.Fori(0, NB) as blk:
                        for j in range(4):
                            m = j % 2
                            act.wait_ge(s_full, blk * SF + (j + 1))
                            if j < 2:
                                bias = qbias[:, m:m + 1] if l == 0 else 0.0
                                act.activation(qT[:, m, :], ps[:, j, :], ACT.Identity, bias=bias, scale=scale).then_inc(s_read, 1)
                            else:
                                wait(act, km_in, blk * 4)
                                bias = col("L0_bk", m) if l == 0 else 0.0
                                act.activation(kT[:, m, :], ps[:, j, :], ACT.Identity, bias=bias).then_inc(s_read, 1)
                        exps(blk, 0)
                        for st in range(STEPS):
                            if st + 1 < STEPS:
                                exps(blk, st + 1)
                            if st >= 5 and (st - 5) % 4 == 0:
                                context(blk, (st - 5) // 4)
                            turned(blk, st)
                            if st == 14:
                                norm_T(blk, 0)
                        context(blk, 3)
                        norm_T(blk, 1)

                @block.vector
                def _(dve):
                    def maxima(blk, st):
                        for qt in range(2):
                            i = 2 * st + qt
                            kk = keys(qt)
                            dve.wait_ge(s_full, tile_full(blk, i))
                            dve.tensor_reduce(negmax[:, st % 2, qt, :], ps[:, i % 4, :].rearrange("p (h s) -> p h s", h=2)[:, :, 0:kk],
                                              AXX, ALU.max, negate=True).then_inc(maxed, 1)

                    def normalise(blk, st):
                        for qt in range(2):
                            kk = keys(qt)
                            dve.wait_ge(s_read, tile_read(blk, 2 * st + qt))
                            dve.reciprocal(rinv[:, st % 2, qt, :], rowsum[:, st % 2, qt, :]).then_inc(inv, 1)
                            dve.wait_ge(inv, blk * 32 + 2 * st + qt + 1)
                            for hh in range(2):
                                p = prob[:, st % 2, qt, hh, 0:kk]
                                ins = dve.tensor_scalar(p, p, rinv[:, st % 2, qt, hh:hh + 1], None, ALU.mult)
                            ins.then_inc(normed, 1)

                    def turned(blk, st):
                        dve.wait_ge(turned_s, blk * 32 + (2 * st + 2))
                        wait(dve, av, blk * STEPS + max(0, st - 1))
                        s = (2 * st + 1) % 4
                        if causal_l:
                            dve.tensor_copy(probT[:, s, 0, :], ps[:, 5, 0:SEQ])
                            dve.tensor_copy(probT[:, s, 1, P:], ps[:, 5, SEQ + P:]).then_inc(pt_in[1], 1)
                        else:
                            dve.tensor_copy(probT[:, s].rearrange("p a b -> p (a b)"), ps[:, 5, :]).then_inc(pt_in[1], 1)

                    def values(blk, u):
                        dve.wait_ge(a_full, blk * 6 + (u + 1))
                        for t in range(2):
                            whole = vm[u][:, t].rearrange("p h c -> p (h c)")
                            for g in range(2):
                                o = g * GH * P
                                dst = whole[:, o:o + GH * P].rearrange("p (j c) -> p j c", c=P)
                                dst = bass.AP(dst.tensor, dst.offset, [dst.ap[0], [P + HD, GH], [1, HD]])
                                src = ps[:, 7, t * SEQ + g * P:t * SEQ + (g + 1) * P].rearrange("p (j c) -> p j c", c=HD)
                                if l == 0:
                                    row = rowsA[:, 0, g * P:(g + 1) * P].rearrange("p (j c) -> p j c", c=HD)
                                    ins = dve.tensor_tensor(dst, src, row, ALU.add)
                                else:
                                    ins = dve.tensor_copy(dst, src)
                        ins.then_inc(v_in, 1)

                    def update(blk, u):
                        dve.wait_ge(a_full, blk * 6 + (3 + 2 * u))
                        xp = x_pair(blk, u)
                        for t in range(2):
                            ins = dve.scalar_tensor_tensor(xp(t)[:, 0, :], ps[:, 7, t * D:(t + 1) * D], gate(l), xp(t)[:, 0, :],
                                                           ALU.mult, ALU.add)
                        ins.then_inc(wo_in, 1)
                        dve.wait_ge(wo_in, blk * 2 + (u + 1))
                        for t in range(2):
                            ins = dve.scalar_tensor_tensor(xp(t)[:, 0, :], bo, gate(l), xp(t)[:, 0, :], ALU.mult, ALU.add)
                        ins.then_inc(xup, 1)
                        dve.wait_ge(xup, blk * 2 + (u + 1))
                        nrm.statistics(dve, blk, u, xp)
                        wait(dve, a_full, blk * 6 + (0 if u == 0 else 4))
                        nrm.result(dve, blk, u, lambda t: xs[:, t, :], xp)

                    dve.wait_ge(ld_rowsA, 16 * (l + 1))
                    with dve.Fori(0, NB) as blk:
                        values(blk, 0)
                        maxima(blk, 0)
                        for st in range(STEPS):
                            if st == 0:
                                values(blk, 1)
                            if st + 1 < STEPS:
                                maxima(blk, st + 1)
                            normalise(blk, st)
                            turned(blk, st)
                            if st == 10:
                                update(blk, 0)
                        update(blk, 1)

                @block.tensor
                def _(pe):
                    def scores(blk, st):
                        u, g, p = where(st)
                        for qt in range(2):
                            i = 2 * st + qt
                            kk = keys(qt)
                            if p == 0 and qt == 0:
                                pe.wait_ge(km_in, blk * 4 + (2 * u + g + 1))
                            pe.wait_ge(s_read, blk * SR + 4 if i < 4 else tile_read(blk, i - 4))
                            bank = ps[:, i % 4, :].rearrange("p (h s) -> p h s", h=2)
                            ins = pe.matmul(bank[:, :, 0:kk], qT[:, g, u * SEQ + qt * P:u * SEQ + (qt + 1) * P],
                                            km[:, g, 2 * p:2 * p + 2, 0:kk], start=True, stop=not causal_l)
                            if causal_l:
                                ins = pe.matmul(bank[:, :, qt * P:(qt + 1) * P], identb[:, :],
                                                causal[:, :].unsqueeze(1).broadcast_to([P, 2, P]), start=False, stop=True)
                            ins.then_inc(s_full, 1)

                    def turn(blk, st):
                        for hh in range(2):
                            wait(pe, pt_in[hh], blk * STEPS + st)
                            if hh == 0:
                                pe.wait_ge(normed, blk * 32 + (2 * st + 2))
                            for kt in range(2):
                                for qt in range(2):
                                    if causal_l and kt > qt:
                                        continue
                                    o = kt * SEQ + qt * P
                                    ins = pe.transpose(ps[:, 4 + hh, o:o + P], prob[:, st % 2, qt, hh, kt * P:(kt + 1) * P], ident[:, :])
                            ins.then_inc(turned_s, 1)

                    def attend(blk, st):
                        u, g, p = where(st)
                        if p == 0:
                            wait(pe, o_in, blk * 4 + (2 * u + g))
                            if g == 0:
                                pe.wait_ge(v_in, blk * 2 + (u + 1))
                        for hh in range(2):
                            pe.wait_ge(pt_in[hh], blk * STEPS + (st + 1))
                            for kt in range(2):
                                q0 = P if causal_l and kt == 1 else 0
                                ins = pe.matmul(ps[:, 6, q0:SEQ], vm[u][:, kt, g * GH + 2 * p + hh, :],
                                                probT[:, (2 * st + hh) % 4, kt, q0:], start=(p == 0 and hh == 0 and kt == 0),
                                                stop=(p == 3 and hh == 1 and kt == 1))
                        ins.then_inc(av, 1)

                    def project_out(blk, u):
                        pe.wait_ge(*((v_in, blk * 2 + 2) if u == 0 else (xT_in, blk * 2 + 1)))
                        pe.wait_ge(o_in, blk * 4 + (2 * u + 2))
                        for t in range(2):
                            for g in range(2):
                                ins = pe.matmul(ps[:, 7, t * D:(t + 1) * D], oT[:, g, t * P:(t + 1) * P], wo[:, g, :],
                                                start=(g == 0), stop=(g == 1))
                        ins.then_inc(a_full, 1)

                    def norm_T(blk, u):
                        pe.wait_ge(nrm.link, nrm.done(blk, u))
                        transpose_pair(pe, 7, xs).then_inc(a_full, 1)

                    pe.wait_ge(ld_att[slot], 16)
                    if l == 1:
                        pe.wait_ge(wbd, 1)
                    with pe.Fori(0, NB) as blk:
                        for j in range(4):
                            m = j % 2
                            w, src = (wq, xnT) if j < 2 else (wk, ctxT)
                            for k in parts(m):
                                ins = pe.matmul(ps[:, j, :], w[:, k, m * P:(m + 1) * P], src[:, k, ds(blk * BLK, BLK)],
                                                start=(k == parts(m)[0]), stop=(k == parts(m)[-1]))
                            ins.then_inc(s_full, 1)
                        pe.wait_ge(staged, blk + 1)
                        for u in range(2):
                            wait(pe, *((xT_in, blk * 2) if u == 0 else (v_in, blk * 2 + 1)))
                            for t in range(2):
                                lhs = [stage[:, k, (2 * u + t) * P:(2 * u + t + 1) * P] for k in range(KD)]
                                if l == 0:
                                    for k in range(KD):
                                        ins = pe.matmul(ps[:, 7, t * D:(t + 1) * D], lhs[k], wv[:, k, :], start=(k == 0), stop=(k == KD - 1))
                                else:
                                    for k in range(KD):
                                        ins = pe.matmul(ps[:, 7, t * D + k * P:t * D + (k + 1) * P], lhs[k], wv[:, k, k * P:(k + 1) * P],
                                                        start=True, stop=True)
                            ins.then_inc(a_full, 1)
                            if u == 0:
                                scores(blk, 0)
                        for st in range(STEPS):
                            if st + 1 < STEPS:
                                scores(blk, st + 1)
                            turn(blk, st)
                            if st:
                                attend(blk, st - 1)
                            if st == 10:
                                project_out(blk, 0)
                            if st == 14:
                                norm_T(blk, 0)
                        attend(blk, STEPS - 1)
                        project_out(blk, 1)
                        norm_T(blk, 1)

        def phase_experts(l, n_exp, func, gi, first_load, keep, sync_body):
            n = f"L{l}f_"
            n_log = E0 - 1 if l == 0 else E1
            go = 0 if l == 0 else E0 - 1
            h_full = psem(n + "h_full")
            h_in = psem(n + "h_in")
            y_full = psem(n + "y_full")
            y_in = [psem(n + f"y_in{tp}") for tp in range(2)]
            n_full = psem(n + "n_full")
            xT_in = psem(n + "xT_in")
            staged = psem(n + "staged")
            routed = psem(n + "routed")
            xup = psem(n + "xup")
            link = psem(n + "link")
            expw = psem(n + "expw")
            nrm = Norm(n + "norm", 2)
            copied = psem(n + "copied")
            b1 = f"L{l}_b1"

            def sched(eng, body, last):
                pairs, single = (n_exp - 1) // 2, (n_exp - 1) % 2
                with eng.Fori(0, pairs) as ep:
                    for v in range(2):
                        with eng.Fori(0, NB) as blk:
                            body(ep * 2 + v, v, blk, (ep * 2 + v) * NB + blk)
                if single:
                    with eng.Fori(0, NB) as blk:
                        body(2 * pairs, 0, blk, blk + 2 * pairs * NB)
                with eng.Fori(0, NB) as blk:
                    last(n_exp - 1, (n_exp - 1) % 2, blk, blk + (n_exp - 1) * NB)

            def wslot(v):
                return (first_load + v) % 2

            with nc.Block() as block:
                @block.sync
                def _(sp):
                    sync_body(sp, y_full, wslot)

                @block.gpsimd
                def _(pool):
                    with pool.Fori(0, NB) as blk:
                        wait(pool, routed, blk)
                        pool.tensor_copy(stage[:, :, :], xnT[:, :, ds(blk * BLK, BLK)]).then_inc(staged, 1)
                    with pool.Fori(0, NB) as blk:
                        for u in range(2):
                            nrm.power(pool, blk, u)
                            if keep:
                                pool.wait_ge(nrm.link, nrm.done(blk, u))
                                pool.tensor_copy(xn_tok[:, ds(blk * 4 + 2 * u, 2), :], xs[:, :, :]).then_inc(copied, 1)

                @block.scalar
                def _(act):
                    def body(e, v, blk, s):
                        for f in range(NF):
                            act.wait_ge(h_full, s * NF + (f + 1))
                            act.activation(hT[:, f, :], ps[:, f % 4, :], func, bias=col(b1, e * NF + f)).then_inc(h_in, 1)

                    def last(e, v, blk, s):
                        body(e, v, blk, s)
                        for u in range(2):
                            act.wait_ge(n_full, blk * 2 + (u + 1))
                            store_T(act, xnT, 6, blk, u).then_inc(xT_in, 1)

                    if l == 0:
                        act.wait_ge(link, 13)
                        act.activation(r1[:, 5, :], r1[:, 4, :], ACT.Exp).then_inc(expw, 1)
                    sched(act, body, last)

                @block.vector
                def _(dve):
                    count = [0]

                    def step(ins):
                        count[0] += 1
                        ins.then_inc(link, 1)
                        dve.wait_ge(link, count[0])

                    def wide(i):
                        return rt[:, i, :, 0:n_log]

                    def over(v):
                        return v.unsqueeze(2).broadcast_to([P, NT, n_log])

                    lg = logit[:, :, 0:n_log]
                    order = rank[:, 0:n_log].unsqueeze(1).broadcast_to([P, NT, n_log])

                    def one_hot(src, mx, dst):
                        step(dve.tensor_reduce(mx, src, AXX, ALU.max))
                        step(dve.tensor_tensor(dst, src, over(mx), ALU.is_equal))
                        step(dve.tensor_tensor(dst, dst, order, ALU.mult))
                        step(dve.tensor_reduce(r1[:, 7, :], dst, AXX, ALU.max))
                        step(dve.tensor_tensor(dst, dst, over(r1[:, 7, :]), ALU.is_equal))

                    dve.wait_ge(ld_rowsF, 16 * (l + 1))
                    dve.wait_ge(routed, NB)
                    raw = ps[:, 7, 0:NT * n_log].rearrange("p (t e) -> p t e", e=n_log)
                    combT = comb[:, 0:n_log, :].rearrange("p e t -> p t e")
                    if l == 0:
                        step(dve.tensor_copy(lg, raw))
                        one_hot(lg, r1[:, 0, :], wide(0))
                        step(dve.scalar_tensor_tensor(wide(1).rearrange("p t e -> p (t e)"), wide(0).rearrange("p t e -> p (t e)"), -BIG,
                                                      lg.rearrange("p t e -> p (t e)"), ALU.mult, ALU.add))
                        one_hot(wide(1), r1[:, 1, :], wide(2))
                        step(dve.tensor_tensor(r1[:, 4, :], r1[:, 1, :], r1[:, 0, :], ALU.subtract))
                        assert count[0] == 13
                        dve.wait_ge(expw, 1)
                        step(dve.tensor_scalar(r1[:, 6, :], r1[:, 5, :], 1.0, None, ALU.add))
                        step(dve.reciprocal(r1[:, 2, :], r1[:, 6, :]))
                        step(dve.tensor_scalar(r1[:, 2, :], r1[:, 2, :], gate(gi), None, ALU.mult))
                        step(dve.tensor_tensor(r1[:, 3, :], r1[:, 5, :], r1[:, 2, :], ALU.mult))
                        step(dve.tensor_tensor(wide(0), wide(0), over(r1[:, 2, :]), ALU.mult))
                        step(dve.tensor_tensor(wide(2), wide(2), over(r1[:, 3, :]), ALU.mult))
                        step(dve.tensor_tensor(combT, wide(0), wide(2), ALU.add))
                        step(dve.tensor_scalar(comb[:, E0 - 1, :], r1[:, 0, :], 0.0, gate(gi), ALU.mult, ALU.add))
                    else:
                        bg = small[:, 0:E1].unsqueeze(1).broadcast_to([P, NT, E1])
                        step(dve.tensor_tensor(lg, raw, bg, ALU.add))
                        one_hot(lg, r1[:, 0, :], wide(0))
                        step(dve.tensor_scalar(combT, wide(0), gate(gi), None, ALU.mult))

                    def body(e, v, blk, s):
                        dve.wait_ge(xup, s * 2)
                        for tp in range(2):
                            dve.wait_ge(y_full, s * 2 + (tp + 1))
                            for t in range(2):
                                i = blk * 4 + (2 * tp + t)
                                x = x_tok[:, ds(i, 1), :][:, 0, :]
                                ins = dve.scalar_tensor_tensor(x, ps[:, 4 + tp, t * D:(t + 1) * D], comb_at(e, i), x, ALU.mult, ALU.add)
                            ins.then_inc(y_in[tp], 1)
                            dve.wait_ge(y_in[tp], s + 1)
                            for t in range(2):
                                i = blk * 4 + (2 * tp + t)
                                x = x_tok[:, ds(i, 1), :][:, 0, :]
                                b2 = rowsF[:, e, :] if isinstance(e, int) else rowsF[:, ds(e, 1), :][:, 0, :]
                                ins = dve.scalar_tensor_tensor(x, b2, comb_at(e, i), x, ALU.mult, ALU.add)
                            ins.then_inc(xup, 1)

                    def comb_at(e, i):
                        flat = comb[:, :, :].rearrange("p e t -> p (e t)")
                        return flat[:, ds(i + e * NT, 1)]

                    def last(e, v, blk, s):
                        body(e, v, blk, s)
                        dve.wait_ge(xup, s * 2 + 2)
                        for u in range(2):
                            xp = x_pair(blk, u)
                            nrm.statistics(dve, blk, u, xp)
                            wait(dve, n_full, blk * 2 + u)
                            if keep:
                                wait(dve, copied, blk * 2 + u)
                            nrm.result(dve, blk, u, lambda t: xs[:, t, :], xp)

                    sched(dve, body, last)

                @block.tensor
                def _(pe):
                    def gate_logits():
                        with pe.Fori(0, NB) as blk:
                            pe.wait_ge(staged, blk + 1)
                            for t in range(4):
                                for k in range(KD):
                                    ins = pe.matmul(ps[:, 7, ds(blk * 4 * n_log + t * n_log, n_log)], stage[:, k, t * P:(t + 1) * P],
                                                    gatew[:, k, go:go + n_log], start=(k == 0), stop=(k == KD - 1))
                            ins.then_inc(routed, 1)

                    def body(e, v, blk, s):
                        sl = wslot(v)
                        loads = (first_load + e) // 2 if isinstance(e, int) else None
                        if isinstance(e, int):
                            pe.wait_ge(ld_w[sl], 32 * ((first_load + e) // 2 + 1))
                        else:
                            base = (first_load + v) // 2
                            pe.wait_ge(ld_w[sl], ((e - v) * 16) + 32 * (base + 1))
                        for f in range(NF):
                            if f >= 4:
                                pe.wait_ge(h_in, s * NF + (f - 3))
                            for k in range(KD):
                                ins = pe.matmul(ps[:, f % 4, :], w1[sl][:, k, f * P:(f + 1) * P], xnT[:, k, ds(blk * BLK, BLK)],
                                                start=(k == 0), stop=(k == KD - 1))
                            ins.then_inc(h_full, 1)
                        for tp in range(2):
                            wait(pe, y_in[tp], s)
                            for t in range(2):
                                for f in range(NF):
                                    if tp == 0 and t == 0:
                                        pe.wait_ge(h_in, s * NF + (f + 1))
                                    ins = pe.matmul(ps[:, 4 + tp, t * D:(t + 1) * D], hT[:, f, (2 * tp + t) * P:(2 * tp + t + 1) * P],
                                                    w2[sl][:, f, :], start=(f == 0), stop=(f == NF - 1))
                            ins.then_inc(y_full, 1)

                    def last(e, v, blk, s):
                        body(e, v, blk, s)
                        for u in range(2):
                            wait(pe, xT_in, blk * 2 + u)
                            pe.wait_ge(nrm.link, nrm.done(blk, u))
                            transpose_pair(pe, 6, xs).then_inc(n_full, 1)

                    gate_logits()
                    sched(pe, body, last)

        def scale_and_add(dve, link, base, g_row, b_row, blk, u, gate_of):
            both = ts[:, :, :]
            dve.tensor_tensor(both, both, g_row.unsqueeze(1).broadcast_to([P, 2, D]), ALU.mult).then_inc(link, 1)
            dve.wait_ge(link, base + 1)
            dve.tensor_tensor(both, both, b_row.unsqueeze(1).broadcast_to([P, 2, D]), ALU.add).then_inc(link, 1)
            dve.wait_ge(link, base + 2)
            xp = x_pair(blk, u)
            for t in range(2):
                x = xp(t)[:, 0, :]
                ins = dve.scalar_tensor_tensor(x, ts[:, t, :], gate_of(t), x, ALU.mult, ALU.add)
            ins.then_inc(link, 1)
            dve.wait_ge(link, base + 3)

        def phase_linear(sync_tail):
            n = "L2a_"
            wq, wk, wv, wo = (attw[:, 0, i] for i in range(4))
            ktok = prob[:, 0].rearrange("p a b s -> p (a b) s")
            vt = prob[:, 1].rearrange("p a b s -> p (a b) s")
            kv = probT[:, 0]
            staged = psem(n + "staged")
            q_full = psem(n + "q_full")
            q_in = psem(n + "q_in")
            t_full = psem(n + "t_full")
            t_in = psem(n + "t_in")
            kv_full = psem(n + "kv_full")
            kv_in = psem(n + "kv_in")
            c_full = psem(n + "c_full")
            c_in = psem(n + "c_in")
            o_full = psem(n + "o_full")
            o_in = psem(n + "o_in")
            sums = psem(n + "sums")
            n_full = psem(n + "n_full")
            xT_in = psem(n + "xT_in")
            ld_mask = psem(n + "ld_mask")
            link = psem(n + "link")
            poison = psem(n + "poison")
            post, nrm = Norm(n + "post", 2), Norm(n + "norm", 2)
            mask8 = rowsF[:, :, :].rearrange("p a b -> p (a b)")[:, 0:1024].bitcast(U8).rearrange("p (t k) -> p t k", t=NT)

            with nc.Block() as block:
                @block.sync
                def _(sp):
                    sp.dma_start(mask8, a["mask"].rearrange("(t p) k -> p t k", p=P)).then_inc(ld_mask, 16)
                    sync_tail(sp)

                @block.gpsimd
                def _(pool):
                    with pool.Fori(0, NB) as blk:
                        pool.wait_ge(q_full, blk * 2 + 1)
                        pool.tensor_copy(stage[:, :, :], ctxT[:, :, ds(blk * BLK, BLK)]).then_inc(staged, 1)
                        for u in range(2):
                            post.power(pool, blk, u)
                            nrm.power(pool, blk, u)

                @block.scalar
                def _(act):
                    with act.Fori(0, NB) as blk:
                        for m in range(KD):
                            act.wait_ge(q_full, blk * 2 + (m + 1))
                            act.activation(qT[:, m, :], ps[:, m, :], ACT.Identity, bias=col("L2_bq", m)).then_inc(q_in, 1)
                        for u in range(2):
                            act.wait_ge(c_full, blk * 2 + (u + 1))
                            act.activation(kT[:, :, u * SEQ:(u + 1) * SEQ], ps[:, u, :].rearrange("p (m q) -> p m q", m=KD),
                                           ACT.Identity).then_inc(c_in, 1)
                        for u in range(2):
                            act.wait_ge(n_full, blk * 2 + (u + 1))
                            store_T(act, xnT, 4 + u, blk, u).then_inc(xT_in, 1)

                @block.vector
                def _(dve):
                    dve.wait_ge(ld_mask, 16)
                    dve.tensor_reduce(anym[:, 0, :], mask8, AXX, ALU.max).then_inc(poison, 1)
                    dve.wait_ge(poison, 1)
                    dve.tensor_scalar(anym[:, 0, :], anym[:, 0, :], 3.0e38, 3.0e38, ALU.mult, ALU.mult).then_inc(poison, 1)
                    dve.wait_ge(poison, 2)
                    dve.tensor_tensor(anym[:, 1, :], anym[:, 0, :], anym[:, 0, :], ALU.subtract).then_inc(poison, 1)
                    dve.wait_ge(poison, 3)
                    dve.tensor_scalar(anym[:, 1, :], anym[:, 1, :], gate(2), None, ALU.add).then_inc(poison, 1)
                    dve.wait_ge(poison, 4)
                    dve.wait_ge(ld_rowsA, 48)
                    with dve.Fori(0, NB) as blk:
                        for u in range(2):
                            for i, dst in enumerate((ktok, vt)):
                                dve.wait_ge(t_full, blk * 4 + (2 * u + i + 1))
                                dve.tensor_tensor(dst[:, 2 * u:2 * u + 2, :], ps[:, 2 + u + 2 * i, :].rearrange("p (t d) -> p t d", t=2),
                                                  rowsA[:, i, :].unsqueeze(1).broadcast_to([P, 2, D]), ALU.add).then_inc(t_in, 1)
                        dve.wait_ge(kv_full, blk + 1)
                        dve.tensor_tensor(kv.rearrange("p a (m d) -> p (a m) d", m=2), ps[:, 6, :].rearrange("p (a d) -> p a d", a=4),
                                          bmask[:, :].unsqueeze(1).broadcast_to([P, 4, P]), ALU.mult).then_inc(kv_in, 1)
                        for u in range(2):
                            dve.wait_ge(o_full, blk * 2 + (u + 1))
                            dve.tensor_tensor(ts[:, :, :], ps[:, 2 + u, :].rearrange("p (t d) -> p t d", t=2),
                                              rowsA[:, 2, :].unsqueeze(1).broadcast_to([P, 2, D]), ALU.add).then_inc(o_in, 1)
                            dve.wait_ge(o_in, blk * 2 + (u + 1))
                            dve.tensor_tensor(ts[:, :, :], ts[:, :, :], xn_tok[:, ds(blk * 4 + 2 * u, 2), :], ALU.add).then_inc(sums, 1)
                            dve.wait_ge(sums, blk * 2 + (u + 1))
                            tp = lambda t: ts[:, t, :]
                            post.statistics(dve, blk, u, tp)
                            post.result(dve, blk, u, tp, tp)
                            dve.wait_ge(post.link, post.done(blk, u))
                            poisoned = lambda t: anym[:, 1, ds(blk * 4 + (2 * u + t), 1)]
                            scale_and_add(dve, link, (blk * 2 + u) * 3, rowsA[:, 3, :], rowsA[:, 4, :], blk, u, poisoned)
                            xp = x_pair(blk, u)
                            nrm.statistics(dve, blk, u, xp)
                            wait(dve, n_full, blk * 2 + u)
                            nrm.result(dve, blk, u, lambda t: xs[:, t, :], xp)

                @block.tensor
                def _(pe):
                    pe.wait_ge(ld_att[0], 32)
                    with pe.Fori(0, NB) as blk:
                        for m in range(KD):
                            for k in range(KD):
                                ins = pe.matmul(ps[:, m, :], wq[:, k, m * P:(m + 1) * P], xnT[:, k, ds(blk * BLK, BLK)],
                                                start=(k == 0), stop=(k == KD - 1))
                            ins.then_inc(q_full, 1)
                        pe.wait_ge(staged, blk + 1)
                        wait(pe, xT_in, blk * 2)
                        for u in range(2):
                            for i, w in enumerate((wk, wv)):
                                for t in range(2):
                                    for k in range(KD):
                                        ins = pe.matmul(ps[:, 2 + u + 2 * i, t * D:(t + 1) * D], stage[:, k, (2 * u + t) * P:(2 * u + t + 1) * P],
                                                        w[:, k, :], start=(k == 0), stop=(k == KD - 1))
                                ins.then_inc(t_full, 1)
                        for u in range(2):
                            pe.wait_ge(t_in, blk * 4 + (2 * u + 2))
                            for m in range(KD):
                                for t in range(2):
                                    ins = pe.matmul(ps[:, 6, u * SEQ + m * P:u * SEQ + (m + 1) * P], ktok[:, 2 * u + t, m * P:(m + 1) * P],
                                                    vt[:, 2 * u + t, m * P:(m + 1) * P], start=(t == 0), stop=(t == 1))
                        ins.then_inc(kv_full, 1)
                        pe.wait_ge(q_in, blk * 2 + 2)
                        pe.wait_ge(kv_in, blk + 1)
                        for u in range(2):
                            for m in range(KD):
                                ins = pe.matmul(ps[:, u, m * SEQ:(m + 1) * SEQ], kv[:, u, m * P:(m + 1) * P],
                                                qT[:, m, u * SEQ:(u + 1) * SEQ], start=True, stop=True)
                            ins.then_inc(c_full, 1)
                        for u in range(2):
                            pe.wait_ge(c_in, blk * 2 + (u + 1))
                            for t in range(2):
                                for m in range(KD):
                                    ins = pe.matmul(ps[:, 2 + u, t * D:(t + 1) * D], kT[:, m, u * SEQ + t * P:u * SEQ + (t + 1) * P],
                                                    wo[:, m, :], start=(m == 0), stop=(m == 1))
                            ins.then_inc(o_full, 1)
                        for u in range(2):
                            pe.wait_ge(nrm.link, nrm.done(blk, u))
                            transpose_pair(pe, 4 + u, xs).then_inc(n_full, 1)

        class Single:

            def __init__(self, n):
                self.s_full = psem(n + "s_full")
                self.maxed = psem(n + "maxed")
                self.e_in = psem(n + "e_in")
                self.p_full = psem(n + "p_full")
                self.p_in = psem(n + "p_in")

            def scores(self, pe, blk):
                for u in range(2):
                    for qt in range(2):
                        for k in range(KD):
                            ins = pe.matmul(ps[:, 2 * u + qt, 0:SEQ], qT[:, k, u * SEQ + qt * P:u * SEQ + (qt + 1) * P],
                                            kT[:, k, u * SEQ:(u + 1) * SEQ], start=(k == 0), stop=(k == KD - 1))
                        ins.then_inc(self.s_full, 1)

            def turn(self, pe, blk):
                for u in range(2):
                    pe.wait_ge(self.e_in, blk * 4 + (2 * u + 2))
                    for kt in range(2):
                        for qt in range(2):
                            ins = pe.transpose(ps[:, 6 + u, kt * SEQ + qt * P:kt * SEQ + (qt + 1) * P],
                                               prob[:, u, qt, 0, kt * P:(kt + 1) * P], ident[:, :])
                    ins.then_inc(self.p_full, 1)

            def exps(self, act, blk, from_psum):
                for u in range(2):
                    for qt in range(2):
                        act.wait_ge(self.maxed, blk * 4 + (2 * u + qt + 1))
                        dst = prob[:, u, qt, 0, :]
                        src = ps[:, 2 * u + qt, 0:SEQ] if from_psum else prob[:, u, qt, 1, :]
                        act.activation(dst, src, ACT.Exp, bias=negmax[:, u, qt, 0:1], accum_out=rowsum[:, u, qt, 0:1]).then_inc(self.e_in, 1)

            def turned(self, act, blk):
                for u in range(2):
                    act.wait_ge(self.p_full, blk * 2 + (u + 1))
                    act.activation(probT[:, u].rearrange("p a b -> p (a b)"), ps[:, 6 + u, :], ACT.Identity).then_inc(self.p_in, 1)

        vtok = rowsF[:, 4:8, :]

        def phase_trees(sync_tail):
            n = "L2f_"
            staged = psem(n + "staged")
            node_full = psem(n + "node_full")
            link = psem(n + "link")
            sel_full = psem(n + "sel_full")
            sel_in = psem(n + "sel_in")
            selm_in = psem(n + "selm_in")
            h_full = psem(n + "h_full")
            h_in = psem(n + "h_in")
            y_full = psem(n + "y_full")
            y_in = psem(n + "y_in")
            o_full = psem(n + "o_full")
            o_in = psem(n + "o_in")
            rg = psem(n + "rg")
            n_full = psem(n + "n_full")
            xT_in = psem(n + "xT_in")
            cst = psem(n + "cst")
            cleared = psem(n + "cleared")
            ld_b2 = psem(n + "ld_b2")
            nrm = Norm(n + "norm", 2)
            at = Single(n)
            LINKS = 10

            with nc.Block() as block:
                @block.sync
                def _(sp):
                    sp.wait_ge(cleared, 2)
                    for t in range(TREES):
                        sp.dma_start(b2pad[32 * t:32 * t + NLEAF, t, :], a["L2_b2"][t]).then_inc(ld_b2, 16)
                    sync_tail(sp)

                @block.gpsimd
                def _(pool):
                    pool.memset(selpad, 0.0).then_inc(cleared, 1)
                    pool.memset(b2pad[:, :, :], 0.0).then_inc(cleared, 1)
                    pool.tensor_copy(stage[:, :, :], xnT[:, :, 0:BLK]).then_inc(staged, 1)
                    pool.memset(leafw[:, :, :], BIG).then_inc(cst, 1)
                    for t in range(TREES):
                        pool.wait_ge(cst, 2 * t + 1)
                        pool.affine_select(out=leafw[:, t, :], in_=leafw[:, t, :], pattern=[[1, F]], compare_op=ALU.is_ge, fill=0.0,
                                           base=LEAFW * 32 * t, channel_multiplier=-LEAFW).then_inc(cst, 1)
                        pool.wait_ge(cst, 2 * t + 2)
                        pool.affine_select(out=leafw[:, t, :], in_=leafw[:, t, :], pattern=[[-1, F]], compare_op=ALU.is_ge, fill=0.0,
                                           base=LEAFW - 1 - LEAFW * 32 * t, channel_multiplier=LEAFW).then_inc(cst, 1)
                    with pool.Fori(0, NB - 1) as blk:
                        pool.wait_ge(node_full, blk + 1)
                        pool.tensor_copy(stage[:, :, :], xnT[:, :, ds(blk * BLK + BLK, BLK)]).then_inc(staged, 1)
                        for u in range(2):
                            nrm.power(pool, blk, u)
                    for u in range(2):
                        nrm.power(pool, NB - 1, u)

                @block.scalar
                def _(act):
                    with act.Fori(0, NB) as blk:
                        act.wait_ge(sel_full, blk + 1)
                        act.activation(selT, ps[:, 7, :], ACT.Identity).then_inc(sel_in, 1)
                        for t in range(TREES):
                            for f in range(NF):
                                act.wait_ge(h_full, blk * 24 + (8 * t + f + 1))
                                act.activation(hT[:, f, :], ps[:, f % 4, :], ACT.Relu, bias=col("L2_b1", t * NF + f)).then_inc(h_in, 1)
                            for i in range(2):
                                act.wait_ge(y_full, blk * 6 + (2 * t + i + 1))
                                if t < 2:
                                    act.activation((qT, kT)[t][:, i, :], ps[:, 4 + i, :], ACT.Identity, scale=(D ** -0.5 if t == 0 else 1.0)).then_inc(y_in, 1)
                                else:
                                    act.activation(vtok[:, 2 * i:2 * i + 2, :], ps[:, 4 + i, :].rearrange("p (t d) -> p t d", t=2),
                                                   ACT.Identity).then_inc(y_in, 1)
                        at.exps(act, blk, True)
                        at.turned(act, blk)
                        for u in range(2):
                            act.wait_ge(n_full, blk * 2 + (u + 1))
                            store_T(act, xnT, 6 + u, blk, u).then_inc(xT_in, 1)

                @block.vector
                def _(dve):
                    dve.wait_ge(cleared, 1)
                    with dve.Fori(0, NB) as blk:
                        count = [0]

                        def step(ins):
                            count[0] += 1
                            ins.then_inc(link, 1)
                            dve.wait_ge(link, blk * LINKS + count[0])

                        dve.wait_ge(node_full, blk + 1)
                        nodes = dec[:, :, :, 0:NODES]
                        raw = ps[:, 6, 0:4 * TREES * NODES].rearrange("p (t j) -> p t j", t=4)
                        nb = small[:, E1:].unsqueeze(1).broadcast_to([P, 4, TREES * NODES])
                        flat = rt[:, 0:2, :, :].rearrange("p a b c -> p (a b c)")[:, 0:4 * TREES * NODES]
                        step(dve.tensor_tensor(flat.rearrange("p (t j) -> p t j", t=4), raw, nb, ALU.add))
                        step(dve.tensor_scalar(nodes, flat.rearrange("p (t r j) -> p t r j", t=4, r=TREES), 0.0, None, ALU.is_ge))
                        step(dve.tensor_copy(path[:, 0, :, :, 1:2], dec[:, :, :, 0:1]))
                        step(dve.tensor_scalar(path[:, 0, :, :, 0:1], dec[:, :, :, 0:1], -1.0, 1.0, ALU.mult, ALU.add))
                        for lev in range(1, DEPTH):
                            w = 1 << lev
                            src = path[:, (lev + 1) % 2, :, :, 0:w]
                            if lev == DEPTH - 1:
                                dst = selpad[:, :, 0:32 * TREES].rearrange("p t (r l) -> p t r l", r=TREES)
                            else:
                                dst = path[:, lev % 2]
                            right, left = dst[:, :, :, 1:2 * w:2], dst[:, :, :, 0:2 * w:2]
                            step(dve.tensor_tensor(right, src, dec[:, :, :, w - 1:2 * w - 1], ALU.mult))
                            step(dve.tensor_tensor(left, src, right, ALU.subtract))
                        assert count[0] == LINKS
                        dve.wait_ge(sel_in, blk + 1)
                        dve.tensor_scalar(selm[:, :], selT, -1.0, None, ALU.add).then_inc(selm_in, 1)
                        for u in range(2):
                            for qt in range(2):
                                dve.wait_ge(at.s_full, blk * 4 + (2 * u + qt + 1))
                                dve.tensor_reduce(negmax[:, u, qt, 0:1], ps[:, 2 * u + qt, 0:SEQ], AXX, ALU.max, negate=True).then_inc(at.maxed, 1)
                        for u in range(2):
                            dve.wait_ge(at.e_in, blk * 4 + (2 * u + 2))
                            dve.reciprocal(rinv[:, u, :, 0], rowsum[:, u, :, 0]).then_inc(rg, 1)
                            dve.wait_ge(rg, blk * 4 + (2 * u + 1))
                            dve.tensor_scalar(rinv[:, u, :, 1], rinv[:, u, :, 0], gate(4 + 2), None, ALU.mult).then_inc(rg, 1)
                            dve.wait_ge(rg, blk * 4 + (2 * u + 2))
                            dve.wait_ge(o_full, blk * 2 + (u + 1))
                            xp = x_pair(blk, u)
                            for t in range(2):
                                x = xp(t)[:, 0, :]
                                ins = dve.scalar_tensor_tensor(x, ps[:, 4 + u, t * D:(t + 1) * D], rinv[:, u, t, 1:2], x, ALU.mult, ALU.add)
                            ins.then_inc(o_in, 1)
                            dve.wait_ge(o_in, blk * 2 + (u + 1))
                            nrm.statistics(dve, blk, u, xp)
                            wait(dve, n_full, blk * 2 + u)
                            nrm.result(dve, blk, u, lambda t: xs[:, t, :], xp)

                @block.tensor
                def _(pe):
                    go = E0 - 1 + E1
                    pe.wait_ge(cst, 7)
                    pe.wait_ge(ld_b2, 48)
                    for s, loads in TREE_LOADS:
                        pe.wait_ge(ld_w[s], 32 * loads)
                    with pe.Fori(0, NB) as blk:
                        pe.wait_ge(staged, blk + 1)
                        wait(pe, xT_in, blk * 2)
                        for t in range(4):
                            for k in range(KD):
                                ins = pe.matmul(ps[:, 6, t * TREES * NODES:(t + 1) * TREES * NODES], stage[:, k, t * P:(t + 1) * P],
                                                gatew[:, k, go:go + TREES * NODES], start=(k == 0), stop=(k == KD - 1))
                        ins.then_inc(node_full, 1)
                        pe.wait_ge(link, blk * LINKS + LINKS)
                        for t in range(4):
                            ins = pe.transpose(ps[:, 7, t * P:(t + 1) * P], selpad[:, t, :], ident[:, :])
                        ins.then_inc(sel_full, 1)
                        for t in range(TREES):
                            sl = TREE_LOADS[t][0]
                            for f in range(NF):
                                if f >= 4:
                                    pe.wait_ge(h_in, blk * 24 + (8 * t + f - 3))
                                for k in range(KD):
                                    pe.matmul(ps[:, f % 4, :], w1[sl][:, k, f * P:(f + 1) * P], xnT[:, k, ds(blk * BLK, BLK)],
                                              start=(k == 0), stop=False)
                                if t == 0 and f == 0:
                                    pe.wait_ge(selm_in, blk + 1)
                                pe.matmul(ps[:, f % 4, :], leafw[:, t, f * P:(f + 1) * P], selm[:, :], start=False, stop=True).then_inc(h_full, 1)
                            for i in range(2):
                                if t or i:
                                    j = 2 * t + i
                                    if j >= 2:
                                        pe.wait_ge(y_in, blk * 6 + (j - 1))
                                if t < 2:
                                    for f in range(NF):
                                        if i == 0:
                                            pe.wait_ge(h_in, blk * 24 + (8 * t + f + 1))
                                        pe.matmul(ps[:, 4 + i, :], w2[sl][:, f, i * P:(i + 1) * P], hT[:, f, :], start=(f == 0), stop=False)
                                    ins = pe.matmul(ps[:, 4 + i, :], b2pad[:, t, i * P:(i + 1) * P], selT, start=False, stop=True)
                                else:
                                    for tt in range(2):
                                        q = (2 * i + tt) * P
                                        o = ps[:, 4 + i, tt * D:(tt + 1) * D]
                                        for f in range(NF):
                                            if i == 0 and tt == 0:
                                                pe.wait_ge(h_in, blk * 24 + (8 * t + f + 1))
                                            pe.matmul(o, hT[:, f, q:q + P], w2[sl][:, f, :], start=(f == 0), stop=False)
                                        ins = pe.matmul(o, selT[:, q:q + P], b2pad[:, t, :], start=False, stop=True)
                                ins.then_inc(y_full, 1)
                        pe.wait_ge(y_in, blk * 6 + 4)
                        at.scores(pe, blk)
                        at.turn(pe, blk)
                        pe.wait_ge(y_in, blk * 6 + 6)
                        for u in range(2):
                            pe.wait_ge(at.p_in, blk * 2 + (u + 1))
                            for t in range(2):
                                for kt in range(2):
                                    ins = pe.matmul(ps[:, 4 + u, t * D:(t + 1) * D], probT[:, u, kt, t * P:(t + 1) * P], vtok[:, 2 * u + kt, :],
                                                    start=(kt == 0), stop=(kt == 1))
                            ins.then_inc(o_full, 1)
                        for u in range(2):
                            pe.wait_ge(nrm.link, nrm.done(blk, u))
                            transpose_pair(pe, 6 + u, xs).then_inc(n_full, 1)

        def phase_padded(sync_tail):
            n = "L3a_"
            wq, wk, wv, wo = (attw[:, 1, i] for i in range(4))
            padm, pada = wbuf[:, 2, 0:T], wbuf[:, 2, T:2 * T]
            padi = hbuf[:, 0:T].bitcast(I32)
            staged = psem(n + "staged")
            q_full = psem(n + "q_full")
            q_in = psem(n + "q_in")
            v_full = psem(n + "v_full")
            v_in = psem(n + "v_in")
            mskd = psem(n + "masked")
            c_full = psem(n + "c_full")
            c_in = psem(n + "c_in")
            o_full = psem(n + "o_full")
            o_in = psem(n + "o_in")
            n_full = psem(n + "n_full")
            xT_in = psem(n + "xT_in")
            copied = psem(n + "copied")
            link = psem(n + "link")
            pads = psem(n + "pads")
            post, nrm = Norm(n + "post", 2), Norm(n + "norm", 2)
            at = Single(n)

            with nc.Block() as block:
                @block.sync
                def _(sp):
                    sp.dma_start(padi, a["pad"].unsqueeze(0).broadcast_to([P, T])).then_inc(ld_pad, 16)
                    sync_tail(sp)

                @block.gpsimd
                def _(pool):
                    with pool.Fori(0, NB) as blk:
                        pool.wait_ge(q_full, blk * 4 + 1)
                        pool.tensor_copy(stage[:, :, :], ctxT[:, :, ds(blk * BLK, BLK)]).then_inc(staged, 1)
                        for u in range(2):
                            post.power(pool, blk, u)
                            nrm.power(pool, blk, u)
                            pool.wait_ge(nrm.link, nrm.done(blk, u))
                            pool.tensor_copy(xn_tok[:, ds(blk * 4 + 2 * u, 2), :], xs[:, :, :]).then_inc(copied, 1)

                @block.scalar
                def _(act):
                    with act.Fori(0, NB) as blk:
                        for j in range(4):
                            m = j % 2
                            act.wait_ge(q_full, blk * 4 + (j + 1))
                            if j < 2:
                                act.activation(qT[:, m, :], ps[:, j, :], ACT.Identity, bias=qbias[:, 2 + m:3 + m], scale=D ** -0.5).then_inc(q_in, 1)
                            else:
                                act.activation(kT[:, m, :], ps[:, j, :], ACT.Identity, bias=col("L3_bk", m)).then_inc(q_in, 1)
                        at.exps(act, blk, False)
                        at.turned(act, blk)
                        for u in range(2):
                            act.wait_ge(c_full, blk * 2 + (u + 1))
                            act.activation(probT[:, 2 + u].rearrange("p a b -> p (a b)"), ps[:, 4 + u, :], ACT.Identity).then_inc(c_in, 1)
                        for u in range(2):
                            act.wait_ge(n_full, blk * 2 + (u + 1))
                            store_T(act, xnT, 4 + u, blk, u).then_inc(xT_in, 1)

                @block.vector
                def _(dve):
                    dve.wait_ge(ld_pad, 16)
                    dve.tensor_scalar(pada, padi, 0.0, NEG, ALU.is_equal, ALU.mult)
                    dve.tensor_scalar(padm, padi, 0.0, None, ALU.not_equal).then_inc(pads, 1)
                    dve.wait_ge(pads, 1)
                    dve.wait_ge(ld_rowsA, 64)
                    with dve.Fori(0, NB) as blk:
                        for u in range(2):
                            dve.wait_ge(v_full, blk * 2 + (u + 1))
                            dve.tensor_tensor(vtok[:, 2 * u:2 * u + 2, :], ps[:, 4 + u, :].rearrange("p (t d) -> p t d", t=2),
                                              rowsA[:, 0, :].unsqueeze(1).broadcast_to([P, 2, D]), ALU.add).then_inc(v_in, 1)
                        for u in range(2):
                            for qt in range(2):
                                j = 2 * u + qt
                                sc = prob[:, u, qt, 1, :]
                                dve.wait_ge(at.s_full, blk * 4 + (j + 1))
                                dve.tensor_tensor(sc, ps[:, j, 0:SEQ], padm[:, ds(blk * BLK + u * SEQ, SEQ)], ALU.mult).then_inc(mskd, 1)
                                dve.wait_ge(mskd, blk * 8 + (2 * j + 1))
                                dve.tensor_tensor(sc, sc, pada[:, ds(blk * BLK + u * SEQ, SEQ)], ALU.add).then_inc(mskd, 1)
                                dve.wait_ge(mskd, blk * 8 + (2 * j + 2))
                                dve.tensor_reduce(negmax[:, u, qt, 0:1], sc, AXX, ALU.max, negate=True).then_inc(at.maxed, 1)
                        for u in range(2):
                            dve.wait_ge(at.e_in, blk * 4 + (2 * u + 2))
                            dve.reciprocal(rinv[:, u, :, 0], rowsum[:, u, :, 0]).then_inc(o_in, 1)
                            dve.wait_ge(o_in, blk * 4 + (2 * u + 1))
                            dve.wait_ge(o_full, blk * 2 + (u + 1))
                            for t in range(2):
                                ins = dve.scalar_tensor_tensor(ts[:, t, :], ps[:, 6 + u, t * D:(t + 1) * D], rinv[:, u, t, 0:1], rowsA[:, 1, :],
                                                               ALU.mult, ALU.add)
                            ins.then_inc(o_in, 1)
                            dve.wait_ge(o_in, blk * 4 + (2 * u + 2))
                            tp = lambda t: ts[:, t, :]
                            post.statistics(dve, blk, u, tp)
                            post.result(dve, blk, u, tp, tp)
                            dve.wait_ge(post.link, post.done(blk, u))
                            scale_and_add(dve, link, (blk * 2 + u) * 3, rowsA[:, 2, :], rowsA[:, 3, :], blk, u, lambda t: gate(3))
                            xp = x_pair(blk, u)
                            nrm.statistics(dve, blk, u, xp)
                            wait(dve, n_full, blk * 2 + u)
                            wait(dve, copied, blk * 2 + u)
                            nrm.result(dve, blk, u, lambda t: xs[:, t, :], xp)

                @block.tensor
                def _(pe):
                    pe.wait_ge(ld_att[1], 32)
                    with pe.Fori(0, NB) as blk:
                        for j in range(4):
                            m = j % 2
                            w, src = (wq, xnT) if j < 2 else (wk, ctxT)
                            for k in range(KD):
                                ins = pe.matmul(ps[:, j, :], w[:, k, m * P:(m + 1) * P], src[:, k, ds(blk * BLK, BLK)],
                                                start=(k == 0), stop=(k == KD - 1))
                            ins.then_inc(q_full, 1)
                        pe.wait_ge(staged, blk + 1)
                        wait(pe, xT_in, blk * 2)
                        for u in range(2):
                            for t in range(2):
                                for k in range(KD):
                                    ins = pe.matmul(ps[:, 4 + u, t * D:(t + 1) * D], stage[:, k, (2 * u + t) * P:(2 * u + t + 1) * P], wv[:, k, :],
                                                    start=(k == 0), stop=(k == KD - 1))
                            ins.then_inc(v_full, 1)
                        pe.wait_ge(q_in, blk * 4 + 4)
                        at.scores(pe, blk)
                        at.turn(pe, blk)
                        pe.wait_ge(v_in, blk * 2 + 2)
                        for u in range(2):
                            pe.wait_ge(at.p_in, blk * 2 + (u + 1))
                            for m in range(KD):
                                for kt in range(2):
                                    ins = pe.matmul(ps[:, 4 + u, m * SEQ:(m + 1) * SEQ], vtok[:, 2 * u + kt, m * P:(m + 1) * P],
                                                    probT[:, u, kt, :], start=(kt == 0), stop=(kt == 1))
                            ins.then_inc(c_full, 1)
                        for u in range(2):
                            pe.wait_ge(c_in, blk * 2 + (u + 1))
                            for t in range(2):
                                for m in range(KD):
                                    ins = pe.matmul(ps[:, 6 + u, t * D:(t + 1) * D], probT[:, 2 + u, m, t * P:(t + 1) * P], wo[:, m, :],
                                                    start=(m == 0), stop=(m == 1))
                            ins.then_inc(o_full, 1)
                        for u in range(2):
                            pe.wait_ge(nrm.link, nrm.done(blk, u))
                            transpose_pair(pe, 4 + u, xs).then_inc(n_full, 1)

        def phase_last():
            n = "L3f_"
            sl, loads = LAST_LOAD
            h_full, h_in = psem(n + "h_full"), psem(n + "h_in")
            y_full, y_in = psem(n + "y_full"), psem(n + "y_in")
            sums = psem(n + "sums")
            link = psem(n + "link")
            post = Norm(n + "post", 2)

            with nc.Block() as block:
                @block.sync
                def _(sp):
                    rows_out = out.rearrange("(t p) d -> p t d", p=P)
                    with sp.Fori(0, NB) as blk:
                        for u in range(2):
                            sp.wait_ge(link, (blk * 2 + (u + 1)) * 3)
                            sp.dma_start(rows_out[:, ds(blk * 4 + 2 * u, 2), :], x_tok[:, ds(blk * 4 + 2 * u, 2), :]).then_inc(stored, 16)
                    sp.wait_ge(stored, 2 * NB * 16)

                @block.gpsimd
                def _(pool):
                    with pool.Fori(0, NB) as blk:
                        for u in range(2):
                            post.power(pool, blk, u)

                @block.scalar
                def _(act):
                    with act.Fori(0, NB) as blk:
                        for f in range(NF):
                            act.wait_ge(h_full, blk * NF + (f + 1))
                            act.activation(hT[:, f, :], ps[:, f % 4, :], ACT.Relu, bias=col("L3_b1", f)).then_inc(h_in, 1)

                @block.vector
                def _(dve):
                    dve.wait_ge(ld_rowsF, 48)
                    with dve.Fori(0, NB) as blk:
                        for u in range(2):
                            dve.wait_ge(y_full, blk * 2 + (u + 1))
                            dve.tensor_tensor(ts[:, :, :], ps[:, 4 + u, :].rearrange("p (t d) -> p t d", t=2),
                                              rowsF[:, 0, :].unsqueeze(1).broadcast_to([P, 2, D]), ALU.add).then_inc(y_in, 1)
                            dve.wait_ge(y_in, blk * 2 + (u + 1))
                            dve.tensor_tensor(ts[:, :, :], ts[:, :, :], xn_tok[:, ds(blk * 4 + 2 * u, 2), :], ALU.add).then_inc(sums, 1)
                            dve.wait_ge(sums, blk * 2 + (u + 1))
                            tp = lambda t: ts[:, t, :]
                            post.statistics(dve, blk, u, tp)
                            post.result(dve, blk, u, tp, tp)
                            dve.wait_ge(post.link, post.done(blk, u))
                            scale_and_add(dve, link, (blk * 2 + u) * 3, rowsF[:, 1, :], rowsF[:, 2, :], blk, u, lambda t: gate(4 + 3))

                @block.tensor
                def _(pe):
                    pe.wait_ge(ld_w[sl], 32 * loads)
                    with pe.Fori(0, NB) as blk:
                        for f in range(NF):
                            if f >= 4:
                                pe.wait_ge(h_in, blk * NF + (f - 3))
                            for k in range(KD):
                                ins = pe.matmul(ps[:, f % 4, :], w1[sl][:, k, f * P:(f + 1) * P], xnT[:, k, ds(blk * BLK, BLK)],
                                                start=(k == 0), stop=(k == KD - 1))
                            ins.then_inc(h_full, 1)
                        for u in range(2):
                            wait(pe, y_in, blk * 2)
                            for t in range(2):
                                for f in range(NF):
                                    if u == 0 and t == 0:
                                        pe.wait_ge(h_in, blk * NF + (f + 1))
                                    ins = pe.matmul(ps[:, 4 + u, t * D:(t + 1) * D], hT[:, f, (2 * u + t) * P:(2 * u + t + 1) * P],
                                                    w2[sl][:, f, :], start=(f == 0), stop=(f == NF - 1))
                            ins.then_inc(y_full, 1)

        TREE_LOADS = ((1, 7), (0, 8), (2, 1))
        LAST_LOAD = (1, 8)

        def during_attn0(sp):
            sp.dma_start(attw[:, 1, 3], a["L1_wo"].rearrange("(k p) n -> p k n", p=P)).then_inc(ld_att[1], 16)

        def during_ffn0(sp, y_full, wslot):
            load_rows(sp, rowsA, "attn1", ld_rowsA)
            load_att(sp, 0, 1)
            with sp.Fori(0, (E0 - 3) // 2) as i:
                for v in range(2):
                    sp.wait_ge(y_full, i * 16 + 8 * (v + 1))
                    load_expert(sp, v, a["L0_w1"][ds(i * 2 + (2 + v), 1)].rearrange("e d f -> (e d) f"),
                                a["L0_w2"][ds(i * 2 + (2 + v), 1)].rearrange("e d f -> (e d) f"))
            sp.wait_ge(y_full, 8 * (E0 - 2))
            load_expert(sp, 0, a["L0_w1"][E0 - 1], a["L0_w2"][E0 - 1])
            sp.wait_ge(y_full, 8 * (E0 - 1))
            load_expert(sp, 1, a["L1_w1"][0], a["L1_w2"][0])
            sp.wait_ge(y_full, 8 * E0)
            load_expert(sp, 0, a["L1_w1"][1], a["L1_w2"][1])

        def during_attn1(sp):
            load_rows(sp, rowsF, "ffn1", ld_rowsF)

        def during_ffn1(sp, y_full, wslot):
            load_rows(sp, rowsA, "attn2", ld_rowsA)
            load_att(sp, 1, 2)
            load_expert(sp, 2, a["L2_w1"][2], a["L2_w2"][2])
            for e, (f, s) in enumerate(((a["L1_w1"][2], a["L1_w2"][2]), (a["L1_w1"][3], a["L1_w2"][3]),
                                        (a["L2_w1"][0], a["L2_w2"][0]), (a["L2_w1"][1], a["L2_w2"][1]))):
                sp.wait_ge(y_full, 8 * (e + 1))
                load_expert(sp, wslot(e), f, s)

        def during_ffn2(sp):
            load_rows(sp, rowsA, "attn3", ld_rowsA)
            load_rows(sp, rowsF, "ffn3", ld_rowsF)

        def during_attn3(sp):
            load_expert(sp, LAST_LOAD[0], a["L3_w1"], a["L3_w2"])

        phase_setup()
        end_phase()
        phase_heads(0, during_attn0)
        end_phase()
        phase_experts(0, E0, ACT.Relu, 4, 0, False, during_ffn0)
        end_phase()
        phase_heads(1, during_attn1)
        end_phase()
        phase_experts(1, E1, ACT.Gelu, 5, E0, True, during_ffn1)
        end_phase()
        phase_linear(lambda sp: None)
        end_phase()
        phase_trees(during_ffn2)
        end_phase()
        phase_padded(during_attn3)
        end_phase()
        phase_last()


def kernel(**inputs):
    import numpy as np
    import concourse.bacc as bacc
    from concourse.bass_utils import run_bass_kernel_spmd

    v = {k: np.asarray(x) for k, x in inputs.items()}

    def colsof(x, n):
        return x.reshape(n, P).T

    arrays = {
        "x": v["x"].reshape(T, D), "ctx": v["ctx_1024"].reshape(T, D),
        "mask": v["mask_Bx1xSxS2_bf0"].reshape(T, SEQ), "pad": v["mask_Bx1xS2_ik1"].reshape(T),
        "g": np.concatenate([v["g_xattn"], v["g_ffn"]]),
        "attw": np.stack([np.stack([v[f"L0_xattn_{w}"] for w in ("Wq", "Wk", "Wv", "Wo")]),
                          np.stack([v[f"L2_xattn_{w}"].T for w in ("wq_w", "wk_w", "wv_w", "wo_w")]),
                          np.stack([v[f"L3_xattn_{w}"] for w in ("Wq", "Wk", "Wv", "Wo")])]),
        "L1_wo": v["L1_xattn_Wo"].T,
        "rep": np.stack([np.tile(v[f"L1_xattn_{w}"].T, (GH, 1)) for w in ("Wq", "Wk", "Wv")], axis=1),
        "L0_w1": np.concatenate([v["L0_ffn_W1"], v["L0_ffn_Ws1"][None]]),
        "L0_w2": np.concatenate([v["L0_ffn_W2"], v["L0_ffn_Ws2"][None]]),
        "L1_w1": v["L1_ffn_W1"], "L1_w2": v["L1_ffn_W2"],
        "L2_w1": np.stack([v[f"L2_ffn_{t}_w1"].transpose(1, 0, 2).reshape(D, F) for t in "qkv"]),
        "L2_w2": np.stack([v[f"L2_ffn_{t}_w2"].reshape(F, D) for t in "qkv"]),
        "L2_b2": np.stack([v[f"L2_ffn_{t}_b2"] for t in "qkv"]),
        "L3_w1": v["L3_ffn_w1"][0], "L3_w2": v["L3_ffn_w2"][0],
    }
    columns = {
        "L0_bq": v["L0_xattn_bq"], "L0_bk": v["L0_xattn_bk"],
        "L0_b1": np.concatenate([v["L0_ffn_b1"].reshape(-1), v["L0_ffn_bs1"]]), "L1_b1": v["L1_ffn_b1"].reshape(-1),
        "L2_bq": v["L2_xattn_wq_b"], "L2_b1": np.concatenate([v[f"L2_ffn_{t}_b1"].reshape(-1) for t in "qkv"]),
        "L3_bq": v["L3_xattn_bq"], "L3_bk": v["L3_xattn_bk"], "L3_b1": v["L3_ffn_b1"][0],
    }
    arrays["cols"] = np.concatenate([colsof(columns[k], n) for k, (_, n) in COLS.items()], axis=1)
    arrays["rows"] = np.stack([
        v["L0_xattn_bv"], v["L0_xattn_bo"], *v["L0_ffn_b2"], v["L0_ffn_bs2"], v["L1_xattn_bo"], *v["L1_ffn_b2"],
        v["L2_xattn_wk_b"], v["L2_xattn_wv_b"], v["L2_xattn_wo_b"], v["L2_xattn_ln_g"], v["L2_xattn_ln_b"],
        v["L3_xattn_bv"], v["L3_xattn_bo"], v["L3_xattn_g0"], v["L3_xattn_beta0"],
        v["L3_ffn_b2"][0], v["L3_ffn_gamma"], v["L3_ffn_beta"]])
    gatew = np.concatenate([v["L0_ffn_Wg"], v["L1_ffn_Wg"], *[v[f"L2_ffn_{t}_node_w"].T for t in "qkv"]], axis=1)
    arrays["gatew"] = gatew.reshape(KD, P, NGATEW).transpose(1, 0, 2)
    arrays["small"] = np.concatenate([v["L1_ffn_bg"], *[v[f"L2_ffn_{t}_node_b"] for t in "qkv"]])

    nc = bacc.Bacc("TRN2", target_bir_lowering=False, num_devices=1)
    a, feed = {}, {}
    for name, x in arrays.items():
        feed["in_" + name] = np.ascontiguousarray(x)
        a[name] = nc.dram_tensor("in_" + name, x.shape, mybir.dt.from_np(x.dtype), kind="ExternalInput").ap()
    out = nc.dram_tensor("out_x", (T, D), F32, kind="ExternalOutput").ap()
    decoder_kernel(nc, a, out)
    r = run_bass_kernel_spmd(nc, [feed], core_ids=[0])
    return r.results[0]["out_x"].reshape(NBATCH, SEQ, D)
```

```python
from contextlib import ExitStack

import concourse.bass as bass
from concourse import mybir

P = 128
NBATCH, SEQ, D = 8, 256, 256
T = NBATCH * SEQ
NT = T // P
BLK = 512
NB = T // BLK
KD = D // P
H, HD = 16, 16
GH = P // HD
F = 1024
NF = F // P
E0, E1 = 9, 4
NLEAF, LEAFW, DEPTH, TREES = 16, 64, 4, 3
NODES = NLEAF - 1
EPS = 1e-5
NEG = -1.0e9
BIG = 1.0e30

ALU = mybir.AluOpType
ACT = mybir.ActivationFunctionType
AXX = mybir.AxisListType.X
F32 = mybir.dt.float32
BF16 = mybir.dt.bfloat16
I32 = mybir.dt.int32
U8 = mybir.dt.uint8
ds = bass.ds

COLS, ROWS = {}, {}
for _name, _n in (("L0_bq", 2), ("L0_bk", 2), ("L0_bs1", NF), ("L2_bq", 2),
                  ("L2_b1", TREES * NF), ("L3_bq", 2), ("L3_bk", 2), ("L3_b1", NF)):
    COLS[_name] = (sum(n for _, n in COLS.values()), _n)
for _name, _n in (("attn0", 2), ("ffn0", 1), ("attn1", 1), ("attn2", 5), ("attn3", 4), ("ffn3", 3)):
    ROWS[_name] = (sum(n for _, n in ROWS.values()), _n)
NCOLS = sum(n for _, n in COLS.values())
NROWS = sum(n for _, n in ROWS.values())
NSMALL = E1 + TREES * NODES
NGATEW = (E0 - 1) + E1 + TREES * NODES

SUB = 256
STEPS_OF = tuple((n - e) // SUB + e for e, n in ((E0 - 1, 2 * T), (E1, T)))
XROWS = max(STEPS_OF) * SUB
LOADED = ((0, 0), (STEPS_OF[0] // 2 + 1, STEPS_OF[0] // 2))
EXP_LINK = 13
CHOSEN_LINK = (14, 7)
EXPERT_LINK = (30, 22)
PLACED_LINK = (39, 28)


def wait(eng, sem, value):
    if not isinstance(value, int) or value > 0:
        eng.wait_ge(sem, value)


def decoder_kernel(nc, a, out):
    ctx = ExitStack()
    with ctx:
        def sb(name, shape, dt=F32):
            return ctx.enter_context(nc.sbuf_tensor(name, shape, dt))

        def sem(name):
            return ctx.enter_context(nc.semaphore(name))

        phase_sems = []

        def psem(name):
            phase_sems.append(nc.alloc_semaphore(name=name))
            return phase_sems[-1]

        def end_phase():
            nc.clear_and_free_semaphores(phase_sems)
            nc.all_engine_barrier()
            phase_sems.clear()

        x_tok = sb("x_tok", [P, NT, D])
        xnT = sb("xnT", [P, KD, T])
        ctxT = sb("ctxT", [P, KD, T])
        wbuf = sb("wbuf", [P, 3, 4096])
        hbuf = sb("hbuf", [P, 4096])
        vbuf = sb("vbuf", [P, 4096])
        attw = sb("attw", [P, 2, 4, KD, D])
        rowsA = sb("rowsA", [P, 5, D])
        rowsF = sb("rowsF", [P, 8, D])
        stage = sb("stage", [P, KD, BLK])
        qT = sb("qT", [P, KD, BLK])
        kT = sb("kT", [P, KD, BLK])
        prob = sb("prob", [P, 2, 2, 2, SEQ])
        probT = sb("probT", [P, 4, 2, SEQ])
        oT = sb("oT", [P, KD, SEQ])
        xs = sb("xs", [P, 2, D])
        ts = sb("ts", [P, 2, D])
        stats = sb("stats", [P, 2, 6])
        sm = sb("sm", [P, 8, 2])
        negmax = sb("negmax", [P, 2, 2, 2])
        rowsum = sb("rowsum", [P, 2, 2, 2])
        rinv = sb("rinv", [P, 2, 2, 2])
        cols = sb("cols", [P, NCOLS])
        qbias = sb("qbias", [P, 4])
        gates = sb("gates", [P, 8])
        small = sb("small", [P, NSMALL])
        gatew = sb("gatew", [P, KD, NGATEW])
        ident = sb("ident", [P, P])
        identb = sb("identb", [P, P], BF16)
        causal = sb("causal", [P, P], BF16)
        hmask = sb("hmask", [P, GH])
        bmask = sb("bmask", [P, P])
        mhalf = sb("mhalf", [P, 2])
        rank = sb("rank", [P, E0 - 1])
        logit = sb("logit", [P, NT, E0 - 1])
        rt = sb("rt", [P, 3, NT, E0 - 1])
        r1 = sb("r1", [P, 8, NT])
        rsum = sb("rsum", [P, 4, NT * (E0 - 1)])
        ew = sb("ew", [P, 4, E0 - 1])
        step_exp = sb("step_exp", [P, max(STEPS_OF)], I32)
        rowno = sb("rowno", [P, 2, NT], I32)
        dest = sb("dest", [P, 2, 2, 4], I32)
        b1_sb = sb("b1_sb", [P, 2, NF])
        dec = sb("dec", [P, 4, TREES, NLEAF])
        path = sb("path", [P, 2, 4, TREES, NLEAF])
        spare = sb("spare", [P, 2])
        anym = sb("anym", [P, 2, NT])
        rep = sb("rep", [P, 3, HD])
        ps = ctx.enter_context(nc.psum_tensor("ps", [P, 8, 512], F32))

        km = hbuf[:, :].rearrange("p (g j s) -> p g j s", g=2, j=GH)
        hT = hbuf[:, :].rearrange("p (f t) -> p f t", f=NF)
        vm = [wbuf[:, 2, :].rearrange("p (t h c) -> p t h c", t=2, h=H),
              vbuf[:, :].rearrange("p (t h c) -> p t h c", t=2, h=H)]
        xn_tok = vbuf[:, :].rearrange("p (t d) -> p t d", t=NT)
        selpad = vbuf[:, 0:512].rearrange("p (t c) -> p t c", t=4)
        selT = vbuf[:, 512:1024]
        leafw = vbuf[:, 1024:2560].bitcast(BF16).rearrange("p (t f) -> p t f", t=TREES)
        b2pad = vbuf[:, 2560:3328].rearrange("p (t d) -> p t d", t=TREES)
        selm = vbuf[:, 3328:3584].bitcast(BF16)
        w1 = [wbuf[:, s, 0:2048].rearrange("p (k f) -> p k f", k=KD) for s in range(3)]
        w2 = [wbuf[:, s, 2048:4096].rearrange("p (f d) -> p f d", f=NF) for s in range(3)]

        def rs(i, n):
            return rsum[:, i, 0:NT * n].rearrange("p (t e) -> p t e", e=n)

        def col(name, j):
            o = COLS[name][0]
            if isinstance(j, int):
                return cols[:, o + j:o + j + 1]
            return cols[:, ds(j + o, 1)]

        ld_const = sem("ld_const")
        ld_x = sem("ld_x")
        ld_att = [sem(f"ld_att{s}") for s in range(2)]
        ld_w = [sem(f"ld_w{s}") for s in range(3)]
        ld_rowsA = sem("ld_rowsA")
        ld_rowsF = sem("ld_rowsF")
        ld_pad = sem("ld_pad")
        stored = sem("stored")
        zeroed = sem("zeroed")

        def load_rows(sp, dst, name, signal):
            o, n = ROWS[name]
            sp.dma_start(dst[:, 0:n, :], a["rows"][o:o + n, :].unsqueeze(0).broadcast_to([P, n, D])).then_inc(signal, 16)

        def load_att(sp, slot, l):
            sp.dma_start(attw[:, slot], a["attw"][l].rearrange("w (k p) n -> p w k n", p=P)).then_inc(ld_att[slot], 16)

        def load_expert(sp, slot, first, second):
            sp.dma_start(w1[slot], first.rearrange("(k p) f -> p k f", p=P)).then_inc(ld_w[slot], 16)
            sp.dma_start(w2[slot], second.rearrange("(f p) d -> p f d", p=P)).then_inc(ld_w[slot], 16)

        def gate(i):
            return gates[:, i:i + 1]

        class Norm:
            LINKS = 7

            def __init__(self, name, per):
                self.per = per
                self.link = psem(name + "_link")
                self.rstd = psem(name + "_rstd")
                self.used = psem(name + "_used")

            def statistics(self, dve, blk, j, tiles):
                base = (blk * self.per + j) * self.LINKS
                dve.memset(spare[:, 0:1], 0.0)
                for t in range(2):
                    ins = dve.bn_stats(stats[:, t, :], tiles(t))
                ins.then_inc(self.link, 1)
                me, mo = stats[:, :, 1], stats[:, :, 4]
                dve.wait_ge(self.link, base + 1)
                dve.tensor_tensor(sm[:, 0, :], me, mo, ALU.add)
                dve.tensor_tensor(sm[:, 1, :], me, mo, ALU.subtract)
                dve.tensor_tensor(sm[:, 2, :], stats[:, :, 2], stats[:, :, 5], ALU.add).then_inc(self.link, 1)
                dve.wait_ge(self.link, base + 2)
                dve.tensor_tensor(sm[:, 3, :], sm[:, 1, :], sm[:, 1, :], ALU.mult).then_inc(self.link, 1)
                dve.tensor_scalar(sm[:, 4, :], sm[:, 0, :], 0.5, None, ALU.mult).then_inc(self.link, 1)
                dve.wait_ge(self.link, base + 4)
                dve.scalar_tensor_tensor(sm[:, 5, :], sm[:, 3, :], D / 4.0, sm[:, 2, :], ALU.mult, ALU.add).then_inc(self.link, 1)
                dve.wait_ge(self.link, base + 5)
                dve.tensor_scalar(sm[:, 6, :], sm[:, 5, :], 1.0 / D, EPS, ALU.mult, ALU.add).then_inc(self.link, 1)

            def power(self, pool, blk, j):
                pool.wait_ge(self.link, (blk * self.per + j) * self.LINKS + 6)
                pool.tensor_tensor(sm[:, 7, :], sm[:, 6, :], mhalf[:, :], ALU.pow).then_inc(self.rstd, 1)

            def result(self, dve, blk, j, outs, tiles):
                dve.wait_ge(self.rstd, blk * self.per + j + 1)
                for t in range(2):
                    ins = dve.tensor_scalar(outs(t), tiles(t), sm[:, 4, t:t + 1], sm[:, 7, t:t + 1], ALU.subtract, ALU.mult)
                ins.then_inc(self.link, 1)

            def done(self, blk, j):
                return (blk * self.per + j + 1) * self.LINKS

        def x_pair(blk, u):
            return lambda t: x_tok[:, ds(blk * 4 + (2 * u + t), 1), :]

        def transpose_pair(pe, bank, src):
            for k in range(KD):
                for t in range(2):
                    ins = pe.transpose(ps[:, bank, k * SEQ + t * P:k * SEQ + (t + 1) * P], src[:, t, k * P:(k + 1) * P], ident[:, :])
            return ins

        def store_T(act, dst, bank, blk, u):
            return act.activation(dst[:, :, ds(blk * BLK + u * SEQ, SEQ)],
                                  ps[:, bank, :].rearrange("p (k t) -> p k t", k=KD), ACT.Identity)

        def phase_setup():
            cst = psem("cst")
            dcst = psem("dcst")
            got_gates = psem("got_gates")
            ctx_in = [psem(f"ctx_in{s}") for s in range(2)]
            turned = psem("setup_turned")
            kept = [psem(f"setup_kept{j}") for j in range(4)]
            nrm = Norm("setup_norm", 2)
            ctx_rows = a["ctx"].rearrange("(t p) d -> p t d", p=P)
            cst_n = 24

            with nc.Block() as block:
                @block.sync
                def _(sp):
                    sp.dma_start(x_tok[:, :, :], a["x"].rearrange("(t p) d -> p t d", p=P)).then_inc(ld_x, 16)
                    for dst, src in ((cols, "cols"), (gatew, "gatew"), (rep, "rep")):
                        sp.dma_start(dst[:], a[src]).then_inc(ld_const, 16)
                    sp.dma_start(gates[:, :], a["g"].unsqueeze(0).broadcast_to([P, 8])).then_inc(ld_const, 16)
                    sp.dma_start(small[:, :], a["small"].unsqueeze(0).broadcast_to([P, NSMALL])).then_inc(ld_const, 16)
                    with sp.Fori(0, NB) as blk:
                        for u in range(2):
                            wait(sp, turned, blk * 4)
                            dst = prob[:, u].rearrange("p a b s -> p (a b) s")[:, 0:2, :]
                            sp.dma_start(dst, ctx_rows[:, ds(blk * 4 + 2 * u, 2), :]).then_inc(ctx_in[u], 16)
                    load_att(sp, 0, 0)
                    load_rows(sp, rowsA, "attn0", ld_rowsA)
                    load_rows(sp, rowsF, "ffn0", ld_rowsF)
                    load_expert(sp, 0, a["L0_w1"][E0 - 1], a["L0_w2"][E0 - 1])
                    sp.wait_ge(cst, 5)
                    zero = rt[:, :, :, :].rearrange("p a b c -> p (a b c)")[:, 0:D]
                    sp.dma_start(a["xg"].rearrange("(n p) d -> p n d", p=P), zero.unsqueeze(1).broadcast_to([P, XROWS // P, D])).then_inc(zeroed, 16)

                @block.gpsimd
                def _(pool):
                    ones = probT[:, 0, 0, 0:P]
                    pool.memset(ones, 1.0).then_inc(cst, 1)
                    pool.memset(mhalf[:, :], -0.5).then_inc(cst, 1)
                    pool.wait_ge(cst, 2)
                    pool.affine_select(out=ident[:, :], in_=ones, pattern=[[-1, P]], compare_op=ALU.is_equal, fill=0.0,
                                       base=0, channel_multiplier=1).then_inc(cst, 1)
                    pool.affine_select(out=identb[:, :], in_=ones, pattern=[[-1, P]], compare_op=ALU.is_equal, fill=0.0,
                                       base=0, channel_multiplier=1).then_inc(cst, 1)
                    with pool.Fori(0, NB) as blk:
                        for u in range(2):
                            nrm.power(pool, blk, u)
                    pool.memset(rt[:, :, :, :].rearrange("p a b c -> p (a b c)"), 0.0).then_inc(cst, 1)
                    pool.wait_ge(cst, 5)
                    zeros = rt[:, 0, :, :].rearrange("p a b -> p (a b)")
                    pool.affine_select(out=causal[:, :], in_=zeros, pattern=[[-1, P]], compare_op=ALU.is_ge, fill=NEG,
                                       base=0, channel_multiplier=1).then_inc(cst, 1)
                    pool.affine_select(out=hmask[:, :], in_=ones[:, 0:GH], pattern=[[-HD, GH]], compare_op=ALU.is_ge, fill=0.0,
                                       base=0, channel_multiplier=1).then_inc(cst, 1)
                    pool.wait_ge(cst, 7)
                    pool.affine_select(out=hmask[:, :], in_=hmask[:, :], pattern=[[HD, GH]], compare_op=ALU.is_ge, fill=0.0,
                                       base=HD - 1, channel_multiplier=-1).then_inc(cst, 1)
                    pool.wait_ge(cst, 8)
                    pool.tensor_scalar(bmask[:, :].rearrange("p (j c) -> p j c", c=HD),
                                       hmask[:, :].unsqueeze(2).broadcast_to([P, GH, HD]), 0.25, None, ALU.mult).then_inc(cst, 1)
                    for e in range(E0 - 1):
                        pool.memset(rank[:, e:e + 1], float(E0 - 1 - e))
                    pool.memset(wbuf[:, 2, :], 0.0)
                    pool.memset(vbuf[:, :], 0.0)

                @block.vector
                def _(dve):
                    dve.wait_ge(ld_x, 16)
                    with dve.Fori(0, NB) as blk:
                        for u in range(2):
                            xp = x_pair(blk, u)
                            nrm.statistics(dve, blk, u, xp)
                            wait(dve, turned, blk * 4 + 2 * u)
                            nrm.result(dve, blk, u, lambda t: xs[:, t, :], xp)

                @block.scalar
                def _(act):
                    act.wait_ge(ld_const, 80)
                    act.activation(gates[:, :], gates[:, :], ACT.Tanh).then_inc(got_gates, 1)
                    act.mul(qbias[:, 0:2], cols[:, COLS["L0_bq"][0]:COLS["L0_bq"][0] + 2], HD ** -0.5)
                    act.mul(qbias[:, 2:4], cols[:, COLS["L3_bq"][0]:COLS["L3_bq"][0] + 2], D ** -0.5)
                    with act.Fori(0, NB) as blk:
                        for u in range(2):
                            for j, dst in ((2 * u, xnT), (2 * u + 1, ctxT)):
                                act.wait_ge(turned, blk * 4 + (j + 1))
                                store_T(act, dst, j, blk, u).then_inc(kept[j], 1)

                @block.tensor
                def _(pe):
                    pe.wait_ge(cst, 4)
                    with pe.Fori(0, NB) as blk:
                        for u in range(2):
                            pe.wait_ge(nrm.link, nrm.done(blk, u))
                            wait(pe, kept[2 * u], blk)
                            transpose_pair(pe, 2 * u, xs).then_inc(turned, 1)
                            pe.wait_ge(ctx_in[u], blk * 16 + 16)
                            wait(pe, kept[2 * u + 1], blk)
                            transpose_pair(pe, 2 * u + 1, prob[:, u].rearrange("p a b s -> p (a b) s")).then_inc(turned, 1)

        def phase_heads(l, sync_tail):
            causal_l = l == 0
            slot = l % 2
            scale = HD ** -0.5 if l == 0 else D ** -0.5
            wq, wk, wv, wo = (attw[:, slot, i] for i in range(4))
            parts = (lambda m: list(range(KD))) if l == 0 else (lambda m: [m])
            n = f"L{l}a_"
            s_full = psem(n + "s_full")
            s_read = psem(n + "s_read")
            turned_s = psem(n + "turned")
            pt_in = [psem(n + f"pt_in{hh}") for hh in range(2)]
            av = psem(n + "av")
            o_in = psem(n + "o_in")
            a_full = psem(n + "a_full")
            v_in = psem(n + "v_in")
            wo_in = psem(n + "wo_in")
            xT_in = psem(n + "xT_in")
            staged = psem(n + "staged")
            km_in = psem(n + "km_in")
            maxed = psem(n + "maxed")
            inv = psem(n + "inv")
            normed = psem(n + "normed")
            xup = psem(n + "xup")
            nrm = Norm(n + "norm", 2)
            wbd = psem(n + "wbd")
            STEPS = 16
            SF, SR = 36, 68

            def tile_full(blk, i):
                return blk * SF + (4 + i + 1)

            def tile_read(blk, i):
                return blk * SR + (4 + 2 * (i + 1))

            bo = rowsA[:, 1 if l == 0 else 0, :]

            def where(st):
                return st // 8, st // 4 % 2, st % 4

            def keys(qt):
                return P if causal_l and qt == 0 else SEQ

            with nc.Block() as block:
                @block.sync
                def _(sp):
                    sync_tail(sp)

                @block.gpsimd
                def _(pool):
                    if l == 1:
                        for i in range(3):
                            for m in range(KD):
                                ins = pool.tensor_tensor(attw[:, slot, i, m, m * P:(m + 1) * P].rearrange("p (j c) -> p j c", c=HD),
                                                         rep[:, i, :].unsqueeze(1).broadcast_to([P, GH, HD]),
                                                         hmask[:, :].unsqueeze(2).broadcast_to([P, GH, HD]), ALU.mult)
                        ins.then_inc(wbd, 1)
                    with pool.Fori(0, NB) as blk:
                        pool.wait_ge(s_read, blk * SR + 1)
                        pool.tensor_copy(stage[:, :, :], ctxT[:, :, ds(blk * BLK, BLK)]).then_inc(staged, 1)
                        for u in range(2):
                            for g in range(2):
                                pool.wait_ge(s_read, blk * SR + (3 + g))
                                if u:
                                    pool.wait_ge(s_full, tile_full(blk, 8 * g + 7))
                                pool.tensor_tensor(km[:, g], kT[:, g, u * SEQ:(u + 1) * SEQ].unsqueeze(1).broadcast_to([P, GH, SEQ]),
                                                   hmask[:, :].unsqueeze(2).broadcast_to([P, GH, SEQ]), ALU.mult).then_inc(km_in, 1)
                            if u == 1:
                                nrm.power(pool, blk, 0)
                        nrm.power(pool, blk, 1)

                @block.scalar
                def _(act):
                    def exps(blk, st):
                        for qt in range(2):
                            i = 2 * st + qt
                            kk = keys(qt)
                            act.wait_ge(maxed, blk * 32 + (2 * st + qt + 1))
                            if qt == 0:
                                wait(act, turned_s, blk * 32 + max(0, 2 * st - 2))
                            for hh in range(2):
                                ins = act.activation(prob[:, st % 2, qt, hh, 0:kk], ps[:, i % 4, hh * SEQ:hh * SEQ + kk], ACT.Exp,
                                                     bias=negmax[:, st % 2, qt, hh:hh + 1], accum_out=rowsum[:, st % 2, qt, hh:hh + 1])
                                ins.then_inc(s_read, 1)

                    def turned(blk, st):
                        act.wait_ge(turned_s, blk * 32 + (2 * st + 1))
                        wait(act, av, blk * STEPS + max(0, st - 1))
                        s = (2 * st) % 4
                        if causal_l:
                            act.activation(probT[:, s, 0, :], ps[:, 4, 0:SEQ], ACT.Identity)
                            act.activation(probT[:, s, 1, P:], ps[:, 4, SEQ + P:], ACT.Identity).then_inc(pt_in[0], 1)
                        else:
                            act.activation(probT[:, s].rearrange("p a b -> p (a b)"), ps[:, 4, :], ACT.Identity).then_inc(pt_in[0], 1)

                    def context(blk, i):
                        act.wait_ge(av, blk * STEPS + 4 * (i + 1))
                        wait(act, a_full, blk * 6 + (0 if i < 2 else 3))
                        act.activation(oT[:, i % 2, :], ps[:, 6, 0:SEQ], ACT.Identity).then_inc(o_in, 1)

                    def norm_T(blk, u):
                        act.wait_ge(a_full, blk * 6 + (4 + 2 * u))
                        store_T(act, xnT, 7, blk, u).then_inc(xT_in, 1)

                    with act.Fori(0, NB) as blk:
                        for j in range(4):
                            m = j % 2
                            act.wait_ge(s_full, blk * SF + (j + 1))
                            if j < 2:
                                bias = qbias[:, m:m + 1] if l == 0 else 0.0
                                act.activation(qT[:, m, :], ps[:, j, :], ACT.Identity, bias=bias, scale=scale).then_inc(s_read, 1)
                            else:
                                wait(act, km_in, blk * 4)
                                bias = col("L0_bk", m) if l == 0 else 0.0
                                act.activation(kT[:, m, :], ps[:, j, :], ACT.Identity, bias=bias).then_inc(s_read, 1)
                        exps(blk, 0)
                        for st in range(STEPS):
                            if st + 1 < STEPS:
                                exps(blk, st + 1)
                            if st and st % 4 == 0:
                                context(blk, st // 4 - 1)
                            turned(blk, st)
                            if st == 14:
                                norm_T(blk, 0)
                        context(blk, 3)
                        norm_T(blk, 1)

                @block.vector
                def _(dve):
                    def maxima(blk, st):
                        for qt in range(2):
                            i = 2 * st + qt
                            kk = keys(qt)
                            dve.wait_ge(s_full, tile_full(blk, i))
                            dve.tensor_reduce(negmax[:, st % 2, qt, :], ps[:, i % 4, :].rearrange("p (h s) -> p h s", h=2)[:, :, 0:kk],
                                              AXX, ALU.max, negate=True).then_inc(maxed, 1)

                    def normalise(blk, st):
                        for qt in range(2):
                            kk = keys(qt)
                            dve.wait_ge(s_read, tile_read(blk, 2 * st + qt))
                            dve.reciprocal(rinv[:, st % 2, qt, :], rowsum[:, st % 2, qt, :]).then_inc(inv, 1)
                            dve.wait_ge(inv, blk * 32 + 2 * st + qt + 1)
                            for hh in range(2):
                                p = prob[:, st % 2, qt, hh, 0:kk]
                                ins = dve.tensor_scalar(p, p, rinv[:, st % 2, qt, hh:hh + 1], None, ALU.mult)
                            ins.then_inc(normed, 1)

                    def turned(blk, st):
                        dve.wait_ge(turned_s, blk * 32 + (2 * st + 2))
                        wait(dve, av, blk * STEPS + max(0, st - 1))
                        s = (2 * st + 1) % 4
                        if causal_l:
                            dve.tensor_copy(probT[:, s, 0, :], ps[:, 5, 0:SEQ])
                            dve.tensor_copy(probT[:, s, 1, P:], ps[:, 5, SEQ + P:]).then_inc(pt_in[1], 1)
                        else:
                            dve.tensor_copy(probT[:, s].rearrange("p a b -> p (a b)"), ps[:, 5, :]).then_inc(pt_in[1], 1)

                    def values(blk, u):
                        dve.wait_ge(a_full, blk * 6 + (u + 1))
                        for t in range(2):
                            whole = vm[u][:, t].rearrange("p h c -> p (h c)")
                            for g in range(2):
                                o = g * GH * P
                                dst = whole[:, o:o + GH * P].rearrange("p (j c) -> p j c", c=P)
                                dst = bass.AP(dst.tensor, dst.offset, [dst.ap[0], [P + HD, GH], [1, HD]])
                                src = ps[:, 7, t * SEQ + g * P:t * SEQ + (g + 1) * P].rearrange("p (j c) -> p j c", c=HD)
                                if l == 0:
                                    row = rowsA[:, 0, g * P:(g + 1) * P].rearrange("p (j c) -> p j c", c=HD)
                                    ins = dve.tensor_tensor(dst, src, row, ALU.add)
                                else:
                                    ins = dve.tensor_copy(dst, src)
                        ins.then_inc(v_in, 1)

                    def update(blk, u):
                        dve.wait_ge(a_full, blk * 6 + (3 + 2 * u))
                        xp = x_pair(blk, u)
                        for t in range(2):
                            ins = dve.scalar_tensor_tensor(xp(t)[:, 0, :], ps[:, 7, t * D:(t + 1) * D], gate(l), xp(t)[:, 0, :],
                                                           ALU.mult, ALU.add)
                        ins.then_inc(wo_in, 1)
                        dve.wait_ge(wo_in, blk * 2 + (u + 1))
                        for t in range(2):
                            ins = dve.scalar_tensor_tensor(xp(t)[:, 0, :], bo, gate(l), xp(t)[:, 0, :], ALU.mult, ALU.add)
                        ins.then_inc(xup, 1)
                        dve.wait_ge(xup, blk * 2 + (u + 1))
                        nrm.statistics(dve, blk, u, xp)
                        wait(dve, a_full, blk * 6 + (0 if u == 0 else 4))
                        nrm.result(dve, blk, u, lambda t: xs[:, t, :], xp)

                    dve.wait_ge(ld_rowsA, 16 * (l + 1))
                    with dve.Fori(0, NB) as blk:
                        values(blk, 0)
                        maxima(blk, 0)
                        for st in range(STEPS):
                            if st == 0:
                                values(blk, 1)
                            normalise(blk, st)
                            if st + 1 < STEPS:
                                maxima(blk, st + 1)
                            turned(blk, st)
                            if st == 10:
                                update(blk, 0)
                        update(blk, 1)

                @block.tensor
                def _(pe):
                    def scores(blk, st):
                        u, g, p = where(st)
                        for qt in range(2):
                            i = 2 * st + qt
                            kk = keys(qt)
                            if p == 0 and qt == 0:
                                pe.wait_ge(km_in, blk * 4 + (2 * u + g + 1))
                            pe.wait_ge(s_read, blk * SR + 4 if i < 4 else tile_read(blk, i - 4))
                            bank = ps[:, i % 4, :].rearrange("p (h s) -> p h s", h=2)
                            ins = pe.matmul(bank[:, :, 0:kk], qT[:, g, u * SEQ + qt * P:u * SEQ + (qt + 1) * P],
                                            km[:, g, 2 * p:2 * p + 2, 0:kk], start=True, stop=not causal_l)
                            if causal_l:
                                ins = pe.matmul(bank[:, :, qt * P:(qt + 1) * P], identb[:, :],
                                                causal[:, :].unsqueeze(1).broadcast_to([P, 2, P]), start=False, stop=True)
                            ins.then_inc(s_full, 1)

                    def turn(blk, st):
                        for hh in range(2):
                            wait(pe, pt_in[hh], blk * STEPS + st)
                            if hh == 0:
                                pe.wait_ge(normed, blk * 32 + (2 * st + 2))
                            for kt in range(2):
                                for qt in range(2):
                                    if causal_l and kt > qt:
                                        continue
                                    o = kt * SEQ + qt * P
                                    ins = pe.transpose(ps[:, 4 + hh, o:o + P], prob[:, st % 2, qt, hh, kt * P:(kt + 1) * P], ident[:, :])
                            ins.then_inc(turned_s, 1)

                    def attend(blk, st):
                        u, g, p = where(st)
                        if p == 0:
                            wait(pe, o_in, blk * 4 + (2 * u + g))
                            if g == 0:
                                pe.wait_ge(v_in, blk * 2 + (u + 1))
                        for hh in range(2):
                            pe.wait_ge(pt_in[hh], blk * STEPS + (st + 1))
                            for kt in range(2):
                                q0 = P if causal_l and kt == 1 else 0
                                ins = pe.matmul(ps[:, 6, q0:SEQ], vm[u][:, kt, g * GH + 2 * p + hh, :],
                                                probT[:, (2 * st + hh) % 4, kt, q0:], start=(p == 0 and hh == 0 and kt == 0),
                                                stop=(p == 3 and hh == 1 and kt == 1))
                        ins.then_inc(av, 1)

                    def project_out(blk, u):
                        pe.wait_ge(*((v_in, blk * 2 + 2) if u == 0 else (xT_in, blk * 2 + 1)))
                        pe.wait_ge(o_in, blk * 4 + (2 * u + 2))
                        for t in range(2):
                            for g in range(2):
                                ins = pe.matmul(ps[:, 7, t * D:(t + 1) * D], oT[:, g, t * P:(t + 1) * P], wo[:, g, :],
                                                start=(g == 0), stop=(g == 1))
                        ins.then_inc(a_full, 1)

                    def norm_T(blk, u):
                        pe.wait_ge(nrm.link, nrm.done(blk, u))
                        transpose_pair(pe, 7, xs).then_inc(a_full, 1)

                    pe.wait_ge(ld_att[slot], 16)
                    if l == 1:
                        pe.wait_ge(wbd, 1)
                    with pe.Fori(0, NB) as blk:
                        for j in range(4):
                            m = j % 2
                            w, src = (wq, xnT) if j < 2 else (wk, ctxT)
                            for k in parts(m):
                                ins = pe.matmul(ps[:, j, :], w[:, k, m * P:(m + 1) * P], src[:, k, ds(blk * BLK, BLK)],
                                                start=(k == parts(m)[0]), stop=(k == parts(m)[-1]))
                            ins.then_inc(s_full, 1)
                        pe.wait_ge(staged, blk + 1)
                        for u in range(2):
                            wait(pe, *((xT_in, blk * 2) if u == 0 else (v_in, blk * 2 + 1)))
                            for t in range(2):
                                lhs = [stage[:, k, (2 * u + t) * P:(2 * u + t + 1) * P] for k in range(KD)]
                                if l == 0:
                                    for k in range(KD):
                                        ins = pe.matmul(ps[:, 7, t * D:(t + 1) * D], lhs[k], wv[:, k, :], start=(k == 0), stop=(k == KD - 1))
                                else:
                                    for k in range(KD):
                                        ins = pe.matmul(ps[:, 7, t * D + k * P:t * D + (k + 1) * P], lhs[k], wv[:, k, k * P:(k + 1) * P],
                                                        start=True, stop=True)
                            ins.then_inc(a_full, 1)
                            if u == 0:
                                scores(blk, 0)
                        for st in range(STEPS):
                            if st + 1 < STEPS:
                                scores(blk, st + 1)
                            if st:
                                attend(blk, st - 1)
                            turn(blk, st)
                            if st == 10:
                                project_out(blk, 0)
                            if st == 14:
                                norm_T(blk, 0)
                        attend(blk, STEPS - 1)
                        project_out(blk, 1)
                        norm_T(blk, 1)

        def phase_experts(l, func, gi, keep, prefetch):
            n = f"L{l}f_"
            shared = l == 0
            n_exp = E0 - 1 if l == 0 else E1
            n_ch = 2 if l == 0 else 1
            steps = STEPS_OF[l]
            pairs = steps // 2
            go = 0 if l == 0 else E0 - 1
            lead = 2 if shared else 0
            RING = (1, 2)
            base = LOADED[l]
            h_full = psem(n + "h_full")
            h_in = psem(n + "h_in")
            s_full = psem(n + "s_full")
            s_in = psem(n + "s_in")
            y_full = [psem(n + f"y_full{v}") for v in range(2)]
            y_out = [psem(n + f"y_out{v}") for v in range(2)]
            y_st = [psem(n + f"y_st{v}") for v in range(2)]
            g_full = psem(n + "g_full")
            g_in = psem(n + "g_in")
            routed = psem(n + "routed")
            counted = psem(n + "counted")
            n_full = psem(n + "n_full")
            xT_in = psem(n + "xT_in")
            staged = psem(n + "staged")
            r_full = psem(n + "r_full")
            r_in = psem(n + "r_in")
            link = psem(n + "link")
            expw = psem(n + "expw")
            cst = psem(n + "cst")
            copied = psem(n + "copied")
            sent = [psem(n + f"sent{v}") for v in range(2)]
            ld_b = [psem(n + f"ld_b{v}") for v in range(2)]
            ld_g = [psem(n + f"ld_g{v}") for v in range(2)]
            got = [psem(n + f"got{v}") for v in range(2)]
            added = psem(n + "added")
            sadd = psem(n + "sadd")
            kept = psem(n + "kept")
            nrm = Norm(n + "norm", 2)

            upper, ones = oT[:, 0, 0:P], oT[:, 0, P:2 * P]
            stepno = dec[:, :, :, :].rearrange("p a b c -> p (a b c)")[:, 0:steps]
            x_rows = vbuf[:, :].rearrange("p (t d) -> p t d", t=NT)
            row4 = [prob[:, v].rearrange("p a b s -> p (a b) s") for v in range(2)]
            xg_sb = [qT[:, v, :].rearrange("p (t d) -> p t d", t=2) for v in range(2)]
            xgT = kT[:, 0, :].rearrange("p (k t) -> p k t", k=KD)
            hs = hbuf[:, 0:NF * SUB].rearrange("p (f t) -> p f t", f=NF)
            y_sb = [probT[:, v] for v in range(2)]
            b2_sb = ts
            gat = [prob[:, :, :, :, :].rearrange("p a b c s -> p (a b c) s"), probT[:, :, :, :].rearrange("p a b s -> p (a b) s")]
            LINKS = (42 if l == 0 else 30)
            TILES_LINK = [0]

            def ring(eng, step):
                with eng.Fori(0, pairs) as i:
                    for v in range(2):
                        step(i * 2 + v, v, i, False)
                step(steps - 1, 0, pairs, True)

            def unit(j):
                return j if isinstance(j, int) and j < lead else (j + steps if isinstance(j, int) else j)

            with nc.Block() as block:
                @block.vector
                def _(dve):
                    count = [0]

                    def step(ins):
                        count[0] += 1
                        ins.then_inc(link, 1)
                        dve.wait_ge(link, count[0])

                    def wide(i):
                        return rt[:, i, :, 0:n_exp]

                    def over(v):
                        return v.unsqueeze(2).broadcast_to([P, NT, n_exp])

                    def over_t(v):
                        return v.unsqueeze(1).broadcast_to([P, NT, n_exp])

                    lg = logit[:, :, 0:n_exp]
                    order = rank[:, 0:n_exp].unsqueeze(1).broadcast_to([P, NT, n_exp])

                    def one_hot(src, mx, dst):
                        step(dve.tensor_reduce(mx, src, AXX, ALU.max))
                        step(dve.tensor_tensor(dst, src, over(mx), ALU.is_equal))
                        step(dve.tensor_tensor(dst, dst, order, ALU.mult))
                        step(dve.tensor_reduce(r1[:, 7, :], dst, AXX, ALU.max))
                        step(dve.tensor_tensor(dst, dst, over(r1[:, 7, :]), ALU.is_equal))

                    if shared:
                        dve.wait_ge(ld_rowsF, 16)
                        dve.wait_ge(zeroed, 16)
                    dve.wait_ge(routed, NB)
                    raw = ps[:, 7, 0:NT * n_exp].rearrange("p (t e) -> p t e", e=n_exp)
                    if l == 0:
                        step(dve.tensor_copy(lg, raw))
                        one_hot(lg, r1[:, 0, :], wide(0))
                        step(dve.scalar_tensor_tensor(wide(1).rearrange("p t e -> p (t e)"), wide(0).rearrange("p t e -> p (t e)"), -BIG,
                                                      lg.rearrange("p t e -> p (t e)"), ALU.mult, ALU.add))
                        one_hot(wide(1), r1[:, 1, :], wide(2))
                        step(dve.tensor_tensor(r1[:, 4, :], r1[:, 1, :], r1[:, 0, :], ALU.subtract))
                        assert count[0] == EXP_LINK
                        step(dve.tensor_tensor(rs(0, n_exp), wide(0), wide(2), ALU.add))
                    else:
                        bg = small[:, 0:E1].unsqueeze(1).broadcast_to([P, NT, E1])
                        step(dve.tensor_tensor(lg, raw, bg, ALU.add))
                        one_hot(lg, r1[:, 0, :], wide(0))
                        step(dve.tensor_copy(rs(0, n_exp), wide(0)))
                    assert count[0] == CHOSEN_LINK[l]
                    dve.wait_ge(counted, 1)
                    before = ps[:, 7, P:P + NT * n_exp].rearrange("p (t e) -> p t e", e=n_exp)
                    total = ps[:, 7, 2 * P:2 * P + NT * n_exp].rearrange("p (t e) -> p t e", e=n_exp)
                    step(dve.tensor_copy(rs(1, n_exp), total))
                    src, dst, sh = rs(1, n_exp), rs(2, n_exp), 1
                    while sh < NT:
                        dve.tensor_copy(dst[:, 0:sh, :], src[:, 0:sh, :])
                        step(dve.tensor_tensor(dst[:, sh:, :], src[:, sh:, :], src[:, 0:NT - sh, :], ALU.add))
                        src, dst, sh = dst, src, 2 * sh
                    step(dve.tensor_tensor(dst, src, total, ALU.subtract))
                    step(dve.tensor_tensor(dst, dst, before, ALU.add))
                    place = dst
                    q, ne = ew[:, 0, 0:n_exp], ew[:, 1, 0:n_exp]
                    step(dve.tensor_scalar(q, src[:, NT - 1, :], 1.0 / SUB, 1.0, ALU.mult, ALU.add))
                    below = rs(3, 8)[:, 0:n_exp, :]
                    step(dve.tensor_tensor(below, q.unsqueeze(2).broadcast_to([P, n_exp, 8]),
                                           rank[:, :].unsqueeze(1).broadcast_to([P, n_exp, 8]), ALU.is_gt))
                    step(dve.tensor_reduce(ne, below, AXX, ALU.add))
                    src, dst, other, sh = ne, ew[:, 2, 0:n_exp], ew[:, 3, 0:n_exp], 1
                    while sh < n_exp:
                        dve.tensor_copy(dst[:, 0:sh], src[:, 0:sh])
                        step(dve.tensor_tensor(dst[:, sh:], src[:, sh:], src[:, 0:n_exp - sh], ALU.add))
                        src, dst, other, sh = dst, other, dst, 2 * sh
                    dve.wait_ge(cst, 3)
                    full = path[:, :, :, :, :].rearrange("p a b c d -> p (a b c d)")[:, 0:steps * n_exp].rearrange("p (s e) -> p s e", e=n_exp)
                    step(dve.tensor_tensor(full, src.unsqueeze(1).broadcast_to([P, steps, n_exp]),
                                           stepno.unsqueeze(2).broadcast_to([P, steps, n_exp]), ALU.is_le))
                    et = rs(3, 8).rearrange("p t e -> p (t e)")[:, 0:steps]
                    step(dve.tensor_reduce(et, full, AXX, ALU.add))
                    step(dve.tensor_scalar(step_exp[:, 0:steps], et, float(n_exp - 1), None, ALU.min))
                    assert count[0] == EXPERT_LINK[l], count[0]
                    step(dve.tensor_tensor(q, src, ne, ALU.subtract))
                    step(dve.tensor_scalar(q, q, float(SUB), None, ALU.mult))
                    step(dve.tensor_tensor(place, place, over_t(q), ALU.add))
                    for c in range(n_ch):
                        step(dve.tensor_tensor(rs(3, n_exp), wide(2 * c), place, ALU.mult))
                        step(dve.tensor_reduce(r1[:, 0, :], rs(3, n_exp), AXX, ALU.add))
                        step(dve.tensor_copy(rowno[:, c, :], r1[:, 0, :]))
                    assert count[0] == PLACED_LINK[l], count[0]
                    if l == 0:
                        dve.wait_ge(expw, 1)
                        step(dve.tensor_scalar(r1[:, 6, :], r1[:, 5, :], 1.0, None, ALU.add))
                        step(dve.reciprocal(r1[:, 2, :], r1[:, 6, :]))
                        step(dve.tensor_scalar(r1[:, 2, :], r1[:, 2, :], gate(gi), None, ALU.mult))
                        step(dve.tensor_tensor(r1[:, 3, :], r1[:, 5, :], r1[:, 2, :], ALU.mult))

                    def shared_block(blk):
                        for tp in range(2):
                            dve.wait_ge(s_full, blk * 2 + (tp + 1))
                            xp = x_pair(blk, tp)
                            for t in range(2):
                                x = xp(t)[:, 0, :]
                                ins = dve.scalar_tensor_tensor(x, ps[:, 4 + tp, t * D:(t + 1) * D], gate(gi), x, ALU.mult, ALU.add)
                            ins.then_inc(s_in, 1)
                            dve.wait_ge(s_in, blk * 2 + (tp + 1))
                            for t in range(2):
                                x = xp(t)[:, 0, :]
                                ins = dve.scalar_tensor_tensor(x, rowsF[:, 0, :], gate(gi), x, ALU.mult, ALU.add)
                            ins.then_inc(sadd, 1)

                    def ring_step(s, v, k, last):
                        dve.wait_ge(y_full[v], k + 1)
                        dve.wait_ge(y_st[v], k * 16)
                        dve.wait_ge(ld_b[v], k * 32 + 32)
                        dve.tensor_tensor(y_sb[v], ps[:, 4 + v, :].rearrange("p (t d) -> p t d", t=2),
                                          b2_sb[:, v, :].unsqueeze(1).broadcast_to([P, 2, D]), ALU.add).then_inc(y_out[v], 1)

                    def combine(blk):
                        v = blk % 2
                        dve.wait_ge(got[v], 64 * n_ch * (blk // 2 + 1))
                        for c in range(n_ch):
                            for t in range(4):
                                i = blk * 4 + t
                                w = r1[:, 2 + c, i:i + 1] if l == 0 else gate(gi)
                                ins = dve.scalar_tensor_tensor(x_tok[:, i, :], gat[v][:, c * 4 + t, :], w, x_tok[:, i, :], ALU.mult, ALU.add)
                            ins.then_inc(added, 1)
                            dve.wait_ge(added, blk * n_ch + c + 1)

                    def norms(blk):
                        if shared and blk >= lead:
                            dve.wait_ge(sadd, blk * 2 + 2)
                        for u in range(2):
                            xp = x_pair(blk, u)
                            nrm.statistics(dve, blk, u, xp)
                            wait(dve, n_full, blk * 2 + u)
                            if keep:
                                wait(dve, kept, blk * 2 + u)
                            nrm.result(dve, blk, u, lambda t: xs[:, t, :], xp)

                    if shared:
                        with dve.Fori(0, lead) as j:
                            shared_block(j)
                    ring(dve, ring_step)
                    if shared:
                        dve.wait_ge(sadd, 2 * lead)
                    for blk in range(NB):
                        combine(blk)
                        if shared and blk == NB - 1:
                            shared_block(NB - 1)
                        norms(blk)
                        if shared and blk == 1:
                            shared_block(2)
                            dve.wait_ge(sadd, 6)

                @block.sync
                def _(sp):
                    prefetch(sp)
                    w1_all, w2_all, b1_all, b2_all = (a[f"L{l}_{w}"] for w in ("w1", "w2", "b1r", "b2"))

                    def load_weights(s, v):
                        e = sp.value_load(step_exp[0:1, ds(s, 1)], min_val=0, max_val=n_exp - 1)
                        load_expert(sp, RING[v], w1_all[ds(e, 1)].rearrange("e d f -> (e d) f"),
                                    w2_all[ds(e, 1)].rearrange("e d f -> (e d) f"))
                        sp.dma_start(b1_sb[:, v, :], b1_all[ds(e, 1)].rearrange("e p f -> (e p) f")).then_inc(ld_b[v], 16)
                        sp.dma_start(b2_sb[:, v, :], b2_all[ds(e, 1)].broadcast_to([P, D])).then_inc(ld_b[v], 16)

                    def load_rows_of(s, v):
                        sp.dma_start(xg_sb[v], a["xg"][ds(s * SUB, SUB)].rearrange("(t p) d -> p t d", p=P)).then_inc(ld_g[v], 16)

                    def store(s, v, k):
                        sp.wait_ge(y_out[v], k + 1)
                        sp.dma_start(a["yg"][ds(s * SUB, SUB)].rearrange("(t p) d -> p t d", p=P), y_sb[v]).then_inc(y_st[v], 16)

                    sp.wait_ge(link, EXPERT_LINK[l])
                    for v in range(2):
                        load_weights(v, v)
                    for v in range(2):
                        sp.wait_ge(sent[v], 4 * n_ch * 16 * (NB // 2))
                    for v in range(2):
                        load_rows_of(v, v)
                    with sp.Fori(0, pairs - 1) as i:
                        for v in range(2):
                            store(i * 2 + v, v, i)
                            load_weights(i * 2 + (v + 2), v)
                            load_rows_of(i * 2 + (v + 2), v)
                    store(steps - 3, 0, pairs - 1)
                    load_weights(steps - 1, 0)
                    load_rows_of(steps - 1, 0)
                    store(steps - 2, 1, pairs - 1)
                    store(steps - 1, 0, pairs)

                @block.gpsimd
                def _(pool):
                    with pool.Fori(0, NB) as blk:
                        wait(pool, r_full, blk * 2)
                        pool.tensor_copy(stage[:, :, :], xnT[:, :, ds(blk * BLK, BLK)]).then_inc(staged, 1)
                    pool.memset(ones, 1.0).then_inc(cst, 1)
                    pool.wait_ge(cst, 1)
                    pool.affine_select(out=upper, in_=ones, pattern=[[1, P]], compare_op=ALU.is_gt, fill=0.0,
                                       base=0, channel_multiplier=-1).then_inc(cst, 1)
                    pool.iota(stepno, pattern=[[1, steps]], base=0, channel_multiplier=0, allow_small_or_imprecise_dtypes=True).then_inc(cst, 1)
                    pool.wait_ge(zeroed, 16)
                    pool.wait_ge(link, PLACED_LINK[l])
                    pool.wait_ge(r_in, 2 * NB)
                    with pool.Fori(0, NB // 2) as i:
                        for v in range(2):
                            wait(pool, sent[v], i * (4 * n_ch * 16))
                            pool.tensor_copy(row4[v], x_rows[:, ds(i * 8 + 4 * v, 4), :])
                            pool.tensor_copy(dest[:, v], rowno[:, :, ds(i * 8 + 4 * v, 4)]).then_inc(copied, 1)
                            pool.wait_ge(copied, i * 2 + (v + 1))
                            pool.tensor_tensor(spare[:, 1:2], mhalf[:, 0:1], mhalf[:, 1:2], ALU.mult)
                            for c in range(n_ch):
                                for t in range(4):
                                    pool.indirect_dma_start(a["xg"], bass.IndirectOffsetOnAxis(dest[:, v, c, t:t + 1], 0),
                                                            row4[v][:, t, :], None).then_inc(sent[v], 16)
                    if l == 0:
                        for v in range(2):
                            pool.wait_ge(sent[v], 4 * n_ch * 16 * (NB // 2))
                        pool.memset(vbuf[:, :], 0.0)
                    pool.wait_ge(y_st[0], 16 * (pairs + 1))
                    pool.wait_ge(y_st[1], 16 * pairs)

                    def gather(blk):
                        v = blk % 2
                        wait(pool, added, n_ch * max(0, blk - 1))
                        for c in range(n_ch):
                            for t in range(4):
                                pool.indirect_dma_start(gat[v][:, c * 4 + t, :], None, a["yg"],
                                                        bass.IndirectOffsetOnAxis(rowno[:, c, blk * 4 + t:blk * 4 + t + 1], 0)).then_inc(got[v], 16)

                    gather(0)
                    for blk in range(NB):
                        if blk + 1 < NB:
                            gather(blk + 1)
                        if shared and blk == NB - 1:
                            pool.memset(wbuf[:, 2, :], 0.0)
                        for u in range(2):
                            nrm.power(pool, blk, u)
                            if keep:
                                pool.wait_ge(nrm.link, nrm.done(blk, u))
                                pool.tensor_copy(xn_tok[:, blk * 4 + 2 * u:blk * 4 + 2 * u + 2, :], xs[:, :, :]).then_inc(kept, 1)

                @block.scalar
                def _(act):
                    with act.Fori(0, NB) as blk:
                        for u in range(2):
                            act.wait_ge(r_full, blk * 2 + (u + 1))
                            act.activation(x_rows[:, ds(blk * 4 + 2 * u, 2), :], ps[:, u, :].rearrange("p (t d) -> p t d", t=2),
                                           ACT.Identity).then_inc(r_in, 1)
                    if l == 0:
                        act.wait_ge(link, EXP_LINK)
                        act.activation(r1[:, 5, :], r1[:, 4, :], ACT.Exp).then_inc(expw, 1)

                    def shared_block(u):
                        for f in range(NF):
                            act.wait_ge(h_full, u * NF + (f + 1))
                            act.activation(hT[:, f, :], ps[:, f % 4, :], func, bias=col("L0_bs1", f)).then_inc(h_in, 1)

                    def rows_in(s):
                        act.wait_ge(g_full, s + 1)
                        act.activation(xgT, ps[:, 6, :].rearrange("p (k t) -> p k t", k=KD), ACT.Identity).then_inc(g_in, 1)

                    def ring_step(s, v, k, last):
                        act.wait_ge(ld_b[v], k * 32 + 32)
                        for f in range(NF):
                            act.wait_ge(h_full, (s + lead) * NF + (f + 1))
                            act.activation(hs[:, f, :], ps[:, f % 4, 0:SUB], func, bias=b1_sb[:, v, f:f + 1]).then_inc(h_in, 1)
                        if not last:
                            rows_in(s + 1)

                    def norm_T(blk):
                        for u in range(2):
                            act.wait_ge(n_full, blk * 2 + u + 1)
                            store_T(act, xnT, 7, blk, u).then_inc(xT_in, 1)

                    if shared:
                        with act.Fori(0, lead) as j:
                            shared_block(j)
                    rows_in(0)
                    ring(act, ring_step)
                    for blk in range(NB):
                        if shared and blk % 2 == 0:
                            shared_block(lead + steps + blk // 2)
                        norm_T(blk)

                @block.tensor
                def _(pe):
                    with pe.Fori(0, NB) as blk:
                        pe.wait_ge(staged, blk + 1)
                        for t in range(4):
                            for k in range(KD):
                                ins = pe.matmul(ps[:, 7, ds(blk * 4 * n_exp + t * n_exp, n_exp)], stage[:, k, t * P:(t + 1) * P],
                                                gatew[:, k, go:go + n_exp], start=(k == 0), stop=(k == KD - 1))
                        ins.then_inc(routed, 1)
                        for u in range(2):
                            wait(pe, r_in, blk * 2)
                            for t in range(2):
                                for k in range(KD):
                                    o = t * D + k * P
                                    ins = pe.transpose(ps[:, u, o:o + P], stage[:, k, (2 * u + t) * P:(2 * u + t + 1) * P], ident[:, :])
                            ins.then_inc(r_full, 1)
                    pe.wait_ge(r_in, 2 * NB)
                    pe.wait_ge(link, CHOSEN_LINK[l])
                    pe.wait_ge(cst, 2)
                    chosen = rs(0, n_exp)
                    pe.matmul(ps[:, 7, P:P + NT * n_exp].rearrange("p (t e) -> p t e", e=n_exp), upper, chosen, start=True, stop=True)
                    pe.matmul(ps[:, 7, 2 * P:2 * P + NT * n_exp].rearrange("p (t e) -> p t e", e=n_exp), ones, chosen,
                              start=True, stop=True).then_inc(counted, 1)

                    def shared_block(blk, u):
                        for f in range(NF):
                            if f >= 4:
                                pe.wait_ge(h_in, u * NF + (f - 3))
                            for k in range(KD):
                                ins = pe.matmul(ps[:, f % 4, :], w1[0][:, k, f * P:(f + 1) * P], xnT[:, k, ds(blk * BLK, BLK)],
                                                start=(k == 0), stop=(k == KD - 1))
                            ins.then_inc(h_full, 1)
                        for tp in range(2):
                            wait(pe, s_in, blk * 2)
                            for t in range(2):
                                for f in range(NF):
                                    if tp == 0 and t == 0:
                                        pe.wait_ge(h_in, u * NF + (f + 1))
                                    ins = pe.matmul(ps[:, 4 + tp, t * D:(t + 1) * D], hT[:, f, (2 * tp + t) * P:(2 * tp + t + 1) * P],
                                                    w2[0][:, f, :], start=(f == 0), stop=(f == NF - 1))
                            ins.then_inc(s_full, 1)

                    def rows_T(v, k):
                        pe.wait_ge(ld_g[v], k * 16 + 16)
                        transpose_pair(pe, 6, xg_sb[v]).then_inc(g_full, 1)

                    def ring_step(s, v, k, last):
                        w = RING[v]
                        pe.wait_ge(g_in, s + 1)
                        pe.wait_ge(ld_w[w], k * 32 + 32 * (base[v] + 1))
                        for f in range(NF):
                            if f >= 4:
                                pe.wait_ge(h_in, (s + lead) * NF + (f - 3))
                            for kk in range(KD):
                                ins = pe.matmul(ps[:, f % 4, 0:SUB], w1[w][:, kk, f * P:(f + 1) * P], xgT[:, kk, :],
                                                start=(kk == 0), stop=(kk == KD - 1))
                            ins.then_inc(h_full, 1)
                        if not last:
                            rows_T(1 - v, k + v)
                        wait(pe, y_out[v], k)
                        for t in range(2):
                            for f in range(NF):
                                if t == 0:
                                    pe.wait_ge(h_in, (s + lead) * NF + (f + 1))
                                ins = pe.matmul(ps[:, 4 + v, t * D:(t + 1) * D], hs[:, f, t * P:(t + 1) * P], w2[w][:, f, :],
                                                start=(f == 0), stop=(f == NF - 1))
                        ins.then_inc(y_full[v], 1)

                    def norm_T(blk):
                        for u in range(2):
                            wait(pe, xT_in, blk * 2 + u)
                            pe.wait_ge(nrm.link, nrm.done(blk, u))
                            transpose_pair(pe, 7, xs).then_inc(n_full, 1)

                    if shared:
                        pe.wait_ge(ld_w[0], 32)
                        with pe.Fori(0, lead) as j:
                            shared_block(j, j)
                    rows_T(0, 0)
                    if shared:
                        pe.wait_ge(s_in, 2 * lead)
                    ring(pe, ring_step)
                    pe.wait_ge(y_out[1], pairs)
                    pe.wait_ge(y_out[0], pairs + 1)
                    for blk in range(NB):
                        if shared and blk % 2 == 0:
                            shared_block(lead + blk // 2, lead + steps + blk // 2)
                        norm_T(blk)

        def scale_and_add(dve, link, base, g_row, b_row, blk, u, gate_of):
            both = ts[:, :, :]
            dve.tensor_tensor(both, both, g_row.unsqueeze(1).broadcast_to([P, 2, D]), ALU.mult).then_inc(link, 1)
            dve.wait_ge(link, base + 1)
            dve.tensor_tensor(both, both, b_row.unsqueeze(1).broadcast_to([P, 2, D]), ALU.add).then_inc(link, 1)
            dve.wait_ge(link, base + 2)
            xp = x_pair(blk, u)
            for t in range(2):
                x = xp(t)[:, 0, :]
                ins = dve.scalar_tensor_tensor(x, ts[:, t, :], gate_of(t), x, ALU.mult, ALU.add)
            ins.then_inc(link, 1)
            dve.wait_ge(link, base + 3)

        def phase_linear(sync_tail):
            n = "L2a_"
            wq, wk, wv, wo = (attw[:, 0, i] for i in range(4))
            ktok = prob[:, 0].rearrange("p a b s -> p (a b) s")
            vt = prob[:, 1].rearrange("p a b s -> p (a b) s")
            kv = probT[:, 0]
            staged = psem(n + "staged")
            q_full = psem(n + "q_full")
            q_in = psem(n + "q_in")
            t_full = psem(n + "t_full")
            t_in = psem(n + "t_in")
            kv_full = psem(n + "kv_full")
            kv_in = psem(n + "kv_in")
            c_full = psem(n + "c_full")
            c_in = psem(n + "c_in")
            o_full = psem(n + "o_full")
            o_in = psem(n + "o_in")
            sums = psem(n + "sums")
            n_full = psem(n + "n_full")
            xT_in = psem(n + "xT_in")
            ld_mask = psem(n + "ld_mask")
            link = psem(n + "link")
            poison = psem(n + "poison")
            post, nrm = Norm(n + "post", 2), Norm(n + "norm", 2)
            mask8 = rowsF[:, :, :].rearrange("p a b -> p (a b)")[:, 0:1024].bitcast(U8).rearrange("p (t k) -> p t k", t=NT)

            with nc.Block() as block:
                @block.sync
                def _(sp):
                    sp.dma_start(mask8, a["mask"].rearrange("(t p) k -> p t k", p=P)).then_inc(ld_mask, 16)
                    sync_tail(sp)

                @block.gpsimd
                def _(pool):
                    with pool.Fori(0, NB) as blk:
                        pool.wait_ge(q_full, blk * 2 + 1)
                        pool.tensor_copy(stage[:, :, :], ctxT[:, :, ds(blk * BLK, BLK)]).then_inc(staged, 1)
                        for u in range(2):
                            post.power(pool, blk, u)
                            nrm.power(pool, blk, u)

                @block.scalar
                def _(act):
                    with act.Fori(0, NB) as blk:
                        for m in range(KD):
                            act.wait_ge(q_full, blk * 2 + (m + 1))
                            act.activation(qT[:, m, :], ps[:, m, :], ACT.Identity, bias=col("L2_bq", m)).then_inc(q_in, 1)
                        for u in range(2):
                            act.wait_ge(c_full, blk * 2 + (u + 1))
                            act.activation(kT[:, :, u * SEQ:(u + 1) * SEQ], ps[:, u, :].rearrange("p (m q) -> p m q", m=KD),
                                           ACT.Identity).then_inc(c_in, 1)
                        for u in range(2):
                            act.wait_ge(n_full, blk * 2 + (u + 1))
                            store_T(act, xnT, 4 + u, blk, u).then_inc(xT_in, 1)

                @block.vector
                def _(dve):
                    dve.wait_ge(ld_mask, 16)
                    dve.tensor_reduce(anym[:, 0, :], mask8, AXX, ALU.max).then_inc(poison, 1)
                    dve.wait_ge(poison, 1)
                    dve.tensor_scalar(anym[:, 0, :], anym[:, 0, :], 3.0e38, 3.0e38, ALU.mult, ALU.mult).then_inc(poison, 1)
                    dve.wait_ge(poison, 2)
                    dve.tensor_tensor(anym[:, 1, :], anym[:, 0, :], anym[:, 0, :], ALU.subtract).then_inc(poison, 1)
                    dve.wait_ge(poison, 3)
                    dve.tensor_scalar(anym[:, 1, :], anym[:, 1, :], gate(2), None, ALU.add).then_inc(poison, 1)
                    dve.wait_ge(poison, 4)
                    dve.wait_ge(ld_rowsA, 48)
                    with dve.Fori(0, NB) as blk:
                        for u in range(2):
                            for i, dst in enumerate((ktok, vt)):
                                dve.wait_ge(t_full, blk * 4 + (2 * u + i + 1))
                                dve.tensor_tensor(dst[:, 2 * u:2 * u + 2, :], ps[:, 2 + u + 2 * i, :].rearrange("p (t d) -> p t d", t=2),
                                                  rowsA[:, i, :].unsqueeze(1).broadcast_to([P, 2, D]), ALU.add).then_inc(t_in, 1)
                        dve.wait_ge(kv_full, blk + 1)
                        dve.tensor_tensor(kv.rearrange("p a (m d) -> p (a m) d", m=2), ps[:, 6, :].rearrange("p (a d) -> p a d", a=4),
                                          bmask[:, :].unsqueeze(1).broadcast_to([P, 4, P]), ALU.mult).then_inc(kv_in, 1)
                        for u in range(2):
                            dve.wait_ge(o_full, blk * 2 + (u + 1))
                            dve.tensor_tensor(ts[:, :, :], ps[:, 2 + u, :].rearrange("p (t d) -> p t d", t=2),
                                              rowsA[:, 2, :].unsqueeze(1).broadcast_to([P, 2, D]), ALU.add).then_inc(o_in, 1)
                            dve.wait_ge(o_in, blk * 2 + (u + 1))
                            dve.tensor_tensor(ts[:, :, :], ts[:, :, :], xn_tok[:, ds(blk * 4 + 2 * u, 2), :], ALU.add).then_inc(sums, 1)
                            dve.wait_ge(sums, blk * 2 + (u + 1))
                            tp = lambda t: ts[:, t, :]
                            post.statistics(dve, blk, u, tp)
                            post.result(dve, blk, u, tp, tp)
                            dve.wait_ge(post.link, post.done(blk, u))
                            poisoned = lambda t: anym[:, 1, ds(blk * 4 + (2 * u + t), 1)]
                            scale_and_add(dve, link, (blk * 2 + u) * 3, rowsA[:, 3, :], rowsA[:, 4, :], blk, u, poisoned)
                            xp = x_pair(blk, u)
                            nrm.statistics(dve, blk, u, xp)
                            wait(dve, n_full, blk * 2 + u)
                            nrm.result(dve, blk, u, lambda t: xs[:, t, :], xp)

                @block.tensor
                def _(pe):
                    pe.wait_ge(ld_att[0], 32)
                    with pe.Fori(0, NB) as blk:
                        for m in range(KD):
                            for k in range(KD):
                                ins = pe.matmul(ps[:, m, :], wq[:, k, m * P:(m + 1) * P], xnT[:, k, ds(blk * BLK, BLK)],
                                                start=(k == 0), stop=(k == KD - 1))
                            ins.then_inc(q_full, 1)
                        pe.wait_ge(staged, blk + 1)
                        wait(pe, xT_in, blk * 2)
                        for u in range(2):
                            for i, w in enumerate((wk, wv)):
                                for t in range(2):
                                    for k in range(KD):
                                        ins = pe.matmul(ps[:, 2 + u + 2 * i, t * D:(t + 1) * D], stage[:, k, (2 * u + t) * P:(2 * u + t + 1) * P],
                                                        w[:, k, :], start=(k == 0), stop=(k == KD - 1))
                                ins.then_inc(t_full, 1)
                        for u in range(2):
                            pe.wait_ge(t_in, blk * 4 + (2 * u + 2))
                            for m in range(KD):
                                for t in range(2):
                                    ins = pe.matmul(ps[:, 6, u * SEQ + m * P:u * SEQ + (m + 1) * P], ktok[:, 2 * u + t, m * P:(m + 1) * P],
                                                    vt[:, 2 * u + t, m * P:(m + 1) * P], start=(t == 0), stop=(t == 1))
                        ins.then_inc(kv_full, 1)
                        pe.wait_ge(q_in, blk * 2 + 2)
                        pe.wait_ge(kv_in, blk + 1)
                        for u in range(2):
                            for m in range(KD):
                                ins = pe.matmul(ps[:, u, m * SEQ:(m + 1) * SEQ], kv[:, u, m * P:(m + 1) * P],
                                                qT[:, m, u * SEQ:(u + 1) * SEQ], start=True, stop=True)
                            ins.then_inc(c_full, 1)
                        for u in range(2):
                            pe.wait_ge(c_in, blk * 2 + (u + 1))
                            for t in range(2):
                                for m in range(KD):
                                    ins = pe.matmul(ps[:, 2 + u, t * D:(t + 1) * D], kT[:, m, u * SEQ + t * P:u * SEQ + (t + 1) * P],
                                                    wo[:, m, :], start=(m == 0), stop=(m == 1))
                            ins.then_inc(o_full, 1)
                        for u in range(2):
                            pe.wait_ge(nrm.link, nrm.done(blk, u))
                            transpose_pair(pe, 4 + u, xs).then_inc(n_full, 1)

        class Single:

            def __init__(self, n):
                self.s_full = psem(n + "s_full")
                self.maxed = psem(n + "maxed")
                self.e_in = psem(n + "e_in")
                self.p_full = psem(n + "p_full")
                self.p_in = psem(n + "p_in")

            def scores(self, pe, blk):
                for u in range(2):
                    for qt in range(2):
                        for k in range(KD):
                            ins = pe.matmul(ps[:, 2 * u + qt, 0:SEQ], qT[:, k, u * SEQ + qt * P:u * SEQ + (qt + 1) * P],
                                            kT[:, k, u * SEQ:(u + 1) * SEQ], start=(k == 0), stop=(k == KD - 1))
                        ins.then_inc(self.s_full, 1)

            def turn(self, pe, blk):
                for u in range(2):
                    pe.wait_ge(self.e_in, blk * 4 + (2 * u + 2))
                    for kt in range(2):
                        for qt in range(2):
                            ins = pe.transpose(ps[:, 6 + u, kt * SEQ + qt * P:kt * SEQ + (qt + 1) * P],
                                               prob[:, u, qt, 0, kt * P:(kt + 1) * P], ident[:, :])
                    ins.then_inc(self.p_full, 1)

            def exps(self, act, blk, from_psum):
                for u in range(2):
                    for qt in range(2):
                        act.wait_ge(self.maxed, blk * 4 + (2 * u + qt + 1))
                        dst = prob[:, u, qt, 0, :]
                        src = ps[:, 2 * u + qt, 0:SEQ] if from_psum else prob[:, u, qt, 1, :]
                        act.activation(dst, src, ACT.Exp, bias=negmax[:, u, qt, 0:1], accum_out=rowsum[:, u, qt, 0:1]).then_inc(self.e_in, 1)

            def turned(self, act, blk):
                for u in range(2):
                    act.wait_ge(self.p_full, blk * 2 + (u + 1))
                    act.activation(probT[:, u].rearrange("p a b -> p (a b)"), ps[:, 6 + u, :], ACT.Identity).then_inc(self.p_in, 1)

        vtok = rowsF[:, 4:8, :]

        def phase_trees(sync_tail):
            n = "L2f_"
            staged = psem(n + "staged")
            node_full = psem(n + "node_full")
            link = psem(n + "link")
            sel_full = psem(n + "sel_full")
            sel_in = psem(n + "sel_in")
            selm_in = psem(n + "selm_in")
            h_full = psem(n + "h_full")
            h_in = psem(n + "h_in")
            y_full = psem(n + "y_full")
            y_in = psem(n + "y_in")
            o_full = psem(n + "o_full")
            o_in = psem(n + "o_in")
            rg = psem(n + "rg")
            n_full = psem(n + "n_full")
            xT_in = psem(n + "xT_in")
            cst = psem(n + "cst")
            cleared = psem(n + "cleared")
            ld_b2 = psem(n + "ld_b2")
            nrm = Norm(n + "norm", 2)
            at = Single(n)
            LINKS = 10

            with nc.Block() as block:
                @block.sync
                def _(sp):
                    sp.wait_ge(cleared, 2)
                    for t in range(TREES):
                        sp.dma_start(b2pad[32 * t:32 * t + NLEAF, t, :], a["L2_b2"][t]).then_inc(ld_b2, 16)
                    sync_tail(sp)

                @block.gpsimd
                def _(pool):
                    pool.memset(selpad, 0.0).then_inc(cleared, 1)
                    pool.memset(b2pad[:, :, :], 0.0).then_inc(cleared, 1)
                    pool.tensor_copy(stage[:, :, :], xnT[:, :, 0:BLK]).then_inc(staged, 1)
                    pool.memset(leafw[:, :, :], BIG).then_inc(cst, 1)
                    for t in range(TREES):
                        pool.wait_ge(cst, 2 * t + 1)
                        pool.affine_select(out=leafw[:, t, :], in_=leafw[:, t, :], pattern=[[1, F]], compare_op=ALU.is_ge, fill=0.0,
                                           base=LEAFW * 32 * t, channel_multiplier=-LEAFW).then_inc(cst, 1)
                        pool.wait_ge(cst, 2 * t + 2)
                        pool.affine_select(out=leafw[:, t, :], in_=leafw[:, t, :], pattern=[[-1, F]], compare_op=ALU.is_ge, fill=0.0,
                                           base=LEAFW - 1 - LEAFW * 32 * t, channel_multiplier=LEAFW).then_inc(cst, 1)
                    with pool.Fori(0, NB - 1) as blk:
                        pool.wait_ge(node_full, blk + 1)
                        pool.tensor_copy(stage[:, :, :], xnT[:, :, ds(blk * BLK + BLK, BLK)]).then_inc(staged, 1)
                        for u in range(2):
                            nrm.power(pool, blk, u)
                    for u in range(2):
                        nrm.power(pool, NB - 1, u)

                @block.scalar
                def _(act):
                    with act.Fori(0, NB) as blk:
                        act.wait_ge(sel_full, blk + 1)
                        act.activation(selT, ps[:, 7, :], ACT.Identity).then_inc(sel_in, 1)
                        for t in range(TREES):
                            for f in range(NF):
                                act.wait_ge(h_full, blk * 24 + (8 * t + f + 1))
                                act.activation(hT[:, f, :], ps[:, f % 4, :], ACT.Relu, bias=col("L2_b1", t * NF + f)).then_inc(h_in, 1)
                            for i in range(2):
                                act.wait_ge(y_full, blk * 6 + (2 * t + i + 1))
                                if t < 2:
                                    act.activation((qT, kT)[t][:, i, :], ps[:, 4 + i, :], ACT.Identity, scale=(D ** -0.5 if t == 0 else 1.0)).then_inc(y_in, 1)
                                else:
                                    act.activation(vtok[:, 2 * i:2 * i + 2, :], ps[:, 4 + i, :].rearrange("p (t d) -> p t d", t=2),
                                                   ACT.Identity).then_inc(y_in, 1)
                        at.exps(act, blk, True)
                        at.turned(act, blk)
                        for u in range(2):
                            act.wait_ge(n_full, blk * 2 + (u + 1))
                            store_T(act, xnT, 6 + u, blk, u).then_inc(xT_in, 1)

                @block.vector
                def _(dve):
                    dve.wait_ge(cleared, 1)
                    with dve.Fori(0, NB) as blk:
                        count = [0]

                        def step(ins):
                            count[0] += 1
                            ins.then_inc(link, 1)
                            dve.wait_ge(link, blk * LINKS + count[0])

                        dve.wait_ge(node_full, blk + 1)
                        nodes = dec[:, :, :, 0:NODES]
                        raw = ps[:, 6, 0:4 * TREES * NODES].rearrange("p (t j) -> p t j", t=4)
                        nb = small[:, E1:].unsqueeze(1).broadcast_to([P, 4, TREES * NODES])
                        flat = rt[:, 0:2, :, :].rearrange("p a b c -> p (a b c)")[:, 0:4 * TREES * NODES]
                        step(dve.tensor_tensor(flat.rearrange("p (t j) -> p t j", t=4), raw, nb, ALU.add))
                        step(dve.tensor_scalar(nodes, flat.rearrange("p (t r j) -> p t r j", t=4, r=TREES), 0.0, None, ALU.is_ge))
                        step(dve.tensor_copy(path[:, 0, :, :, 1:2], dec[:, :, :, 0:1]))
                        step(dve.tensor_scalar(path[:, 0, :, :, 0:1], dec[:, :, :, 0:1], -1.0, 1.0, ALU.mult, ALU.add))
                        for lev in range(1, DEPTH):
                            w = 1 << lev
                            src = path[:, (lev + 1) % 2, :, :, 0:w]
                            if lev == DEPTH - 1:
                                dst = selpad[:, :, 0:32 * TREES].rearrange("p t (r l) -> p t r l", r=TREES)
                            else:
                                dst = path[:, lev % 2]
                            right, left = dst[:, :, :, 1:2 * w:2], dst[:, :, :, 0:2 * w:2]
                            step(dve.tensor_tensor(right, src, dec[:, :, :, w - 1:2 * w - 1], ALU.mult))
                            step(dve.tensor_tensor(left, src, right, ALU.subtract))
                        assert count[0] == LINKS
                        dve.wait_ge(sel_in, blk + 1)
                        dve.tensor_scalar(selm[:, :], selT, -1.0, None, ALU.add).then_inc(selm_in, 1)
                        for u in range(2):
                            for qt in range(2):
                                dve.wait_ge(at.s_full, blk * 4 + (2 * u + qt + 1))
                                dve.tensor_reduce(negmax[:, u, qt, 0:1], ps[:, 2 * u + qt, 0:SEQ], AXX, ALU.max, negate=True).then_inc(at.maxed, 1)
                        for u in range(2):
                            dve.wait_ge(at.e_in, blk * 4 + (2 * u + 2))
                            dve.reciprocal(rinv[:, u, :, 0], rowsum[:, u, :, 0]).then_inc(rg, 1)
                            dve.wait_ge(rg, blk * 4 + (2 * u + 1))
                            dve.tensor_scalar(rinv[:, u, :, 1], rinv[:, u, :, 0], gate(4 + 2), None, ALU.mult).then_inc(rg, 1)
                            dve.wait_ge(rg, blk * 4 + (2 * u + 2))
                            dve.wait_ge(o_full, blk * 2 + (u + 1))
                            xp = x_pair(blk, u)
                            for t in range(2):
                                x = xp(t)[:, 0, :]
                                ins = dve.scalar_tensor_tensor(x, ps[:, 4 + u, t * D:(t + 1) * D], rinv[:, u, t, 1:2], x, ALU.mult, ALU.add)
                            ins.then_inc(o_in, 1)
                            dve.wait_ge(o_in, blk * 2 + (u + 1))
                            nrm.statistics(dve, blk, u, xp)
                            wait(dve, n_full, blk * 2 + u)
                            nrm.result(dve, blk, u, lambda t: xs[:, t, :], xp)

                @block.tensor
                def _(pe):
                    go = E0 - 1 + E1
                    pe.wait_ge(cst, 7)
                    pe.wait_ge(ld_b2, 48)
                    for s, loads in TREE_LOADS:
                        pe.wait_ge(ld_w[s], 32 * loads)
                    with pe.Fori(0, NB) as blk:
                        pe.wait_ge(staged, blk + 1)
                        wait(pe, xT_in, blk * 2)
                        for t in range(4):
                            for k in range(KD):
                                ins = pe.matmul(ps[:, 6, t * TREES * NODES:(t + 1) * TREES * NODES], stage[:, k, t * P:(t + 1) * P],
                                                gatew[:, k, go:go + TREES * NODES], start=(k == 0), stop=(k == KD - 1))
                        ins.then_inc(node_full, 1)
                        pe.wait_ge(link, blk * LINKS + LINKS)
                        for t in range(4):
                            ins = pe.transpose(ps[:, 7, t * P:(t + 1) * P], selpad[:, t, :], ident[:, :])
                        ins.then_inc(sel_full, 1)
                        for t in range(TREES):
                            sl = TREE_LOADS[t][0]
                            for f in range(NF):
                                if f >= 4:
                                    pe.wait_ge(h_in, blk * 24 + (8 * t + f - 3))
                                for k in range(KD):
                                    pe.matmul(ps[:, f % 4, :], w1[sl][:, k, f * P:(f + 1) * P], xnT[:, k, ds(blk * BLK, BLK)],
                                              start=(k == 0), stop=False)
                                if t == 0 and f == 0:
                                    pe.wait_ge(selm_in, blk + 1)
                                pe.matmul(ps[:, f % 4, :], leafw[:, t, f * P:(f + 1) * P], selm[:, :], start=False, stop=True).then_inc(h_full, 1)
                            for i in range(2):
                                if t or i:
                                    j = 2 * t + i
                                    if j >= 2:
                                        pe.wait_ge(y_in, blk * 6 + (j - 1))
                                if t < 2:
                                    for f in range(NF):
                                        if i == 0:
                                            pe.wait_ge(h_in, blk * 24 + (8 * t + f + 1))
                                        pe.matmul(ps[:, 4 + i, :], w2[sl][:, f, i * P:(i + 1) * P], hT[:, f, :], start=(f == 0), stop=False)
                                    ins = pe.matmul(ps[:, 4 + i, :], b2pad[:, t, i * P:(i + 1) * P], selT, start=False, stop=True)
                                else:
                                    for tt in range(2):
                                        q = (2 * i + tt) * P
                                        o = ps[:, 4 + i, tt * D:(tt + 1) * D]
                                        for f in range(NF):
                                            if i == 0 and tt == 0:
                                                pe.wait_ge(h_in, blk * 24 + (8 * t + f + 1))
                                            pe.matmul(o, hT[:, f, q:q + P], w2[sl][:, f, :], start=(f == 0), stop=False)
                                        ins = pe.matmul(o, selT[:, q:q + P], b2pad[:, t, :], start=False, stop=True)
                                ins.then_inc(y_full, 1)
                        pe.wait_ge(y_in, blk * 6 + 4)
                        at.scores(pe, blk)
                        at.turn(pe, blk)
                        pe.wait_ge(y_in, blk * 6 + 6)
                        for u in range(2):
                            pe.wait_ge(at.p_in, blk * 2 + (u + 1))
                            for t in range(2):
                                for kt in range(2):
                                    ins = pe.matmul(ps[:, 4 + u, t * D:(t + 1) * D], probT[:, u, kt, t * P:(t + 1) * P], vtok[:, 2 * u + kt, :],
                                                    start=(kt == 0), stop=(kt == 1))
                            ins.then_inc(o_full, 1)
                        for u in range(2):
                            pe.wait_ge(nrm.link, nrm.done(blk, u))
                            transpose_pair(pe, 6 + u, xs).then_inc(n_full, 1)

        def phase_padded(sync_tail):
            n = "L3a_"
            wq, wk, wv, wo = (attw[:, 1, i] for i in range(4))
            padm, pada = wbuf[:, 2, 0:T], wbuf[:, 2, T:2 * T]
            padi = hbuf[:, 0:T].bitcast(I32)
            staged = psem(n + "staged")
            q_full = psem(n + "q_full")
            q_in = psem(n + "q_in")
            v_full = psem(n + "v_full")
            v_in = psem(n + "v_in")
            mskd = psem(n + "masked")
            c_full = psem(n + "c_full")
            c_in = psem(n + "c_in")
            o_full = psem(n + "o_full")
            o_in = psem(n + "o_in")
            n_full = psem(n + "n_full")
            xT_in = psem(n + "xT_in")
            copied = psem(n + "copied")
            link = psem(n + "link")
            pads = psem(n + "pads")
            post, nrm = Norm(n + "post", 2), Norm(n + "norm", 2)
            at = Single(n)

            with nc.Block() as block:
                @block.sync
                def _(sp):
                    sp.dma_start(padi, a["pad"].unsqueeze(0).broadcast_to([P, T])).then_inc(ld_pad, 16)
                    sync_tail(sp)

                @block.gpsimd
                def _(pool):
                    with pool.Fori(0, NB) as blk:
                        pool.wait_ge(q_full, blk * 4 + 1)
                        pool.tensor_copy(stage[:, :, :], ctxT[:, :, ds(blk * BLK, BLK)]).then_inc(staged, 1)
                        for u in range(2):
                            post.power(pool, blk, u)
                            nrm.power(pool, blk, u)
                            pool.wait_ge(nrm.link, nrm.done(blk, u))
                            pool.tensor_copy(xn_tok[:, ds(blk * 4 + 2 * u, 2), :], xs[:, :, :]).then_inc(copied, 1)

                @block.scalar
                def _(act):
                    with act.Fori(0, NB) as blk:
                        for j in range(4):
                            m = j % 2
                            act.wait_ge(q_full, blk * 4 + (j + 1))
                            if j < 2:
                                act.activation(qT[:, m, :], ps[:, j, :], ACT.Identity, bias=qbias[:, 2 + m:3 + m], scale=D ** -0.5).then_inc(q_in, 1)
                            else:
                                act.activation(kT[:, m, :], ps[:, j, :], ACT.Identity, bias=col("L3_bk", m)).then_inc(q_in, 1)
                        at.exps(act, blk, False)
                        at.turned(act, blk)
                        for u in range(2):
                            act.wait_ge(c_full, blk * 2 + (u + 1))
                            act.activation(probT[:, 2 + u].rearrange("p a b -> p (a b)"), ps[:, 4 + u, :], ACT.Identity).then_inc(c_in, 1)
                        for u in range(2):
                            act.wait_ge(n_full, blk * 2 + (u + 1))
                            store_T(act, xnT, 4 + u, blk, u).then_inc(xT_in, 1)

                @block.vector
                def _(dve):
                    dve.wait_ge(ld_pad, 16)
                    dve.tensor_scalar(pada, padi, 0.0, NEG, ALU.is_equal, ALU.mult)
                    dve.tensor_scalar(padm, padi, 0.0, None, ALU.not_equal).then_inc(pads, 1)
                    dve.wait_ge(pads, 1)
                    dve.wait_ge(ld_rowsA, 64)
                    with dve.Fori(0, NB) as blk:
                        for u in range(2):
                            dve.wait_ge(v_full, blk * 2 + (u + 1))
                            dve.tensor_tensor(vtok[:, 2 * u:2 * u + 2, :], ps[:, 4 + u, :].rearrange("p (t d) -> p t d", t=2),
                                              rowsA[:, 0, :].unsqueeze(1).broadcast_to([P, 2, D]), ALU.add).then_inc(v_in, 1)
                        for u in range(2):
                            for qt in range(2):
                                j = 2 * u + qt
                                sc = prob[:, u, qt, 1, :]
                                dve.wait_ge(at.s_full, blk * 4 + (j + 1))
                                dve.tensor_tensor(sc, ps[:, j, 0:SEQ], padm[:, ds(blk * BLK + u * SEQ, SEQ)], ALU.mult).then_inc(mskd, 1)
                                dve.wait_ge(mskd, blk * 8 + (2 * j + 1))
                                dve.tensor_tensor(sc, sc, pada[:, ds(blk * BLK + u * SEQ, SEQ)], ALU.add).then_inc(mskd, 1)
                                dve.wait_ge(mskd, blk * 8 + (2 * j + 2))
                                dve.tensor_reduce(negmax[:, u, qt, 0:1], sc, AXX, ALU.max, negate=True).then_inc(at.maxed, 1)
                        for u in range(2):
                            dve.wait_ge(at.e_in, blk * 4 + (2 * u + 2))
                            dve.reciprocal(rinv[:, u, :, 0], rowsum[:, u, :, 0]).then_inc(o_in, 1)
                            dve.wait_ge(o_in, blk * 4 + (2 * u + 1))
                            dve.wait_ge(o_full, blk * 2 + (u + 1))
                            for t in range(2):
                                ins = dve.scalar_tensor_tensor(ts[:, t, :], ps[:, 6 + u, t * D:(t + 1) * D], rinv[:, u, t, 0:1], rowsA[:, 1, :],
                                                               ALU.mult, ALU.add)
                            ins.then_inc(o_in, 1)
                            dve.wait_ge(o_in, blk * 4 + (2 * u + 2))
                            tp = lambda t: ts[:, t, :]
                            post.statistics(dve, blk, u, tp)
                            post.result(dve, blk, u, tp, tp)
                            dve.wait_ge(post.link, post.done(blk, u))
                            scale_and_add(dve, link, (blk * 2 + u) * 3, rowsA[:, 2, :], rowsA[:, 3, :], blk, u, lambda t: gate(3))
                            xp = x_pair(blk, u)
                            nrm.statistics(dve, blk, u, xp)
                            wait(dve, n_full, blk * 2 + u)
                            wait(dve, copied, blk * 2 + u)
                            nrm.result(dve, blk, u, lambda t: xs[:, t, :], xp)

                @block.tensor
                def _(pe):
                    pe.wait_ge(ld_att[1], 32)
                    with pe.Fori(0, NB) as blk:
                        for j in range(4):
                            m = j % 2
                            w, src = (wq, xnT) if j < 2 else (wk, ctxT)
                            for k in range(KD):
                                ins = pe.matmul(ps[:, j, :], w[:, k, m * P:(m + 1) * P], src[:, k, ds(blk * BLK, BLK)],
                                                start=(k == 0), stop=(k == KD - 1))
                            ins.then_inc(q_full, 1)
                        pe.wait_ge(staged, blk + 1)
                        wait(pe, xT_in, blk * 2)
                        for u in range(2):
                            for t in range(2):
                                for k in range(KD):
                                    ins = pe.matmul(ps[:, 4 + u, t * D:(t + 1) * D], stage[:, k, (2 * u + t) * P:(2 * u + t + 1) * P], wv[:, k, :],
                                                    start=(k == 0), stop=(k == KD - 1))
                            ins.then_inc(v_full, 1)
                        pe.wait_ge(q_in, blk * 4 + 4)
                        at.scores(pe, blk)
                        at.turn(pe, blk)
                        pe.wait_ge(v_in, blk * 2 + 2)
                        for u in range(2):
                            pe.wait_ge(at.p_in, blk * 2 + (u + 1))
                            for m in range(KD):
                                for kt in range(2):
                                    ins = pe.matmul(ps[:, 4 + u, m * SEQ:(m + 1) * SEQ], vtok[:, 2 * u + kt, m * P:(m + 1) * P],
                                                    probT[:, u, kt, :], start=(kt == 0), stop=(kt == 1))
                            ins.then_inc(c_full, 1)
                        for u in range(2):
                            pe.wait_ge(c_in, blk * 2 + (u + 1))
                            for t in range(2):
                                for m in range(KD):
                                    ins = pe.matmul(ps[:, 6 + u, t * D:(t + 1) * D], probT[:, 2 + u, m, t * P:(t + 1) * P], wo[:, m, :],
                                                    start=(m == 0), stop=(m == 1))
                            ins.then_inc(o_full, 1)
                        for u in range(2):
                            pe.wait_ge(nrm.link, nrm.done(blk, u))
                            transpose_pair(pe, 4 + u, xs).then_inc(n_full, 1)

        def phase_last():
            n = "L3f_"
            sl, loads = LAST_LOAD
            h_full, h_in = psem(n + "h_full"), psem(n + "h_in")
            y_full, y_in = psem(n + "y_full"), psem(n + "y_in")
            sums = psem(n + "sums")
            link = psem(n + "link")
            post = Norm(n + "post", 2)

            with nc.Block() as block:
                @block.sync
                def _(sp):
                    rows_out = out.rearrange("(t p) d -> p t d", p=P)
                    with sp.Fori(0, NB) as blk:
                        for u in range(2):
                            sp.wait_ge(link, (blk * 2 + (u + 1)) * 3)
                            sp.dma_start(rows_out[:, ds(blk * 4 + 2 * u, 2), :], x_tok[:, ds(blk * 4 + 2 * u, 2), :]).then_inc(stored, 16)
                    sp.wait_ge(stored, 2 * NB * 16)

                @block.gpsimd
                def _(pool):
                    with pool.Fori(0, NB) as blk:
                        for u in range(2):
                            post.power(pool, blk, u)

                @block.scalar
                def _(act):
                    with act.Fori(0, NB) as blk:
                        for f in range(NF):
                            act.wait_ge(h_full, blk * NF + (f + 1))
                            act.activation(hT[:, f, :], ps[:, f % 4, :], ACT.Relu, bias=col("L3_b1", f)).then_inc(h_in, 1)

                @block.vector
                def _(dve):
                    dve.wait_ge(ld_rowsF, 32)
                    with dve.Fori(0, NB) as blk:
                        for u in range(2):
                            dve.wait_ge(y_full, blk * 2 + (u + 1))
                            dve.tensor_tensor(ts[:, :, :], ps[:, 4 + u, :].rearrange("p (t d) -> p t d", t=2),
                                              rowsF[:, 0, :].unsqueeze(1).broadcast_to([P, 2, D]), ALU.add).then_inc(y_in, 1)
                            dve.wait_ge(y_in, blk * 2 + (u + 1))
                            dve.tensor_tensor(ts[:, :, :], ts[:, :, :], xn_tok[:, ds(blk * 4 + 2 * u, 2), :], ALU.add).then_inc(sums, 1)
                            dve.wait_ge(sums, blk * 2 + (u + 1))
                            tp = lambda t: ts[:, t, :]
                            post.statistics(dve, blk, u, tp)
                            post.result(dve, blk, u, tp, tp)
                            dve.wait_ge(post.link, post.done(blk, u))
                            scale_and_add(dve, link, (blk * 2 + u) * 3, rowsF[:, 1, :], rowsF[:, 2, :], blk, u, lambda t: gate(4 + 3))

                @block.tensor
                def _(pe):
                    pe.wait_ge(ld_w[sl], 32 * loads)
                    with pe.Fori(0, NB) as blk:
                        for f in range(NF):
                            if f >= 4:
                                pe.wait_ge(h_in, blk * NF + (f - 3))
                            for k in range(KD):
                                ins = pe.matmul(ps[:, f % 4, :], w1[sl][:, k, f * P:(f + 1) * P], xnT[:, k, ds(blk * BLK, BLK)],
                                                start=(k == 0), stop=(k == KD - 1))
                            ins.then_inc(h_full, 1)
                        for u in range(2):
                            wait(pe, y_in, blk * 2)
                            for t in range(2):
                                for f in range(NF):
                                    if u == 0 and t == 0:
                                        pe.wait_ge(h_in, blk * NF + (f + 1))
                                    ins = pe.matmul(ps[:, 4 + u, t * D:(t + 1) * D], hT[:, f, (2 * u + t) * P:(2 * u + t + 1) * P],
                                                    w2[sl][:, f, :], start=(f == 0), stop=(f == NF - 1))
                            ins.then_inc(y_full, 1)

        TREE_LOADS = ((0, 2), (1, LOADED[1][0] + STEPS_OF[1] // 2 + 2),
                      (2, LOADED[1][1] + STEPS_OF[1] // 2 + 1))
        LAST_LOAD = (0, 3)

        def during_attn0(sp):
            sp.dma_start(attw[:, 1, 3], a["L1_wo"].rearrange("(k p) n -> p k n", p=P)).then_inc(ld_att[1], 16)

        def during_ffn0(sp):
            load_rows(sp, rowsA, "attn1", ld_rowsA)
            load_att(sp, 0, 1)

        def during_attn1(sp):
            load_expert(sp, 0, a["L2_w1"][0], a["L2_w2"][0])

        def during_ffn1(sp):
            load_rows(sp, rowsA, "attn2", ld_rowsA)
            load_att(sp, 1, 2)

        def during_attn2(sp):
            for t in (1, 2):
                load_expert(sp, t, a["L2_w1"][t], a["L2_w2"][t])

        def during_ffn2(sp):
            load_rows(sp, rowsA, "attn3", ld_rowsA)
            load_rows(sp, rowsF, "ffn3", ld_rowsF)

        def during_attn3(sp):
            load_expert(sp, LAST_LOAD[0], a["L3_w1"], a["L3_w2"])

        phase_setup()
        end_phase()
        phase_heads(0, during_attn0)
        end_phase()
        phase_experts(0, ACT.Relu, 4, False, during_ffn0)
        end_phase()
        phase_heads(1, during_attn1)
        end_phase()
        phase_experts(1, ACT.Gelu, 5, True, during_ffn1)
        end_phase()
        phase_linear(during_attn2)
        end_phase()
        phase_trees(during_ffn2)
        end_phase()
        phase_padded(during_attn3)
        end_phase()
        phase_last()


def kernel(**inputs):
    import numpy as np
    import concourse.bacc as bacc
    from concourse.bass_utils import run_bass_kernel_spmd

    v = {k: np.asarray(x) for k, x in inputs.items()}

    def colsof(x, n):
        return x.reshape(n, P).T

    arrays = {
        "x": v["x"].reshape(T, D), "ctx": v["ctx_1024"].reshape(T, D),
        "mask": v["mask_Bx1xSxS2_bf0"].reshape(T, SEQ), "pad": v["mask_Bx1xS2_ik1"].reshape(T),
        "g": np.concatenate([v["g_xattn"], v["g_ffn"]]),
        "attw": np.stack([np.stack([v[f"L0_xattn_{w}"] for w in ("Wq", "Wk", "Wv", "Wo")]),
                          np.stack([v[f"L2_xattn_{w}"].T for w in ("wq_w", "wk_w", "wv_w", "wo_w")]),
                          np.stack([v[f"L3_xattn_{w}"] for w in ("Wq", "Wk", "Wv", "Wo")])]),
        "L1_wo": v["L1_xattn_Wo"].T,
        "rep": np.stack([np.tile(v[f"L1_xattn_{w}"].T, (GH, 1)) for w in ("Wq", "Wk", "Wv")], axis=1),
        "L0_w1": np.concatenate([v["L0_ffn_W1"], v["L0_ffn_Ws1"][None]]),
        "L0_w2": np.concatenate([v["L0_ffn_W2"], v["L0_ffn_Ws2"][None]]),
        "L1_w1": v["L1_ffn_W1"], "L1_w2": v["L1_ffn_W2"],
        "L0_b1r": v["L0_ffn_b1"].reshape(E0 - 1, NF, P).transpose(0, 2, 1), "L0_b2": v["L0_ffn_b2"],
        "L1_b1r": v["L1_ffn_b1"].reshape(E1, NF, P).transpose(0, 2, 1), "L1_b2": v["L1_ffn_b2"],
        "L2_w1": np.stack([v[f"L2_ffn_{t}_w1"].transpose(1, 0, 2).reshape(D, F) for t in "qkv"]),
        "L2_w2": np.stack([v[f"L2_ffn_{t}_w2"].reshape(F, D) for t in "qkv"]),
        "L2_b2": np.stack([v[f"L2_ffn_{t}_b2"] for t in "qkv"]),
        "L3_w1": v["L3_ffn_w1"][0], "L3_w2": v["L3_ffn_w2"][0],
    }
    columns = {
        "L0_bq": v["L0_xattn_bq"], "L0_bk": v["L0_xattn_bk"],
        "L0_bs1": v["L0_ffn_bs1"],
        "L2_bq": v["L2_xattn_wq_b"], "L2_b1": np.concatenate([v[f"L2_ffn_{t}_b1"].reshape(-1) for t in "qkv"]),
        "L3_bq": v["L3_xattn_bq"], "L3_bk": v["L3_xattn_bk"], "L3_b1": v["L3_ffn_b1"][0],
    }
    arrays["cols"] = np.concatenate([colsof(columns[k], n) for k, (_, n) in COLS.items()], axis=1)
    arrays["rows"] = np.stack([
        v["L0_xattn_bv"], v["L0_xattn_bo"], v["L0_ffn_bs2"], v["L1_xattn_bo"],
        v["L2_xattn_wk_b"], v["L2_xattn_wv_b"], v["L2_xattn_wo_b"], v["L2_xattn_ln_g"], v["L2_xattn_ln_b"],
        v["L3_xattn_bv"], v["L3_xattn_bo"], v["L3_xattn_g0"], v["L3_xattn_beta0"],
        v["L3_ffn_b2"][0], v["L3_ffn_gamma"], v["L3_ffn_beta"]])
    gatew = np.concatenate([v["L0_ffn_Wg"], v["L1_ffn_Wg"], *[v[f"L2_ffn_{t}_node_w"].T for t in "qkv"]], axis=1)
    arrays["gatew"] = gatew.reshape(KD, P, NGATEW).transpose(1, 0, 2)
    arrays["small"] = np.concatenate([v["L1_ffn_bg"], *[v[f"L2_ffn_{t}_node_b"] for t in "qkv"]])

    nc = bacc.Bacc("TRN2", target_bir_lowering=False, num_devices=1)
    a, feed = {}, {}
    for name, x in arrays.items():
        feed["in_" + name] = np.ascontiguousarray(x)
        a[name] = nc.dram_tensor("in_" + name, x.shape, mybir.dt.from_np(x.dtype), kind="ExternalInput").ap()
    out = nc.dram_tensor("out_x", (T, D), F32, kind="ExternalOutput").ap()
    a["xg"] = nc.dram_tensor("expert_rows", (XROWS, D), F32).ap()
    a["yg"] = nc.dram_tensor("expert_outputs", (XROWS, D), F32).ap()
    decoder_kernel(nc, a, out)
    r = run_bass_kernel_spmd(nc, [feed], core_ids=[0])
    return r.results[0]["out_x"].reshape(NBATCH, SEQ, D)
```

```python
from contextlib import ExitStack

import concourse.bass as bass
from concourse import mybir

P = 128
NBATCH, SEQ, D = 8, 256, 256
T = NBATCH * SEQ
NT = T // P
BLK = 512
NB = T // BLK
KD = D // P
H, HD = 16, 16
GH = P // HD
F = 1024
NF = F // P
E0, E1 = 9, 4
NLEAF, LEAFW, DEPTH, TREES = 16, 64, 4, 3
NODES = NLEAF - 1
EPS = 1e-5
NEG = -1.0e9
BIG = 1.0e30

ALU = mybir.AluOpType
ACT = mybir.ActivationFunctionType
AXX = mybir.AxisListType.X
F32 = mybir.dt.float32
F32R = mybir.dt.float32r
BF16 = mybir.dt.bfloat16
I32 = mybir.dt.int32
U8 = mybir.dt.uint8
ds = bass.ds

COLS, ROWS = {}, {}
for _name, _n in (("L0_bq", 2), ("L0_bk", 2), ("L0_bs1", NF), ("L2_bq", 2),
                  ("L3_bq", 2), ("L3_bk", 2), ("L3_b1", NF)):
    COLS[_name] = (sum(n for _, n in COLS.values()), _n)
for _name, _n in (("attn0", 2), ("ffn0", 1), ("attn1", 1), ("attn2", 5), ("attn3", 4), ("ffn3", 3)):
    ROWS[_name] = (sum(n for _, n in ROWS.values()), _n)
NCOLS = sum(n for _, n in COLS.values())
NROWS = sum(n for _, n in ROWS.values())
NSMALL = E1 + TREES * NODES
NGATEW = (E0 - 1) + E1 + TREES * NODES

SUB = 256
STEPS_OF = tuple((n - e) // SUB + e for e, n in ((E0 - 1, 2 * T), (E1, T)))
XROWS = max(STEPS_OF) * SUB
NPAIR = NLEAF // 2
TSTEPS = (T - NPAIR) // SUB + NPAIR
NFLAG = 2 * TREES
ROW = D + NFLAG
REC = 2 * D + 1
EXP_LINK = 13
CHOSEN_LINK = (14, 7)
EXPERT_LINK = (30, 22)
PLACED_LINK = (39, 28)
T_CHOSEN, T_PLACED, T_STEPS = 12, 35, 38


def wait(eng, sem, value):
    if not isinstance(value, int) or value > 0:
        eng.wait_ge(sem, value)


def decoder_kernel(nc, a, out):
    ctx = ExitStack()
    with ctx:
        places = {}

        def sb(name, shape, dt=F32):
            places[name] = -(-nc.sbuf_base // 32) * 32
            return ctx.enter_context(nc.sbuf_tensor(name, shape, dt))

        def rounded(name, first, n):
            return nc.alloc_sbuf_tensor_at(f"{name}_r{first}", [P, n], F32R, offset=places[name] + 4 * first)[:, :]

        def sem(name):
            return ctx.enter_context(nc.semaphore(name))

        phase_sems = []

        def psem(name):
            phase_sems.append(nc.alloc_semaphore(name=name))
            return phase_sems[-1]

        def end_phase():
            nc.clear_and_free_semaphores(phase_sems)
            nc.all_engine_barrier()
            phase_sems.clear()

        x_tok = sb("x_tok", [P, NT, D])
        xnT = sb("xnT", [P, KD, T])
        ctxT = sb("ctxT", [P, KD, T])
        wbuf = sb("wbuf", [P, 3, 4096])
        hbuf = sb("hbuf", [P, 4096])
        vbuf = sb("vbuf", [P, 4096])
        attw = sb("attw", [P, 2, 4, KD, D])
        rowsA = sb("rowsA", [P, 5, D])
        rowsF = sb("rowsF", [P, 8, D])
        stage = sb("stage", [P, KD, BLK])
        qT = sb("qT", [P, KD, BLK])
        kT = sb("kT", [P, KD, BLK])
        prob = sb("prob", [P, 2, 2, 2, SEQ])
        probT = sb("probT", [P, 4, 2, SEQ])
        oT = sb("oT", [P, KD, SEQ])
        xs = sb("xs", [P, 2, D])
        ts = sb("ts", [P, 2, D])
        stats = sb("stats", [P, 4, 6])
        sm = sb("sm", [P, 8, 4])
        negmax = sb("negmax", [P, 2, 2, 2])
        rowsum = sb("rowsum", [P, 2, 2, 2])
        rinv = sb("rinv", [P, 2, 2, 2])
        cols = sb("cols", [P, NCOLS])
        qbias = sb("qbias", [P, 4])
        gates = sb("gates", [P, 8])
        small = sb("small", [P, NSMALL])
        gatew = sb("gatew", [P, KD, NGATEW])
        ident = sb("ident", [P, P])
        identb = sb("identb", [P, P], BF16)
        causal = sb("causal", [P, P], BF16)
        hmask = sb("hmask", [P, GH])
        bmask = sb("bmask", [P, P])
        mhalf = sb("mhalf", [P, 4])
        rank = sb("rank", [P, E0 - 1])
        logit = sb("logit", [P, NT, E0 - 1])
        rt = sb("rt", [P, 3, NT, E0 - 1])
        r1 = sb("r1", [P, 8, NT])
        rsum = sb("rsum", [P, 4, NT * (E0 - 1)])
        ew = sb("ew", [P, 4, E0 - 1])
        step_exp = sb("step_exp", [P, TREES * TSTEPS], I32)
        rowno = sb("rowno", [P, 2, NT], I32)
        rowt = sb("rowt", [P, NT * TREES], I32)
        b1_sb = sb("b1_sb", [P, 2, NF])
        dec = sb("dec", [P, 4, TREES, NLEAF])
        path = sb("path", [P, 2, 4, TREES, NLEAF])
        spare = sb("spare", [P, 2])
        anym = sb("anym", [P, 2, NT])
        rep = sb("rep", [P, 3, HD])
        ps = ctx.enter_context(nc.psum_tensor("ps", [P, 8, 512], F32))

        km = hbuf[:, :].rearrange("p (g j s) -> p g j s", g=2, j=GH)
        hT = hbuf[:, :].rearrange("p (f t) -> p f t", f=NF)
        vm = [wbuf[:, 2, :].rearrange("p (t h c) -> p t h c", t=2, h=H),
              vbuf[:, :].rearrange("p (t h c) -> p t h c", t=2, h=H)]
        xn_tok = vbuf[:, :].rearrange("p (t d) -> p t d", t=NT)
        mask8 = stage[:, :, :].rearrange("p a b -> p (a b)").bitcast(U8).rearrange("p (t k) -> p t k", t=NT)
        kv_all = rowsF[:, :, :].rearrange("p (b u) d -> p b (u d)", u=2)
        w1 = [wbuf[:, s, 0:2048].rearrange("p (k f) -> p k f", k=KD) for s in range(3)]
        w2 = [wbuf[:, s, 2048:4096].rearrange("p (f d) -> p f d", f=NF) for s in range(3)]

        prob_r, kT_r, hbuf_r, vbuf_r = (rounded(*x) for x in (("prob", 0, 2048), ("kT", 0, 1024), ("hbuf", 0, 4096), ("vbuf", 0, 4096)))
        wbuf_r = [rounded("wbuf", i * 4096, 4096) for i in range(3)]
        attw_r, attw1_r = rounded("attw", 0, 2048), rounded("attw", 2048, 2048)
        qT_r = rounded("qT", 0, 1024)
        xnT_r, ctxT_r = (rounded(x, 0, KD * T).rearrange("p (k t) -> p k t", k=KD) for x in ("xnT", "ctxT"))

        def rs(i, n):
            return rsum[:, i, 0:NT * n].rearrange("p (t e) -> p t e", e=n)

        def col(name, j):
            o = COLS[name][0]
            if isinstance(j, int):
                return cols[:, o + j:o + j + 1]
            return cols[:, ds(j + o, 1)]

        ld_const = sem("ld_const")
        ld_x = sem("ld_x")
        ld_att = [sem(f"ld_att{s}") for s in range(2)]
        ld_w = [sem(f"ld_w{s}") for s in range(3)]
        ld_rowsA = sem("ld_rowsA")
        ld_rowsF = sem("ld_rowsF")
        ld_pad = sem("ld_pad")
        ld_mask = sem("ld_mask")
        stored = sem("stored")
        zeroed = sem("zeroed")

        def load_rows(sp, dst, name, signal):
            o, n = ROWS[name]
            sp.dma_start(dst[:, 0:n, :], a["rows"][o:o + n, :].unsqueeze(0).broadcast_to([P, n, D])).then_inc(signal, 16)

        def load_att(sp, slot, l):
            sp.dma_start(attw[:, slot], a["attw"][l].rearrange("w (k p) n -> p w k n", p=P)).then_inc(ld_att[slot], 16)

        def load_expert(sp, slot, first, second):
            sp.dma_start(w1[slot], first.rearrange("(k p) f -> p k f", p=P)).then_inc(ld_w[slot], 16)
            sp.dma_start(w2[slot], second.rearrange("(f p) d -> p f d", p=P)).then_inc(ld_w[slot], 16)

        def gate(i):
            return gates[:, i:i + 1]

        class Norm:
            LINKS = 7

            def __init__(self, name, per, w=2):
                self.per, self.w = per, w
                self.link = psem(name + "_link")
                self.rstd = psem(name + "_rstd")
                self.centred = psem(name + "_centred")

            def statistics(self, dve, blk, j, tiles):
                self.sums(dve, tiles)
                self.moments(dve, blk, j)

            def sums(self, dve, tiles):
                w = self.w
                dve.memset(spare[:, 0:1], 0.0)
                for t in range(w):
                    ins = dve.bn_stats(stats[:, t, :], tiles(t))
                ins.then_inc(self.link, 1)

            def moments(self, dve, blk, j):
                base = (blk * self.per + j) * self.LINKS
                w = self.w
                me, mo = stats[:, 0:w, 1], stats[:, 0:w, 4]
                dve.wait_ge(self.link, base + 1)
                dve.tensor_tensor(sm[:, 0, 0:w], me, mo, ALU.add)
                dve.tensor_tensor(sm[:, 1, 0:w], me, mo, ALU.subtract)
                dve.tensor_tensor(sm[:, 2, 0:w], stats[:, 0:w, 2], stats[:, 0:w, 5], ALU.add).then_inc(self.link, 1)
                dve.wait_ge(self.link, base + 2)
                dve.tensor_tensor(sm[:, 3, 0:w], sm[:, 1, 0:w], sm[:, 1, 0:w], ALU.mult).then_inc(self.link, 1)
                dve.tensor_scalar(sm[:, 4, 0:w], sm[:, 0, 0:w], 0.5, None, ALU.mult).then_inc(self.link, 1)
                dve.wait_ge(self.link, base + 4)
                dve.scalar_tensor_tensor(sm[:, 5, 0:w], sm[:, 3, 0:w], D / 4.0, sm[:, 2, 0:w], ALU.mult, ALU.add).then_inc(self.link, 1)
                dve.wait_ge(self.link, base + 5)
                dve.tensor_scalar(sm[:, 6, 0:w], sm[:, 5, 0:w], 1.0 / D, EPS, ALU.mult, ALU.add).then_inc(self.link, 1)

            def power(self, pool, blk, j):
                pool.wait_ge(self.link, (blk * self.per + j) * self.LINKS + 6)
                pool.tensor_tensor(sm[:, 7, 0:self.w], sm[:, 6, 0:self.w], mhalf[:, 0:self.w], ALU.pow).then_inc(self.rstd, 1)

            def result(self, dve, blk, j, outs, tiles):
                dve.wait_ge(self.rstd, blk * self.per + j + 1)
                for t in range(self.w):
                    ins = dve.tensor_scalar(outs(t), tiles(t), sm[:, 4, t:t + 1], sm[:, 7, t:t + 1], ALU.subtract, ALU.mult)
                ins.then_inc(self.link, 1)

            def add_scaled(self, dve, blk, j, tiles, row, x):
                for t in range(self.w):
                    ins = dve.scalar_tensor_tensor(tiles(t), tiles(t), sm[:, 4, t:t + 1], row, ALU.subtract, ALU.mult)
                ins.then_inc(self.centred, 1)
                dve.wait_ge(self.centred, blk * self.per + j + 1)
                dve.wait_ge(self.rstd, blk * self.per + j + 1)
                for t in range(self.w):
                    ins = dve.scalar_tensor_tensor(x(t), tiles(t), sm[:, 7, t:t + 1], x(t), ALU.mult, ALU.add)
                ins.then_inc(self.link, 1)

            def done(self, blk, j):
                return (blk * self.per + j + 1) * self.LINKS

        def x_tile(blk):
            return lambda t: x_tok[:, ds(blk * 4 + t, 1), :][:, 0, :]

        def blocks(eng, body, tail):
            body(0, True)
            with eng.Fori(1, NB) as blk:
                body(blk, False)
            tail(NB - 1)

        def x_pair(blk, u):
            return lambda t: x_tok[:, ds(blk * 4 + (2 * u + t), 1), :]

        def transpose_pair(pe, bank, src):
            for k in range(KD):
                for t in range(2):
                    ins = pe.transpose(ps[:, bank, k * SEQ + t * P:k * SEQ + (t + 1) * P], src[:, t, k * P:(k + 1) * P], ident[:, :])
            return ins

        def store_T(act, dst, bank, blk, u):
            return act.activation(dst[:, :, ds(blk * BLK + u * SEQ, SEQ)],
                                  ps[:, bank, :].rearrange("p (k t) -> p k t", k=KD), ACT.Identity)

        def phase_setup():
            cst = psem("cst")
            dcst = psem("dcst")
            got_gates = psem("got_gates")
            ctx_in = [psem(f"ctx_in{s}") for s in range(2)]
            turned = psem("setup_turned")
            kept = [psem(f"setup_kept{j}") for j in range(4)]
            nrm = Norm("setup_norm", 1, 4)
            xs4 = hbuf[:, 3072:4096].rearrange("p (t d) -> p t d", t=4)
            ctx_rows = a["ctx"].rearrange("(t p) d -> p t d", p=P)

            with nc.Block() as block:
                @block.sync
                def _(sp):
                    sp.dma_start(x_tok[:, :, :], a["x"].rearrange("(t p) d -> p t d", p=P)).then_inc(ld_x, 16)
                    for dst, src in ((cols, "cols"), (gatew, "gatew"), (rep, "rep")):
                        sp.dma_start(dst[:], a[src]).then_inc(ld_const, 16)
                    sp.dma_start(gates[:, :], a["g"].unsqueeze(0).broadcast_to([P, 8])).then_inc(ld_const, 16)
                    sp.dma_start(small[:, :], a["small"].unsqueeze(0).broadcast_to([P, NSMALL])).then_inc(ld_const, 16)
                    with sp.Fori(0, NB) as blk:
                        for u in range(2):
                            wait(sp, turned, blk * 4)
                            dst = prob[:, u].rearrange("p a b s -> p (a b) s")[:, 0:2, :]
                            sp.dma_start(dst, ctx_rows[:, ds(blk * 4 + 2 * u, 2), :]).then_inc(ctx_in[u], 16)
                    load_att(sp, 0, 0)
                    load_rows(sp, rowsA, "attn0", ld_rowsA)
                    load_rows(sp, rowsF, "ffn0", ld_rowsF)
                    load_expert(sp, 0, a["L0_w1"][E0 - 1], a["L0_w2"][E0 - 1])
                    sp.wait_ge(cst, 5)
                    zero = rt[:, :, :, :].rearrange("p a b c -> p (a b c)")[:, 0:D]
                    sp.dma_start(a["xg"].rearrange("(n p) d -> p n d", p=P), zero.unsqueeze(1).broadcast_to([P, XROWS // P, D])).then_inc(zeroed, 16)
                    zero = rt[:, :, :, :].rearrange("p a b c -> p (a b c)")[:, 0:ROW]
                    for r in range(TREES):
                        sp.dma_start(a[f"xt{r}"].rearrange("(n p) d -> p n d", p=P),
                                     zero.unsqueeze(1).broadcast_to([P, TSTEPS * SUB // P, ROW])).then_inc(zeroed, 16)

                @block.gpsimd
                def _(pool):
                    ones = probT[:, 0, 0, 0:P]
                    pool.memset(ones, 1.0).then_inc(cst, 1)
                    pool.memset(mhalf[:, :], -0.5).then_inc(cst, 1)
                    pool.wait_ge(cst, 2)
                    pool.affine_select(out=ident[:, :], in_=ones, pattern=[[-1, P]], compare_op=ALU.is_equal, fill=0.0,
                                       base=0, channel_multiplier=1).then_inc(cst, 1)
                    pool.affine_select(out=identb[:, :], in_=ones, pattern=[[-1, P]], compare_op=ALU.is_equal, fill=0.0,
                                       base=0, channel_multiplier=1).then_inc(cst, 1)
                    pool.memset(wbuf[:, 2, :], 0.0)
                    pool.memset(vbuf[:, :], 0.0)
                    with pool.Fori(0, NB) as blk:
                        nrm.power(pool, blk, 0)
                    pool.memset(rt[:, :, :, :].rearrange("p a b c -> p (a b c)"), 0.0).then_inc(cst, 1)
                    pool.wait_ge(cst, 5)
                    zeros = rt[:, 0, :, :].rearrange("p a b -> p (a b)")
                    pool.affine_select(out=causal[:, :], in_=zeros, pattern=[[-1, P]], compare_op=ALU.is_ge, fill=NEG,
                                       base=0, channel_multiplier=1).then_inc(cst, 1)
                    pool.affine_select(out=hmask[:, :], in_=ones[:, 0:GH], pattern=[[-HD, GH]], compare_op=ALU.is_ge, fill=0.0,
                                       base=0, channel_multiplier=1).then_inc(cst, 1)
                    pool.wait_ge(cst, 7)
                    pool.affine_select(out=hmask[:, :], in_=hmask[:, :], pattern=[[HD, GH]], compare_op=ALU.is_ge, fill=0.0,
                                       base=HD - 1, channel_multiplier=-1).then_inc(cst, 1)
                    pool.wait_ge(cst, 8)
                    pool.tensor_scalar(bmask[:, :].rearrange("p (j c) -> p j c", c=HD),
                                       hmask[:, :].unsqueeze(2).broadcast_to([P, GH, HD]), 0.25, None, ALU.mult).then_inc(cst, 1)
                    for e in range(E0 - 1):
                        pool.memset(rank[:, e:e + 1], float(E0 - 1 - e))

                @block.vector
                def _(dve):
                    dve.wait_ge(ld_x, 16)
                    with dve.Fori(0, NB) as blk:
                        xp = x_tile(blk)
                        nrm.statistics(dve, blk, 0, xp)
                        wait(dve, turned, blk * 4)
                        nrm.result(dve, blk, 0, lambda t: xs4[:, t, :], xp)

                @block.scalar
                def _(act):
                    act.wait_ge(ld_const, 80)
                    act.activation(gates[:, :], gates[:, :], ACT.Tanh).then_inc(got_gates, 1)
                    act.mul(qbias[:, 0:2], cols[:, COLS["L0_bq"][0]:COLS["L0_bq"][0] + 2], HD ** -0.5)
                    act.mul(qbias[:, 2:4], cols[:, COLS["L3_bq"][0]:COLS["L3_bq"][0] + 2], D ** -0.5)
                    with act.Fori(0, NB) as blk:
                        for u in range(2):
                            for j, dst in ((2 * u, xnT), (2 * u + 1, ctxT)):
                                act.wait_ge(turned, blk * 4 + (j + 1))
                                store_T(act, dst, j, blk, u).then_inc(kept[j], 1)

                @block.tensor
                def _(pe):
                    pe.wait_ge(cst, 4)
                    with pe.Fori(0, NB) as blk:
                        for u in range(2):
                            pe.wait_ge(nrm.link, nrm.done(blk, 0))
                            wait(pe, kept[2 * u], blk)
                            transpose_pair(pe, 2 * u, xs4[:, 2 * u:2 * u + 2, :]).then_inc(turned, 1)
                            pe.wait_ge(ctx_in[u], blk * 16 + 16)
                            wait(pe, kept[2 * u + 1], blk)
                            transpose_pair(pe, 2 * u + 1, prob[:, u].rearrange("p a b s -> p (a b) s")).then_inc(turned, 1)

        def phase_heads(l, sync_tail):
            causal_l = l == 0
            slot = l % 2
            scale = HD ** -0.5 if l == 0 else D ** -0.5
            wq, wk, wv, wo = (attw[:, slot, i] for i in range(4))
            spare_w = (attw1_r, attw_r)[slot].rearrange("p (i k t) -> p i k t", i=2, k=KD)
            q_hi, k_hi = spare_w[:, 0], spare_w[:, 1]
            q_lo, k_lo = (x.rearrange("p (k t) -> p k t", k=KD) for x in (qT_r, kT_r))
            km_hi, km_lo = (x.rearrange("p (g j s) -> p g j s", g=2, j=GH) for x in (hbuf_r, wbuf_r[1]))
            parts = (lambda m: list(range(KD))) if l == 0 else (lambda m: [m])
            n = f"L{l}a_"
            s_full = psem(n + "s_full")
            s_read = psem(n + "s_read")
            turned_s = psem(n + "turned")
            pt_in = [psem(n + f"pt_in{hh}") for hh in range(2)]
            av = psem(n + "av")
            o_in = psem(n + "o_in")
            a_full = psem(n + "a_full")
            v_in = psem(n + "v_in")
            wo_in = psem(n + "wo_in")
            xT_in = psem(n + "xT_in")
            staged = psem(n + "staged")
            km_in = psem(n + "km_in")
            km_lo_in = psem(n + "km_lo_in")
            qk_hi = psem(n + "qk_hi")
            qk_lo = psem(n + "qk_lo")
            maxed = psem(n + "maxed")
            inv = psem(n + "inv")
            normed = psem(n + "normed")
            scaled = psem(n + "scaled")
            pre = psem(n + "pre")
            nrm = Norm(n + "norm", 2)
            wbd = psem(n + "wbd")
            STEPS = 16
            AHEAD = 3
            SF, SR = 36, 68

            def tile_full(blk, i):
                return blk * SF + (4 + i + 1)

            def tile_read(blk, i):
                return blk * SR + (4 + 2 * (i + 1))

            bo = rowsA[:, 1 if l == 0 else 0, :]

            def v_done(blk, u, first):
                return u + 1 if first else blk * 6 + (u - 1)

            def wo_done(blk, u):
                return blk * 6 + (3 + 4 * u) - (2 if isinstance(blk, int) and blk == NB - 1 and u else 0)

            def norm_done(blk, u):
                return wo_done(blk, u) + 1

            def where(st):
                return st // 8, st // 4 % 2, st % 4

            def keys(qt):
                return P if causal_l and qt == 0 else SEQ

            with nc.Block() as block:
                @block.sync
                def _(sp):
                    sync_tail(sp)

                @block.gpsimd
                def _(pool):
                    if l == 1:
                        for i in range(3):
                            for m in range(KD):
                                ins = pool.tensor_tensor(attw[:, slot, i, m, m * P:(m + 1) * P].rearrange("p (j c) -> p j c", c=HD),
                                                         rep[:, i, :].unsqueeze(1).broadcast_to([P, GH, HD]),
                                                         hmask[:, :].unsqueeze(2).broadcast_to([P, GH, HD]), ALU.mult)
                        ins.then_inc(wbd, 1)
                    def body(blk, first, last):
                        for st in range(STEPS):
                            u, g, p = where(st)
                            if st in (0, 4):
                                pool.wait_ge(qk_lo, blk * 4 + (1 + g))
                            if u:
                                pool.wait_ge(s_full, tile_full(blk, 2 * (st - 8) + 1))
                            pool.tensor_tensor(km_hi[:, g, 2 * p:2 * p + 2], k_hi[:, g, u * SEQ:(u + 1) * SEQ].unsqueeze(1).broadcast_to([P, 2, SEQ]),
                                               hmask[:, 2 * p:2 * p + 2].unsqueeze(2).broadcast_to([P, 2, SEQ]), ALU.mult).then_inc(km_in, 1)
                            if st == 7:
                                x4 = x_tok[:, ds(blk * 4, 4), :]
                                if not first:
                                    nrm.power(pool, blk - 1, 1)
                                if not last:
                                    pool.wait_ge(v_in, blk * 2 + 2)
                                    pool.tensor_copy(stage[:, :, :], ctxT[:, :, ds(blk * BLK + BLK, BLK)]).then_inc(staged, 1)
                                pool.tensor_tensor(x4, x4, bo.unsqueeze(1).broadcast_to([P, 4, D]), ALU.add).then_inc(pre, 1)
                        nrm.power(pool, blk, 0)

                    pool.tensor_copy(stage[:, :, :], ctxT[:, :, 0:BLK]).then_inc(staged, 1)
                    pool.wait_ge(scaled, 1)
                    body(0, True, False)
                    with pool.Fori(1, NB - 1) as blk:
                        body(blk, False, False)
                    body(NB - 1, False, True)
                    nrm.power(pool, NB - 1, 1)

                @block.scalar
                def _(act):
                    def exps(blk, st):
                        for qt in range(2):
                            i = 2 * st + qt
                            kk = keys(qt)
                            act.wait_ge(maxed, blk * 32 + (2 * st + qt + 1))
                            if qt == 0:
                                wait(act, turned_s, blk * 32 + max(0, 2 * st - 2))
                            for hh in range(2):
                                ins = act.activation(prob[:, st % 2, qt, hh, 0:kk], ps[:, i % 4, hh * SEQ:hh * SEQ + kk], ACT.Exp,
                                                     bias=negmax[:, st % 2, qt, hh:hh + 1], accum_out=rowsum[:, st % 2, qt, hh:hh + 1])
                                ins.then_inc(s_read, 1)

                    def turned(blk, st):
                        act.wait_ge(turned_s, blk * 32 + (2 * st + 1))
                        wait(act, av, blk * STEPS + max(0, st - 1))
                        s = (2 * st) % 4
                        if causal_l:
                            act.activation(probT[:, s, 0, :], ps[:, 4, 0:SEQ], ACT.Identity)
                            act.activation(probT[:, s, 1, P:], ps[:, 4, SEQ + P:], ACT.Identity).then_inc(pt_in[0], 1)
                        else:
                            act.activation(probT[:, s].rearrange("p a b -> p (a b)"), ps[:, 4, :], ACT.Identity).then_inc(pt_in[0], 1)

                    def keys_lo(blk, st):
                        u, g, p = where(st)
                        for h in (2 * p, 2 * p + 1):
                            ins = act.activation(km_lo[:, g, h, :], k_lo[:, g, u * SEQ:(u + 1) * SEQ], ACT.Identity, scale=hmask[:, h:h + 1])
                        ins.then_inc(km_lo_in, 1)

                    def context(blk, i, first):
                        act.wait_ge(av, blk * STEPS + 4 * (i + 1))
                        if i >= 2:
                            act.wait_ge(a_full, wo_done(blk, 0))
                        elif not first:
                            act.wait_ge(a_full, wo_done(blk - 1, 1))
                        act.activation(oT[:, i % 2, :], ps[:, 6, 0:SEQ], ACT.Identity).then_inc(o_in, 1)

                    def norm_T(blk, u):
                        act.wait_ge(a_full, norm_done(blk, u))
                        store_T(act, xnT, 7, blk, u).then_inc(xT_in, 1)

                    def body(blk, first):
                        for j in range(4):
                            m = j % 2
                            act.wait_ge(s_full, blk * SF + (j + 1))
                            if j >= 2:
                                bias = qbias[:, m:m + 1] if l == 0 else 0.0
                                act.activation(qT[:, m, :], ps[:, j, :], ACT.Identity, bias=bias, scale=scale).then_inc(s_read, 1)
                            else:
                                wait(act, km_in, blk * STEPS)
                                bias = col("L0_bk", m) if l == 0 else 0.0
                                act.activation(kT[:, m, :], ps[:, j, :], ACT.Identity, bias=bias).then_inc(s_read, 1)
                            act.wait_ge(s_read, blk * SR + (j + 1))
                            act.activation((k_hi, q_hi)[j // 2][:, m, :], (kT, qT)[j // 2][:, m, :], ACT.Identity).then_inc(qk_hi, 1)
                        act.wait_ge(qk_lo, blk * 4 + 2)
                        for st in range(AHEAD):
                            keys_lo(blk, st)
                        exps(blk, 0)
                        for st in range(STEPS):
                            if st + AHEAD < STEPS:
                                keys_lo(blk, st + AHEAD)
                            if st + 1 < STEPS:
                                exps(blk, st + 1)
                            if st and st % 4 == 0:
                                context(blk, st // 4 - 1, first)
                            turned(blk, st)
                            if st == 5 and not first:
                                norm_T(blk - 1, 1)
                            if st == 14:
                                norm_T(blk, 0)
                        context(blk, 3, first)

                    blocks(act, body, lambda blk: norm_T(blk, 1))

                @block.vector
                def _(dve):
                    def maxima(blk, st):
                        for qt in range(2):
                            i = 2 * st + qt
                            kk = keys(qt)
                            dve.wait_ge(s_full, tile_full(blk, i))
                            dve.tensor_reduce(negmax[:, st % 2, qt, :], ps[:, i % 4, :].rearrange("p (h s) -> p h s", h=2)[:, :, 0:kk],
                                              AXX, ALU.max, negate=True).then_inc(maxed, 1)

                    def normalise(blk, st):
                        for qt in range(2):
                            kk = keys(qt)
                            dve.wait_ge(s_read, tile_read(blk, 2 * st + qt))
                            dve.reciprocal(rinv[:, st % 2, qt, :], rowsum[:, st % 2, qt, :]).then_inc(inv, 1)
                            dve.wait_ge(inv, blk * 32 + 2 * st + qt + 1)
                            for hh in range(2):
                                p = prob[:, st % 2, qt, hh, 0:kk]
                                ins = dve.tensor_scalar(p, p, rinv[:, st % 2, qt, hh:hh + 1], None, ALU.mult)
                            ins.then_inc(normed, 1)

                    def turned(blk, st):
                        dve.wait_ge(turned_s, blk * 32 + (2 * st + 2))
                        wait(dve, av, blk * STEPS + max(0, st - 1))
                        s = (2 * st + 1) % 4
                        if causal_l:
                            dve.tensor_copy(probT[:, s, 0, :], ps[:, 5, 0:SEQ])
                            dve.tensor_copy(probT[:, s, 1, P:], ps[:, 5, SEQ + P:]).then_inc(pt_in[1], 1)
                        else:
                            dve.tensor_copy(probT[:, s].rearrange("p a b -> p (a b)"), ps[:, 5, :]).then_inc(pt_in[1], 1)

                    def values(blk, u, first):
                        dve.wait_ge(a_full, v_done(blk, u, first))
                        for t in range(2):
                            whole = vm[u][:, t].rearrange("p h c -> p (h c)")
                            for g in range(2):
                                o = g * GH * P
                                dst = whole[:, o:o + GH * P].rearrange("p (j c) -> p j c", c=P)
                                dst = bass.AP(dst.tensor, dst.offset, [dst.ap[0], [P + HD, GH], [1, HD]])
                                src = ps[:, 7, t * SEQ + g * P:t * SEQ + (g + 1) * P].rearrange("p (j c) -> p j c", c=HD)
                                if l == 0:
                                    row = rowsA[:, 0, g * P:(g + 1) * P].rearrange("p (j c) -> p j c", c=HD)
                                    ins = dve.tensor_tensor(dst, src, row, ALU.add)
                                else:
                                    ins = dve.tensor_copy(dst, src)
                        ins.then_inc(v_in, 1)

                    def update(blk, u):
                        dve.wait_ge(pre, blk + 1)
                        dve.wait_ge(a_full, wo_done(blk, u))
                        xp = x_pair(blk, u)
                        for t in range(2):
                            ins = dve.scalar_tensor_tensor(xp(t)[:, 0, :], ps[:, 7, t * D:(t + 1) * D], gate(l), xp(t)[:, 0, :],
                                                           ALU.mult, ALU.add)
                        ins.then_inc(wo_in, 1)

                    def sums(blk, u):
                        dve.wait_ge(wo_in, blk * 2 + (u + 1))
                        nrm.sums(dve, x_pair(blk, u))

                    def result(blk, u, first):
                        if u == 1:
                            dve.wait_ge(a_full, norm_done(blk, 0))
                        elif not first:
                            dve.wait_ge(a_full, norm_done(blk - 1, 1))
                        nrm.result(dve, blk, u, lambda t: xs[:, t, :], x_pair(blk, u))

                    dve.wait_ge(ld_rowsA, 16 * (l + 1))
                    dve.tensor_scalar(bo, bo, gate(l), None, ALU.mult).then_inc(scaled, 1)
                    def body(blk, first):
                        for j in range(4):
                            dve.wait_ge(qk_hi, blk * 4 + (j + 1))
                            dve.tensor_tensor((k_lo, q_lo)[j // 2][:, j % 2, :], (kT, qT)[j // 2][:, j % 2, :],
                                              (k_hi, q_hi)[j // 2][:, j % 2, :], ALU.subtract).then_inc(qk_lo, 1)
                        values(blk, 0, first)
                        maxima(blk, 0)
                        for st in range(STEPS):
                            if st == 0:
                                values(blk, 1, first)
                            normalise(blk, st)
                            if st + 1 < STEPS:
                                maxima(blk, st + 1)
                            turned(blk, st)
                            if not first:
                                if st == 1:
                                    update(blk - 1, 1)
                                if st == 2:
                                    sums(blk - 1, 1)
                                if st == 3:
                                    nrm.moments(dve, blk - 1, 1)
                                if st == 4:
                                    result(blk - 1, 1, False)
                            if st == 10:
                                update(blk, 0)
                            if st == 11:
                                sums(blk, 0)
                            if st == 12:
                                nrm.moments(dve, blk, 0)
                            if st == 13:
                                result(blk, 0, first)

                    def tail(blk):
                        update(blk, 1)
                        sums(blk, 1)
                        nrm.moments(dve, blk, 1)
                        result(blk, 1, False)

                    blocks(dve, body, tail)

                @block.tensor
                def _(pe):
                    def scores(blk, st):
                        u, g, p = where(st)
                        for qt in range(2):
                            i = 2 * st + qt
                            kk = keys(qt)
                            if qt == 0:
                                pe.wait_ge(km_in, blk * STEPS + (st + 1))
                                pe.wait_ge(km_lo_in, blk * STEPS + (st + 1))
                            pe.wait_ge(s_read, blk * SR + 4 if i < 4 else tile_read(blk, i - 4))
                            bank = ps[:, i % 4, :].rearrange("p (h s) -> p h s", h=2)
                            if st == 0 and qt == 0:
                                pe.wait_ge(qk_lo, blk * 4 + 4)
                            q = slice(u * SEQ + qt * P, u * SEQ + (qt + 1) * P)
                            for i3, (qq, kk3) in enumerate(((q_hi, km_hi), (q_hi, km_lo), (q_lo, km_hi))):
                                ins = pe.matmul(bank[:, :, 0:kk], qq[:, g, q], kk3[:, g, 2 * p:2 * p + 2, 0:kk],
                                                start=(i3 == 0), stop=(i3 == 2 and not causal_l))
                            if causal_l:
                                ins = pe.matmul(bank[:, :, qt * P:(qt + 1) * P], identb[:, :],
                                                causal[:, :].unsqueeze(1).broadcast_to([P, 2, P]), start=False, stop=True)
                            ins.then_inc(s_full, 1)

                    def turn(blk, st):
                        for hh in range(2):
                            wait(pe, pt_in[hh], blk * STEPS + st)
                            if hh == 0:
                                pe.wait_ge(normed, blk * 32 + (2 * st + 2))
                            for kt in range(2):
                                for qt in range(2):
                                    if causal_l and kt > qt:
                                        continue
                                    o = kt * SEQ + qt * P
                                    ins = pe.transpose(ps[:, 4 + hh, o:o + P], prob[:, st % 2, qt, hh, kt * P:(kt + 1) * P], ident[:, :])
                            ins.then_inc(turned_s, 1)

                    def attend(blk, st):
                        u, g, p = where(st)
                        if p == 0:
                            wait(pe, o_in, blk * 4 + (2 * u + g))
                            if g == 0:
                                pe.wait_ge(v_in, blk * 2 + (u + 1))
                        for hh in range(2):
                            pe.wait_ge(pt_in[hh], blk * STEPS + (st + 1))
                            for kt in range(2):
                                q0 = P if causal_l and kt == 1 else 0
                                ins = pe.matmul(ps[:, 6, q0:SEQ], vm[u][:, kt, g * GH + 2 * p + hh, :],
                                                probT[:, (2 * st + hh) % 4, kt, q0:], start=(p == 0 and hh == 0 and kt == 0),
                                                stop=(p == 3 and hh == 1 and kt == 1))
                        ins.then_inc(av, 1)

                    def project_out(blk, u, before, count):
                        pe.wait_ge(before, count)
                        pe.wait_ge(o_in, blk * 4 + (2 * u + 2))
                        for t in range(2):
                            for g in range(2):
                                ins = pe.matmul(ps[:, 7, t * D:(t + 1) * D], oT[:, g, t * P:(t + 1) * P], wo[:, g, :],
                                                start=(g == 0), stop=(g == 1))
                        ins.then_inc(a_full, 1)

                    def norm_T(blk, u):
                        pe.wait_ge(nrm.link, nrm.done(blk, u))
                        transpose_pair(pe, 7, xs).then_inc(a_full, 1)

                    pe.wait_ge(ld_att[slot], 16)
                    if l == 1:
                        pe.wait_ge(wbd, 1)
                    def body(blk, first):
                        for j in range(4):
                            m = j % 2
                            w, src = (wk, ctxT) if j < 2 else (wq, xnT)
                            for k in parts(m):
                                ins = pe.matmul(ps[:, j, :], w[:, k, m * P:(m + 1) * P], src[:, k, ds(blk * BLK, BLK)],
                                                start=(k == parts(m)[0]), stop=(k == parts(m)[-1]))
                            ins.then_inc(s_full, 1)
                        pe.wait_ge(staged, blk + 1)
                        for u in range(2):
                            if u:
                                pe.wait_ge(v_in, blk * 2 + 1)
                            elif not first:
                                pe.wait_ge(xT_in, blk * 2 - 1)
                            for t in range(2):
                                lhs = [stage[:, k, (2 * u + t) * P:(2 * u + t + 1) * P] for k in range(KD)]
                                if l == 0:
                                    for k in range(KD):
                                        ins = pe.matmul(ps[:, 7, t * D:(t + 1) * D], lhs[k], wv[:, k, :], start=(k == 0), stop=(k == KD - 1))
                                else:
                                    for k in range(KD):
                                        ins = pe.matmul(ps[:, 7, t * D + k * P:t * D + (k + 1) * P], lhs[k], wv[:, k, k * P:(k + 1) * P],
                                                        start=True, stop=True)
                            ins.then_inc(a_full, 1)
                            if u == 0:
                                scores(blk, 0)
                        for st in range(STEPS):
                            if st + 1 < STEPS:
                                scores(blk, st + 1)
                            if st:
                                attend(blk, st - 1)
                            turn(blk, st)
                            if not first:
                                if st == 1:
                                    project_out(blk - 1, 1, v_in, blk * 2 + 2)
                                if st == 5:
                                    norm_T(blk - 1, 1)
                            if st == 10:
                                project_out(blk, 0, *((v_in, 2) if first else (xT_in, blk * 2)))
                            if st == 14:
                                norm_T(blk, 0)
                        attend(blk, STEPS - 1)

                    def tail(blk):
                        project_out(blk, 1, xT_in, blk * 2 + 1)
                        norm_T(blk, 1)

                    blocks(pe, body, tail)

        def phase_experts(l, func, gi, keep, prefetch):
            n = f"L{l}f_"
            shared = l == 0
            n_exp = E0 - 1 if l == 0 else E1
            n_ch = 2 if l == 0 else 1
            steps = STEPS_OF[l]
            pairs = steps // 2
            go = 0 if l == 0 else E0 - 1
            lead = 2 if shared else 0
            RING = (1, 2)
            h_full = psem(n + "h_full")
            h_in = psem(n + "h_in")
            s_full = psem(n + "s_full")
            s_in = psem(n + "s_in")
            y_full = [psem(n + f"y_full{v}") for v in range(2)]
            y_out = [psem(n + f"y_out{v}") for v in range(2)]
            y_st = [psem(n + f"y_st{v}") for v in range(2)]
            g_full = psem(n + "g_full")
            g_hi = psem(n + "g_hi")
            g_lo = psem(n + "g_lo")
            ld_w1 = [psem(n + f"ld_w1{v}") for v in range(2)]
            ld_w2 = [psem(n + f"ld_w2{v}") for v in range(2)]
            w_hi = [psem(n + f"w_hi{v}") for v in range(2)]
            w_lo = [psem(n + f"w_lo{v}") for v in range(2)]
            hid_hi = psem(n + "hid_hi")
            hid_lo = psem(n + "hid_lo")
            routed = psem(n + "routed")
            counted = psem(n + "counted")
            n_full = psem(n + "n_full")
            xT_in = psem(n + "xT_in")
            r_full = psem(n + "r_full")
            r_in = psem(n + "r_in")
            link = psem(n + "link")
            expw = psem(n + "expw")
            cst = psem(n + "cst")
            sent = psem(n + "sent")
            ld_b = [psem(n + f"ld_b{v}") for v in range(2)]
            ld_g = [psem(n + f"ld_g{v}") for v in range(2)]
            got = [psem(n + f"got{v}") for v in range(2)]
            added = psem(n + "added")
            sadd = psem(n + "sadd")
            nrm = Norm(n + "norm", 1, 4)
            t_full = psem(n + "t_full")
            t_in = psem(n + "t_in")
            t_bias = psem(n + "t_bias")
            kv_full = psem(n + "kv_full")
            kv_in = psem(n + "kv_in")
            keys = hbuf[:, :].rearrange("p (t d) -> p t d", t=NT)
            values = [prob[:, :, :, :, :].rearrange("p a b c s -> p (a b c) s"), probT[:, :, :, :].rearrange("p a b s -> p (a b) s")]

            upper, ones = oT[:, 0, 0:P], oT[:, 0, P:2 * P]
            stepno = dec[:, :, :, :].rearrange("p a b c -> p (a b c)")[:, 0:steps]
            x_rows = vbuf[:, :].rearrange("p (t d) -> p t d", t=NT)
            xg_sb = [qT[:, v, :].rearrange("p (t d) -> p t d", t=2) for v in range(2)]
            xg_hi, xg_lo = (kT_r[:, i * BLK:(i + 1) * BLK].rearrange("p (k t) -> p k t", k=KD) for i in range(2))
            hs = hbuf[:, 0:NF * SUB].rearrange("p (f t) -> p f t", f=NF)
            hs_lo = hbuf_r[:, 0:NF * SUB].rearrange("p (f t) -> p f t", f=NF)
            hs_hi = prob_r.rearrange("p (f t) -> p f t", f=NF)
            HALF = KD * F
            high = [(vbuf_r[:, 0:HALF], vbuf_r[:, HALF:]),
                    (hbuf_r[:, HALF:], attw_r) if l == 0 else (wbuf_r[0][:, 0:HALF], wbuf_r[0][:, HALF:])]
            low = [(wbuf_r[RING[v]][:, 0:HALF], wbuf_r[RING[v]][:, HALF:]) for v in range(2)]
            whole = [(wbuf[:, RING[v], 0:HALF], wbuf[:, RING[v], HALF:]) for v in range(2)]

            def first_m(part, v):
                return part[v][0].rearrange("p (k f) -> p k f", k=KD)

            def second_m(part, v):
                return part[v][1].rearrange("p (f d) -> p f d", f=NF)

            def quarter(part, v, j):
                return part[v][j // 2][:, j % 2 * HALF // 2:(j % 2 + 1) * HALF // 2]
            y_sb = [probT[:, v] for v in range(2)]
            b2_sb = ts
            xs4 = qT[:, :, :].rearrange("p k t -> p (k t)").rearrange("p (t d) -> p t d", t=4)

            def normalised(blk, t):
                return xn_tok[:, blk * 4 + t, :] if keep else xs4[:, t, :]
            gat = [prob[:, :, :, :, :].rearrange("p a b c s -> p (a b c) s"), probT[:, :, :, :].rearrange("p a b s -> p (a b) s")]

            def ring(eng, step):
                with eng.Fori(0, pairs) as i:
                    for v in range(2):
                        step(i * 2 + v, v, i, False)
                step(steps - 1, 0, pairs, True)

            with nc.Block() as block:
                @block.vector
                def _(dve):
                    count = [0]

                    def step(ins):
                        count[0] += 1
                        ins.then_inc(link, 1)
                        dve.wait_ge(link, count[0])

                    def wide(i):
                        return rt[:, i, :, 0:n_exp]

                    def over(v):
                        return v.unsqueeze(2).broadcast_to([P, NT, n_exp])

                    def over_t(v):
                        return v.unsqueeze(1).broadcast_to([P, NT, n_exp])

                    lg = logit[:, :, 0:n_exp]
                    order = rank[:, 0:n_exp].unsqueeze(1).broadcast_to([P, NT, n_exp])

                    def one_hot(src, mx, dst):
                        step(dve.tensor_reduce(mx, src, AXX, ALU.max))
                        step(dve.tensor_tensor(dst, src, over(mx), ALU.is_equal))
                        step(dve.tensor_tensor(dst, dst, order, ALU.mult))
                        step(dve.tensor_reduce(r1[:, 7, :], dst, AXX, ALU.max))
                        step(dve.tensor_tensor(dst, dst, over(r1[:, 7, :]), ALU.is_equal))

                    if shared:
                        dve.wait_ge(ld_rowsF, 16)
                        dve.wait_ge(zeroed, 64)
                    dve.wait_ge(routed, 1)
                    raw = ps[:, 7, 0:NT * n_exp].rearrange("p (t e) -> p t e", e=n_exp)
                    if l == 0:
                        step(dve.tensor_copy(lg, raw))
                        one_hot(lg, r1[:, 0, :], wide(0))
                        step(dve.scalar_tensor_tensor(wide(1).rearrange("p t e -> p (t e)"), wide(0).rearrange("p t e -> p (t e)"), -BIG,
                                                      lg.rearrange("p t e -> p (t e)"), ALU.mult, ALU.add))
                        one_hot(wide(1), r1[:, 1, :], wide(2))
                        step(dve.tensor_tensor(r1[:, 4, :], r1[:, 1, :], r1[:, 0, :], ALU.subtract))
                        assert count[0] == EXP_LINK
                        step(dve.tensor_tensor(rs(0, n_exp), wide(0), wide(2), ALU.add))
                    else:
                        bg = small[:, 0:E1].unsqueeze(1).broadcast_to([P, NT, E1])
                        step(dve.tensor_tensor(lg, raw, bg, ALU.add))
                        one_hot(lg, r1[:, 0, :], wide(0))
                        step(dve.tensor_copy(rs(0, n_exp), wide(0)))
                    assert count[0] == CHOSEN_LINK[l]
                    dve.wait_ge(counted, 1)
                    before = ps[:, 7, P:P + NT * n_exp].rearrange("p (t e) -> p t e", e=n_exp)
                    total = ps[:, 7, 2 * P:2 * P + NT * n_exp].rearrange("p (t e) -> p t e", e=n_exp)
                    step(dve.tensor_copy(rs(1, n_exp), total))
                    src, dst, sh = rs(1, n_exp), rs(2, n_exp), 1
                    while sh < NT:
                        dve.tensor_copy(dst[:, 0:sh, :], src[:, 0:sh, :])
                        step(dve.tensor_tensor(dst[:, sh:, :], src[:, sh:, :], src[:, 0:NT - sh, :], ALU.add))
                        src, dst, sh = dst, src, 2 * sh
                    step(dve.tensor_tensor(dst, src, total, ALU.subtract))
                    step(dve.tensor_tensor(dst, dst, before, ALU.add))
                    place = dst
                    q, ne = ew[:, 0, 0:n_exp], ew[:, 1, 0:n_exp]
                    step(dve.tensor_scalar(q, src[:, NT - 1, :], 1.0 / SUB, 1.0, ALU.mult, ALU.add))
                    below = rs(3, 8)[:, 0:n_exp, :]
                    step(dve.tensor_tensor(below, q.unsqueeze(2).broadcast_to([P, n_exp, 8]),
                                           rank[:, :].unsqueeze(1).broadcast_to([P, n_exp, 8]), ALU.is_gt))
                    step(dve.tensor_reduce(ne, below, AXX, ALU.add))
                    src, dst, other, sh = ne, ew[:, 2, 0:n_exp], ew[:, 3, 0:n_exp], 1
                    while sh < n_exp:
                        dve.tensor_copy(dst[:, 0:sh], src[:, 0:sh])
                        step(dve.tensor_tensor(dst[:, sh:], src[:, sh:], src[:, 0:n_exp - sh], ALU.add))
                        src, dst, other, sh = dst, other, dst, 2 * sh
                    dve.wait_ge(cst, 3)
                    full = path[:, :, :, :, :].rearrange("p a b c d -> p (a b c d)")[:, 0:steps * n_exp].rearrange("p (s e) -> p s e", e=n_exp)
                    step(dve.tensor_tensor(full, src.unsqueeze(1).broadcast_to([P, steps, n_exp]),
                                           stepno.unsqueeze(2).broadcast_to([P, steps, n_exp]), ALU.is_le))
                    et = rs(3, 8).rearrange("p t e -> p (t e)")[:, 0:steps]
                    step(dve.tensor_reduce(et, full, AXX, ALU.add))
                    step(dve.tensor_scalar(step_exp[:, 0:steps], et, float(n_exp - 1), None, ALU.min))
                    assert count[0] == EXPERT_LINK[l], count[0]
                    step(dve.tensor_tensor(q, src, ne, ALU.subtract))
                    step(dve.tensor_scalar(q, q, float(SUB), None, ALU.mult))
                    step(dve.tensor_tensor(place, place, over_t(q), ALU.add))
                    for c in range(n_ch):
                        step(dve.tensor_tensor(rs(3, n_exp), wide(2 * c), place, ALU.mult))
                        step(dve.tensor_reduce(r1[:, 0, :], rs(3, n_exp), AXX, ALU.add))
                        step(dve.tensor_copy(rowno[:, c, :], r1[:, 0, :]))
                    assert count[0] == PLACED_LINK[l], count[0]
                    if l == 0:
                        dve.wait_ge(expw, 1)
                        step(dve.tensor_scalar(r1[:, 6, :], r1[:, 5, :], 1.0, None, ALU.add))
                        step(dve.reciprocal(r1[:, 2, :], r1[:, 6, :]))
                        step(dve.tensor_scalar(r1[:, 2, :], r1[:, 2, :], gate(gi), None, ALU.mult))
                        step(dve.tensor_tensor(r1[:, 3, :], r1[:, 5, :], r1[:, 2, :], ALU.mult))

                    def shared_block(blk):
                        for tp in range(2):
                            dve.wait_ge(s_full, blk * 2 + (tp + 1))
                            xp = x_pair(blk, tp)
                            for t in range(2):
                                x = xp(t)[:, 0, :]
                                ins = dve.scalar_tensor_tensor(x, ps[:, 4 + tp, t * D:(t + 1) * D], gate(gi), x, ALU.mult, ALU.add)
                            ins.then_inc(s_in, 1)
                            dve.wait_ge(s_in, blk * 2 + (tp + 1))
                            for t in range(2):
                                x = xp(t)[:, 0, :]
                                ins = dve.scalar_tensor_tensor(x, rowsF[:, 0, :], gate(gi), x, ALU.mult, ALU.add)
                            ins.then_inc(sadd, 1)

                    def key_value_bias(blk):
                        dve.wait_ge(t_in, blk * 4 + 4)
                        for i, x in enumerate((keys[:, blk * 4:blk * 4 + 4, :], values[blk // 2][:, blk % 2 * 4:blk % 2 * 4 + 4, :])):
                            dve.tensor_tensor(x, x, rowsA[:, i, :].unsqueeze(1).broadcast_to([P, 4, D]), ALU.add).then_inc(t_bias, 1)

                    def weights_lo(v, k, j):
                        dve.wait_ge(w_hi[v], k * 4 + (j + 1))
                        dve.tensor_tensor(quarter(low, v, j), quarter(whole, v, j), quarter(high, v, j), ALU.subtract).then_inc(w_lo[v], 1)

                    def rows_lo(s):
                        dve.wait_ge(g_hi, s + 1)
                        dve.tensor_tensor(xg_lo, ps[:, 6, :].rearrange("p (k t) -> p k t", k=KD), xg_hi, ALU.subtract).then_inc(g_lo, 1)

                    def ring_step(s, v, k, last):
                        nv, nk = 1 - v, k + v
                        for j in range(NF // 2):
                            dve.wait_ge(hid_hi, s * 4 + (j + 1))
                            f = slice(2 * j, 2 * j + 2)
                            dve.tensor_tensor(hs_lo[:, f, :], hs[:, f, :], hs_hi[:, f, :], ALU.subtract).then_inc(hid_lo, 1)
                            if not last and j < 2:
                                weights_lo(nv, nk, j)
                        if not last:
                            rows_lo(s + 1)
                            for j in range(2, 4):
                                weights_lo(nv, nk, j)
                        dve.wait_ge(y_full[v], k + 1)
                        dve.wait_ge(y_st[v], k * 16)
                        dve.wait_ge(ld_b[v], k * 32 + 32)
                        dve.tensor_tensor(y_sb[v], ps[:, 4 + v, :].rearrange("p (t d) -> p t d", t=2),
                                          b2_sb[:, v, :].unsqueeze(1).broadcast_to([P, 2, D]), ALU.add).then_inc(y_out[v], 1)

                    def combine(blk):
                        v = blk % 2
                        dve.wait_ge(got[v], 64 * n_ch * (blk // 2 + 1))
                        for c in range(n_ch):
                            for t in range(4):
                                i = blk * 4 + t
                                w = r1[:, 2 + c, i:i + 1] if l == 0 else gate(gi)
                                ins = dve.scalar_tensor_tensor(x_tok[:, i, :], gat[v][:, c * 4 + t, :], w, x_tok[:, i, :], ALU.mult, ALU.add)
                            ins.then_inc(added, 1)
                            dve.wait_ge(added, blk * n_ch + c + 1)

                    def norms(blk):
                        if shared and blk >= lead:
                            dve.wait_ge(sadd, blk * 2 + 2)
                        xp = x_tile(blk)
                        nrm.statistics(dve, blk, 0, xp)
                        if not keep:
                            wait(dve, n_full, blk * 2)
                        nrm.result(dve, blk, 0, lambda t: normalised(blk, t), xp)

                    if shared:
                        with dve.Fori(0, lead - 1) as j:
                            shared_block(j)
                    else:
                        dve.wait_ge(ld_rowsA, 48)
                        for blk in range(NB):
                            key_value_bias(blk)
                    for j in range(4):
                        weights_lo(0, 0, j)
                    if shared:
                        shared_block(lead - 1)
                    rows_lo(0)
                    ring(dve, ring_step)
                    if shared:
                        dve.wait_ge(sadd, 2 * lead)
                    for blk in range(NB):
                        combine(blk)
                        if shared and blk == NB - 1:
                            shared_block(NB - 1)
                        norms(blk)
                        if shared and blk == 1:
                            shared_block(2)
                            dve.wait_ge(sadd, 6)

                @block.sync
                def _(sp):
                    prefetch(sp)
                    w1_all, w2_all, b1_all, b2_all = (a[f"L{l}_{w}"] for w in ("w1", "w2", "b1r", "b2"))

                    def load_first(s, v):
                        e = sp.value_load(step_exp[0:1, ds(s, 1)], min_val=0, max_val=n_exp - 1)
                        if not isinstance(s, int) or s >= 2:
                            sp.wait_ge(h_full, (s - 1 + lead) * NF)
                        sp.dma_start(w1[RING[v]], w1_all[ds(e, 1)].rearrange("e (k p) f -> p (e k) f", p=P)).then_inc(ld_w1[v], 16)
                        return e

                    def load_second(e, v):
                        sp.dma_start(w2[RING[v]], w2_all[ds(e, 1)].rearrange("e (f p) d -> p (e f) d", p=P)).then_inc(ld_w2[v], 16)
                        sp.dma_start(b1_sb[:, v, :], b1_all[ds(e, 1)].rearrange("e p f -> (e p) f")).then_inc(ld_b[v], 16)
                        sp.dma_start(b2_sb[:, v, :], b2_all[ds(e, 1)].broadcast_to([P, D])).then_inc(ld_b[v], 16)

                    def load_rows_of(s, v):
                        sp.dma_start(xg_sb[v], a["xg"][ds(s * SUB, SUB)].rearrange("(t p) d -> p t d", p=P)).then_inc(ld_g[v], 16)

                    def store(s, v, k):
                        sp.wait_ge(y_out[v], k + 1)
                        sp.dma_start(a["yg"][ds(s * SUB, SUB)].rearrange("(t p) d -> p t d", p=P), y_sb[v]).then_inc(y_st[v], 16)

                    sp.wait_ge(link, EXPERT_LINK[l])
                    for v in range(2):
                        load_second(load_first(v, v), v)
                    sp.wait_ge(sent, n_ch * NT * 16)
                    for v in range(2):
                        load_rows_of(v, v)
                    sp.wait_ge(g_full, 1)
                    load_rows_of(2, 0)
                    with sp.Fori(0, pairs - 1) as i:
                        for v in range(2):
                            s = i * 2 + v
                            e = load_first(s + 2, v)
                            store(s, v, i)
                            load_second(e, v)
                            sp.wait_ge(g_full, s + 2)
                            load_rows_of(s + 3, 1 - v)
                    e = load_first(steps - 1, 0)
                    store(steps - 3, 0, pairs - 1)
                    load_second(e, 0)
                    store(steps - 2, 1, pairs - 1)
                    store(steps - 1, 0, pairs)

                @block.gpsimd
                def _(pool):
                    pool.memset(ones, 1.0).then_inc(cst, 1)
                    pool.wait_ge(cst, 1)
                    pool.affine_select(out=upper, in_=ones, pattern=[[1, P]], compare_op=ALU.is_gt, fill=0.0,
                                       base=0, channel_multiplier=-1).then_inc(cst, 1)
                    pool.iota(stepno, pattern=[[1, steps]], base=0, channel_multiplier=0, allow_small_or_imprecise_dtypes=True).then_inc(cst, 1)
                    pool.wait_ge(zeroed, 64)
                    pool.wait_ge(link, PLACED_LINK[l])
                    pool.wait_ge(r_in, NT // 2)
                    for t in range(NT):
                        for c in range(n_ch):
                            pool.indirect_dma_start(a["xg"], bass.IndirectOffsetOnAxis(rowno[:, c, t:t + 1], 0),
                                                    x_rows[:, t, :], None).then_inc(sent, 16)
                    def ring_step(s, v, k, last):
                        for j in range(NF // 2):
                            pool.wait_ge(h_in, (s + lead) * NF + (2 * j + 2))
                            f = slice(2 * j, 2 * j + 2)
                            pool.tensor_tensor(hs_hi[:, f, :], hs[:, f, :], ones[:, 0:1].unsqueeze(2).broadcast_to([P, 2, SUB]), ALU.mult).then_inc(hid_hi, 1)

                    ring(pool, ring_step)
                    pool.wait_ge(y_st[0], 16 * (pairs + 1))
                    pool.wait_ge(y_st[1], 16 * pairs)

                    def gather(blk):
                        v = blk % 2
                        wait(pool, added, n_ch * max(0, blk - 1))
                        for c in range(n_ch):
                            for t in range(4):
                                pool.indirect_dma_start(gat[v][:, c * 4 + t, :], None, a["yg"],
                                                        bass.IndirectOffsetOnAxis(rowno[:, c, blk * 4 + t:blk * 4 + t + 1], 0)).then_inc(got[v], 16)

                    gather(0)
                    for blk in range(NB):
                        if blk + 1 < NB:
                            gather(blk + 1)
                        if shared and blk == NB - 1:
                            pool.memset(vbuf[:, :], 0.0)
                            pool.memset(wbuf[:, 2, :], 0.0)
                        nrm.power(pool, blk, 0)

                @block.scalar
                def _(act):
                    for j in range(NT // 2):
                        act.wait_ge(r_full, j + 1)
                        act.activation(x_rows[:, 2 * j:2 * j + 2, :], ps[:, j % 4, :].rearrange("p (t d) -> p t d", t=2),
                                       ACT.Identity).then_inc(r_in, 1)
                    if l == 0:
                        act.wait_ge(link, EXP_LINK)
                        act.activation(r1[:, 5, :], r1[:, 4, :], ACT.Exp).then_inc(expw, 1)

                    def shared_block(u):
                        for f in range(NF):
                            act.wait_ge(h_full, u * NF + (f + 1))
                            act.activation(hT[:, f, :], ps[:, f % 4, :], func, bias=col("L0_bs1", f)).then_inc(h_in, 1)

                    def key_value(e):
                        for i, x in enumerate((keys[:, 2 * e:2 * e + 2, :], values[e // 4][:, e % 4 * 2:e % 4 * 2 + 2, :])):
                            act.wait_ge(t_full, 2 * e + i + 1)
                            act.activation(x, ps[:, (2 * e + i) % 4, :].rearrange("p (t d) -> p t d", t=2), ACT.Identity).then_inc(t_in, 1)

                    def product(blk):
                        act.wait_ge(kv_full, blk + 1)
                        act.activation(kv_all[:, blk, :], ps[:, 4 + blk % 2, :], ACT.Identity).then_inc(kv_in, 1)

                    def rows_hi(s):
                        act.wait_ge(g_full, s + 1)
                        act.activation(xg_hi, ps[:, 6, :].rearrange("p (k t) -> p k t", k=KD), ACT.Identity).then_inc(g_hi, 1)

                    def weights_hi(v, k, j):
                        act.wait_ge((ld_w1, ld_w2)[j // 2][v], k * 16 + 16)
                        act.activation(quarter(high, v, j), quarter(whole, v, j), ACT.Identity).then_inc(w_hi[v], 1)

                    def ring_step(s, v, k, last):
                        act.wait_ge(ld_b[v], k * 32 + 32)
                        for f in range(NF):
                            act.wait_ge(h_full, (s + lead) * NF + (f + 1))
                            act.activation(hs[:, f, :], ps[:, f % 4, 0:SUB], func, bias=b1_sb[:, v, f:f + 1]).then_inc(h_in, 1)
                            if not last and f in (1, 3):
                                weights_hi(1 - v, k + v, f // 2)
                        if not last:
                            rows_hi(s + 1)
                            for j in range(2, 4):
                                weights_hi(1 - v, k + v, j)

                    def norm_T(blk):
                        for u in range(2):
                            act.wait_ge(n_full, blk * 2 + u + 1)
                            store_T(act, xnT, 7 - u, blk, u).then_inc(xT_in, 1)

                    if shared:
                        with act.Fori(0, lead) as j:
                            shared_block(j)
                    else:
                        for e in range(2 * NB - 1):
                            key_value(e)
                            if e >= NB:
                                product(e - NB)
                    act.wait_ge(sent, n_ch * NT * 16)
                    for j in range(4):
                        weights_hi(0, 0, j)
                    if not shared:
                        key_value(2 * NB - 1)
                    rows_hi(0)
                    if not shared:
                        product(NB - 1)
                    ring(act, ring_step)
                    for blk in range(NB):
                        if shared and blk % 2 == 0:
                            shared_block(lead + steps + blk // 2)
                        norm_T(blk)

                @block.tensor
                def _(pe):
                    for t in range(NT):
                        for k in range(KD):
                            ins = pe.matmul(ps[:, 7, t * n_exp:(t + 1) * n_exp], xnT[:, k, t * P:(t + 1) * P],
                                            gatew[:, k, go:go + n_exp], start=(k == 0), stop=(k == KD - 1))
                    ins.then_inc(routed, 1)
                    for j in range(NT // 2):
                        wait(pe, r_in, max(0, j - 3))
                        for t in range(2):
                            for k in range(KD):
                                o = t * D + k * P
                                ins = pe.transpose(ps[:, j % 4, o:o + P], xnT[:, k, (2 * j + t) * P:(2 * j + t + 1) * P], ident[:, :])
                        ins.then_inc(r_full, 1)
                    pe.wait_ge(link, CHOSEN_LINK[l])
                    pe.wait_ge(cst, 2)
                    pe.wait_ge(r_in, NT // 2)
                    chosen = rs(0, n_exp)
                    pe.matmul(ps[:, 7, P:P + NT * n_exp].rearrange("p (t e) -> p t e", e=n_exp), upper, chosen, start=True, stop=True)
                    pe.matmul(ps[:, 7, 2 * P:2 * P + NT * n_exp].rearrange("p (t e) -> p t e", e=n_exp), ones, chosen,
                              start=True, stop=True).then_inc(counted, 1)

                    def shared_block(blk, u):
                        for f in range(NF):
                            if f >= 4:
                                pe.wait_ge(h_in, u * NF + (f - 3))
                            for k in range(KD):
                                ins = pe.matmul(ps[:, f % 4, :], w1[0][:, k, f * P:(f + 1) * P], xnT[:, k, ds(blk * BLK, BLK)],
                                                start=(k == 0), stop=(k == KD - 1))
                            ins.then_inc(h_full, 1)
                        for tp in range(2):
                            wait(pe, s_in, blk * 2)
                            for t in range(2):
                                for f in range(NF):
                                    if tp == 0 and t == 0:
                                        pe.wait_ge(h_in, u * NF + (f + 1))
                                    ins = pe.matmul(ps[:, 4 + tp, t * D:(t + 1) * D], hT[:, f, (2 * tp + t) * P:(2 * tp + t + 1) * P],
                                                    w2[0][:, f, :], start=(f == 0), stop=(f == NF - 1))
                            ins.then_inc(s_full, 1)

                    def key_value(e):
                        for i in range(2):
                            if e >= 2:
                                pe.wait_ge(t_in, 2 * (e - 2) + i + 1)
                            for t in range(2):
                                for k in range(KD):
                                    ins = pe.matmul(ps[:, (2 * e + i) % 4, t * D:(t + 1) * D], ctxT[:, k, (2 * e + t) * P:(2 * e + t + 1) * P],
                                                    attw[:, 0, 1 + i, k, :], start=(k == 0), stop=(k == KD - 1))
                            ins.then_inc(t_full, 1)

                    def product(blk):
                        pe.wait_ge(t_bias, 2 * blk + 2)
                        if blk >= 2:
                            pe.wait_ge(kv_in, blk - 1)
                        for u in range(2):
                            for m in range(KD):
                                for t in range(2):
                                    i = 2 * u + t
                                    ins = pe.matmul(ps[:, 4 + blk % 2, u * SEQ + m * P:u * SEQ + (m + 1) * P],
                                                    keys[:, blk * 4 + i, m * P:(m + 1) * P],
                                                    values[blk // 2][:, blk % 2 * 4 + i, m * P:(m + 1) * P], start=(t == 0), stop=(t == 1))
                        ins.then_inc(kv_full, 1)

                    def rows_T(v, k):
                        pe.wait_ge(ld_g[v], k * 16 + 16)
                        transpose_pair(pe, 6, xg_sb[v]).then_inc(g_full, 1)

                    def ring_step(s, v, k, last):
                        hi1, lo1, hi2, lo2 = first_m(high, v), first_m(low, v), second_m(high, v), second_m(low, v)
                        xh, xl, hh, hl = xg_hi, xg_lo, hs_hi, hs_lo
                        pe.wait_ge(g_lo, s + 1)
                        pe.wait_ge(w_lo[v], k * 4 + 2)
                        for f in range(NF):
                            if f >= 4:
                                pe.wait_ge(h_in, (s + lead) * NF + (f - 3))
                            for kk in range(KD):
                                for m, x in ((hi1, xh), (hi1, xl), (lo1, xh)):
                                    ins = pe.matmul(ps[:, f % 4, 0:SUB], m[:, kk, f * P:(f + 1) * P], x[:, kk, :],
                                                    start=(kk == 0 and x is xh and m is hi1), stop=(kk == KD - 1 and m is lo1))
                            ins.then_inc(h_full, 1)
                        if not last:
                            rows_T(1 - v, k + v)
                        wait(pe, y_out[v], k)
                        pe.wait_ge(w_lo[v], k * 4 + 4)
                        for t in range(2):
                            for f in range(NF):
                                if t == 0 and f % 2 == 0:
                                    pe.wait_ge(hid_lo, s * 4 + (f // 2 + 1))
                                for h, m in ((hh, hi2), (hh, lo2), (hl, hi2)):
                                    ins = pe.matmul(ps[:, 4 + v, t * D:(t + 1) * D], h[:, f, t * P:(t + 1) * P], m[:, f, :],
                                                    start=(f == 0 and h is hh and m is hi2), stop=(f == NF - 1 and h is hl))
                        ins.then_inc(y_full[v], 1)

                    def norm_T(blk):
                        for u in range(2):
                            if u == 0:
                                pe.wait_ge(nrm.link, nrm.done(blk, 0))
                            wait(pe, xT_in, max(0, blk * 2 + u - 1))
                            for k in range(KD):
                                for t in range(2):
                                    o = k * SEQ + t * P
                                    ins = pe.transpose(ps[:, 7 - u, o:o + P], normalised(blk, 2 * u + t)[:, k * P:(k + 1) * P], ident[:, :])
                            ins.then_inc(n_full, 1)

                    if shared:
                        pe.wait_ge(ld_w[0], 32)
                        with pe.Fori(0, lead) as j:
                            shared_block(j, j)
                    else:
                        pe.wait_ge(ld_att[0], 32)
                        for e in range(2 * NB):
                            key_value(e)
                            if NB <= e < 2 * NB - 1:
                                product(e - NB)
                    rows_T(0, 0)
                    if not shared:
                        product(NB - 1)
                        pe.wait_ge(t_in, 4 * NB)
                        pe.wait_ge(kv_in, NB)
                    if shared:
                        pe.wait_ge(s_in, 2 * lead)
                    ring(pe, ring_step)
                    pe.wait_ge(y_out[1], pairs)
                    pe.wait_ge(y_out[0], pairs + 1)
                    for blk in range(NB):
                        if shared and blk % 2 == 0:
                            shared_block(lead + blk // 2, lead + steps + blk // 2)
                        norm_T(blk)

        def phase_linear(sync_tail):
            n = "L2a_"
            wq, wo = attw[:, 0, 0], attw[:, 0, 3]
            kv = probT[:, 0]
            kv_in = psem(n + "kv_in")
            q_full = psem(n + "q_full")
            q_in = psem(n + "q_in")
            c_full = psem(n + "c_full")
            c_in = psem(n + "c_in")
            o_full = psem(n + "o_full")
            o_in = psem(n + "o_in")
            n_full = psem(n + "n_full")
            xT_in = psem(n + "xT_in")
            poison = psem(n + "poison")
            scaled = psem(n + "scaled")
            pre = psem(n + "pre")
            post, nrm = Norm(n + "post", 1, 4), Norm(n + "norm", 1, 4)
            ts4, xs4 = (hbuf[:, i * 1024:(i + 1) * 1024].rearrange("p (t d) -> p t d", t=4) for i in range(2))
            xb = wbuf[:, 0].rearrange("p (t d) -> p t d", t=NT)

            with nc.Block() as block:
                @block.sync
                def _(sp):
                    sync_tail(sp)

                @block.gpsimd
                def _(pool):
                    def add_rows(blk):
                        pool.tensor_tensor(xb[:, ds(blk * 4, 4), :], xn_tok[:, ds(blk * 4, 4), :], rowsA[:, 2, :].unsqueeze(1).broadcast_to([P, 4, D]),
                                           ALU.add).then_inc(pre, 1)
                        x4 = x_tok[:, ds(blk * 4, 4), :]
                        pool.tensor_tensor(x4, x4, rowsA[:, 4, :].unsqueeze(1).broadcast_to([P, 4, D]), ALU.add).then_inc(pre, 1)

                    def body(blk, last):
                        if not last:
                            add_rows(blk + 1)
                            pool.wait_ge(c_full, blk * 2 + 2)
                            own_heads(blk + 1)
                        post.power(pool, blk, 0)
                        nrm.power(pool, blk, 0)

                    def own_heads(blk):
                        pool.tensor_tensor(kv.rearrange("p a (m d) -> p (a m) d", m=2),
                                           kv_all[:, ds(blk, 1), :].rearrange("p b (a d) -> p (b a) d", a=4),
                                           bmask[:, :].unsqueeze(1).broadcast_to([P, 4, P]), ALU.mult).then_inc(kv_in, 1)

                    own_heads(0)
                    pool.wait_ge(scaled, 1)
                    add_rows(0)
                    with pool.Fori(0, NB - 1) as blk:
                        body(blk, False)
                    body(NB - 1, True)

                @block.scalar
                def _(act):
                    def norm_T(blk):
                        for u in range(2):
                            act.wait_ge(n_full, blk * 2 + (u + 1))
                            store_T(act, xnT, 7 - u, blk, u).then_inc(xT_in, 1)

                    def body(blk, first):
                        for m in range(KD):
                            act.wait_ge(q_full, blk * 2 + (m + 1))
                            act.activation(qT[:, m, :], ps[:, m, :], ACT.Identity, bias=col("L2_bq", m)).then_inc(q_in, 1)
                        for u in range(2):
                            act.wait_ge(c_full, blk * 2 + (u + 1))
                            act.activation(kT[:, :, u * SEQ:(u + 1) * SEQ], ps[:, 4 + u, :].rearrange("p (m q) -> p m q", m=KD),
                                           ACT.Identity).then_inc(c_in, 1)
                        if not first:
                            norm_T(blk - 1)

                    blocks(act, body, norm_T)

                @block.vector
                def _(dve):
                    dve.wait_ge(ld_rowsA, 48)
                    dve.tensor_scalar(rowsA[:, 3:5, :], rowsA[:, 3:5, :], gate(2), None, ALU.mult).then_inc(scaled, 1)
                    dve.wait_ge(ld_mask, 16)
                    dve.tensor_reduce(anym[:, 0, :], mask8, AXX, ALU.max).then_inc(poison, 1)
                    dve.wait_ge(poison, 1)
                    dve.tensor_scalar(anym[:, 0, :], anym[:, 0, :], 3.0e38, 3.0e38, ALU.mult, ALU.mult).then_inc(poison, 1)
                    dve.wait_ge(poison, 2)
                    dve.tensor_tensor(anym[:, 1, :], anym[:, 0, :], anym[:, 0, :], ALU.subtract).then_inc(poison, 1)
                    dve.wait_ge(poison, 3)
                    dve.wait_ge(scaled, 1)
                    with dve.Fori(0, NB) as blk:
                        dve.wait_ge(pre, blk * 2 + 2)
                        for u in range(2):
                            dve.wait_ge(o_full, blk * 2 + (u + 1))
                            for t in range(2):
                                i = 2 * u + t
                                ins = dve.scalar_tensor_tensor(ts4[:, i, :], ps[:, 2 + u, t * D:(t + 1) * D], anym[:, 1, ds(blk * 4 + i, 1)],
                                                               xb[:, ds(blk * 4 + i, 1), :][:, 0, :], ALU.add, ALU.add)
                            ins.then_inc(o_in, 1)
                        dve.wait_ge(o_in, blk * 2 + 2)
                        tp = lambda t: ts4[:, t, :]
                        post.statistics(dve, blk, 0, tp)
                        xp = x_tile(blk)
                        post.add_scaled(dve, blk, 0, tp, rowsA[:, 3, :], xp)
                        dve.wait_ge(post.link, post.done(blk, 0))
                        nrm.statistics(dve, blk, 0, xp)
                        wait(dve, xT_in, blk * 2)
                        nrm.result(dve, blk, 0, lambda t: xs4[:, t, :], xp)

                @block.tensor
                def _(pe):
                    def norm_T(blk):
                        pe.wait_ge(nrm.link, nrm.done(blk, 0))
                        for u in range(2):
                            transpose_pair(pe, 7 - u, xs4[:, 2 * u:2 * u + 2, :]).then_inc(n_full, 1)

                    def body(blk, first):
                        for m in range(KD):
                            for k in range(KD):
                                ins = pe.matmul(ps[:, m, :], wq[:, k, m * P:(m + 1) * P], xnT[:, k, ds(blk * BLK, BLK)],
                                                start=(k == 0), stop=(k == KD - 1))
                            ins.then_inc(q_full, 1)
                        pe.wait_ge(q_in, blk * 2 + 2)
                        pe.wait_ge(kv_in, blk + 1)
                        for u in range(2):
                            for m in range(KD):
                                ins = pe.matmul(ps[:, 4 + u, m * SEQ:(m + 1) * SEQ], kv[:, u, m * P:(m + 1) * P],
                                                qT[:, m, u * SEQ:(u + 1) * SEQ], start=True, stop=True)
                            ins.then_inc(c_full, 1)
                        wait(pe, o_in, blk * 2)
                        for u in range(2):
                            pe.wait_ge(c_in, blk * 2 + (u + 1))
                            for t in range(2):
                                for m in range(KD):
                                    ins = pe.matmul(ps[:, 2 + u, t * D:(t + 1) * D], kT[:, m, u * SEQ + t * P:u * SEQ + (t + 1) * P],
                                                    wo[:, m, :], start=(m == 0), stop=(m == 1))
                            ins.then_inc(o_full, 1)
                        if not first:
                            norm_T(blk - 1)

                    pe.wait_ge(ld_att[0], 32)
                    blocks(pe, body, norm_T)

        class Single:

            def __init__(self, n):
                self.s_full = psem(n + "s_full")
                self.maxed = psem(n + "maxed")
                self.e_in = psem(n + "e_in")
                self.p_full = psem(n + "p_full")
                self.p_in = psem(n + "p_in")

            def scores(self, pe, blk):
                for u in range(2):
                    for qt in range(2):
                        for k in range(KD):
                            ins = pe.matmul(ps[:, 2 * u + qt, 0:SEQ], qT[:, k, u * SEQ + qt * P:u * SEQ + (qt + 1) * P],
                                            kT[:, k, u * SEQ:(u + 1) * SEQ], start=(k == 0), stop=(k == KD - 1))
                        ins.then_inc(self.s_full, 1)

            def turn(self, pe, blk):
                for u in range(2):
                    pe.wait_ge(self.e_in, blk * 4 + (2 * u + 2))
                    for kt in range(2):
                        for qt in range(2):
                            ins = pe.transpose(ps[:, 6 + u, kt * SEQ + qt * P:kt * SEQ + (qt + 1) * P],
                                               prob[:, u, qt, 0, kt * P:(kt + 1) * P], ident[:, :])
                    ins.then_inc(self.p_full, 1)

            def exps(self, act, blk, from_psum):
                for u in range(2):
                    for qt in range(2):
                        act.wait_ge(self.maxed, blk * 4 + (2 * u + qt + 1))
                        dst = prob[:, u, qt, 0, :]
                        src = ps[:, 2 * u + qt, 0:SEQ] if from_psum else prob[:, u, qt, 1, :]
                        act.activation(dst, src, ACT.Exp, bias=negmax[:, u, qt, 0:1], accum_out=rowsum[:, u, qt, 0:1]).then_inc(self.e_in, 1)

            def turned(self, act, blk):
                for u in range(2):
                    act.wait_ge(self.p_full, blk * 2 + (u + 1))
                    act.activation(probT[:, u].rearrange("p a b -> p (a b)"), ps[:, 6 + u, :], ACT.Identity).then_inc(self.p_in, 1)

        vtok = rowsF[:, 4:8, :]

        def phase_trees(sync_tail):
            n = "L2f_"
            SLOTS = 3
            PER = TSTEPS // SLOTS
            TOTAL = TREES * TSTEPS
            nodes = psem(n + "nodes")
            link = psem(n + "link")
            counted = psem(n + "counted")
            cst = psem(n + "cst")
            r_full = psem(n + "r_full")
            r_in = psem(n + "r_in")
            ld_leafm = psem(n + "ld_leafm")
            leafm_in = psem(n + "leafm_in")
            sent = [psem(n + f"sent{r}") for r in range(TREES)]
            ld_g = [psem(n + f"ld_g{v}") for v in range(SLOTS)]
            ld_r = [psem(n + f"ld_r{v}") for v in range(SLOTS)]
            g_full = psem(n + "g_full")
            g_in = psem(n + "g_in")
            f_in = psem(n + "f_in")
            h_full = psem(n + "h_full")
            h_in = psem(n + "h_in")
            y_full = [psem(n + f"y_full{v}") for v in range(SLOTS)]
            y_out = [psem(n + f"y_out{v}") for v in range(SLOTS)]
            y_st = [psem(n + f"y_st{v}") for v in range(SLOTS)]
            got = [psem(n + f"got{r}") for r in range(2)]
            got_v = [psem(n + f"got_v{blk}") for blk in range(NB)]
            t_full = psem(n + "t_full")
            t_in = psem(n + "t_in")
            o_full = psem(n + "o_full")
            o_in = psem(n + "o_in")
            rg = psem(n + "rg")
            n_full = psem(n + "n_full")
            xT_in = psem(n + "xT_in")
            nrm = Norm(n + "norm", 1, 4)
            xs4 = hbuf[:, 0:1024].rearrange("p (t d) -> p t d", t=4)
            at = Single(n)

            LT, PT = TREES * NT, NPAIR * TREES
            def hb(o, w):
                return hbuf[:, o:o + w]
            decs, chA, chB = (hb(i * LT * NLEAF, LT * NLEAF).rearrange("p (t l) -> p t l", l=NLEAF) for i in range(3))
            o = 3 * LT * NLEAF
            chosen, s1, s2, tmp = (hb(o + i * LT * NPAIR, LT * NPAIR) for i in range(4))
            o += 4 * LT * NPAIR
            pq, pn, pa, pb = (hb(o + i * PT, PT) for i in range(4))
            flags = hb(o + 4 * PT, 2 * LT).rearrange("p (t f) -> p t f", f=2)
            upper, ones = oT[:, 0, 0:P], oT[:, 0, P:2 * P]
            stepno = dec[:, :, :, :].rearrange("p a b c -> p (a b c)")[:, 0:TSTEPS]
            stage_flat = stage[:, :, :].rearrange("p k t -> p (k t)")
            def x_row(i):
                return vbuf[:, i * ROW:(i + 1) * ROW] if i < NT - 1 else stage_flat[:, 0:ROW]
            leafm = stage_flat[0:NFLAG, ROW:ROW + TREES * P // 2].bitcast(BF16).rearrange("p (r c) -> p r c", r=TREES)
            leafm_ld = rt[0:NFLAG, :, :, :].rearrange("p a b c -> p (a b c)")
            prob_flat = prob[:, :, :, :, :].rearrange("p a b c s -> p (a b c s)")
            probT_flat = probT[:, :, :, :].rearrange("p a b s -> p (a b s)")
            att_flat = attw[:, 0].rearrange("p w k n -> p (w k n)")
            q_flat, k_flat, o_flat = (x[:, :, :].rearrange("p k t -> p (k t)") for x in (qT, kT, oT))
            rows = [prob_flat[:, v * 2 * ROW:(v + 1) * 2 * ROW].rearrange("p (t d) -> p t d", t=2) for v in range(SLOTS)]
            rec = [att_flat[:, v * REC:(v + 1) * REC] for v in range(SLOTS)]
            b2r = [q_flat[0:NFLAG, v * D:(v + 1) * D] for v in range(SLOTS)]
            hid = q_flat[:, SLOTS * D:SLOTS * D + SUB]
            xT = k_flat[:, 0:KD * SUB].rearrange("p (k t) -> p k t", k=KD)
            flagTb = [k_flat[0:NFLAG, KD * SUB + v * SUB // 2:KD * SUB + (v + 1) * SUB // 2].bitcast(BF16) for v in range(SLOTS)]
            flagT = [probT_flat[0:NFLAG, 3 * 2 * D:3 * 2 * D + SUB], o_flat[0:NFLAG, 0:SUB], o_flat[0:NFLAG, SUB:2 * SUB]]
            y_sb = [probT_flat[:, v * 2 * D:(v + 1) * 2 * D].rearrange("p (t d) -> p t d", t=2) for v in range(SLOTS)]
            outs = [x.rearrange("p (t d) -> p t d", t=NT) for x in (wbuf[:, 1, :], wbuf[:, 2, :], vbuf[:, :])]

            def ring(eng, step):
                for r in range(TREES):
                    whole = PER - (r == TREES - 1)
                    with eng.Fori(0, whole) as i:
                        for v in range(SLOTS):
                            step(r, i * SLOTS + (r * TSTEPS + v), v, i + r * PER, False)
                for v in range(SLOTS):
                    step(TREES - 1, TOTAL - SLOTS + v, v, TREES * PER - 1, v == SLOTS - 1)

            def after(v, k):
                return (v + 1) % SLOTS, k + (v == SLOTS - 1)

            with nc.Block() as block:
                @block.vector
                def _(dve):
                    count = [0]

                    def step(ins):
                        count[0] += 1
                        ins.then_inc(link, 1)
                        dve.wait_ge(link, count[0])

                    dve.wait_ge(nodes, 1)
                    raw = chB.rearrange("p t l -> p (t l)")[:, 0:LT * NODES]
                    half = NT // 2 * TREES * NODES
                    nb = small[:, E1:].unsqueeze(1).broadcast_to([P, NT // 2, TREES * NODES])
                    for i in range(2):
                        step(dve.tensor_tensor(raw[:, i * half:(i + 1) * half].rearrange("p (t j) -> p t j", j=TREES * NODES),
                                               ps[:, 4 + i, 0:half].rearrange("p (t j) -> p t j", j=TREES * NODES), nb, ALU.add))
                    step(dve.tensor_scalar(decs[:, :, 0:NODES], raw.rearrange("p (t j) -> p t j", j=NODES), 0.0, None, ALU.is_ge))
                    step(dve.tensor_copy(chA[:, :, 1:2], decs[:, :, 0:1]))
                    step(dve.tensor_scalar(chA[:, :, 0:1], decs[:, :, 0:1], -1.0, 1.0, ALU.mult, ALU.add))
                    src, dst = chA, chB
                    for lev in range(1, DEPTH):
                        w = 1 << lev
                        right, left = dst[:, :, 1:2 * w:2], dst[:, :, 0:2 * w:2]
                        step(dve.tensor_tensor(right, src[:, :, 0:w], decs[:, :, w - 1:2 * w - 1], ALU.mult))
                        step(dve.tensor_tensor(left, src[:, :, 0:w], right, ALU.subtract))
                        src, dst = dst, src
                    first, second = src[:, :, 0::2], src[:, :, 1::2]
                    by_tree = lambda x, e: x.rearrange("p (t e) -> p t e", e=e)
                    step(dve.tensor_tensor(by_tree(chosen, NPAIR), first, second, ALU.add))
                    assert count[0] == T_CHOSEN, count[0]
                    step(dve.tensor_reduce(flags[:, :, 0], first, AXX, ALU.add))
                    step(dve.tensor_reduce(flags[:, :, 1], second, AXX, ALU.add))
                    dve.wait_ge(r_in, NT // 2)
                    per_tok = flags.rearrange("p (t r) f -> p t (r f)", t=NT)
                    step(dve.tensor_copy(vbuf[:, 0:(NT - 1) * ROW].rearrange("p (t d) -> p t d", d=ROW)[:, :, D:ROW], per_tok[:, 0:NT - 1, :]))
                    step(dve.tensor_copy(x_row(NT - 1)[:, D:ROW], per_tok[:, NT - 1, :]))
                    dve.wait_ge(counted, 1)
                    by_tile = lambda x: x.rearrange("p (t e) -> p t e", e=PT)
                    before, total = ps[:, 6, 0:NT * PT], ps[:, 7, 0:NT * PT]
                    step(dve.tensor_copy(s1, total))
                    src, dst, sh = s1, s2, 1
                    while sh < NT:
                        dve.tensor_copy(by_tile(dst)[:, 0:sh, :], by_tile(src)[:, 0:sh, :])
                        step(dve.tensor_tensor(by_tile(dst)[:, sh:, :], by_tile(src)[:, sh:, :], by_tile(src)[:, 0:NT - sh, :], ALU.add))
                        src, dst, sh = dst, src, 2 * sh
                    step(dve.tensor_tensor(dst, src, total, ALU.subtract))
                    step(dve.tensor_tensor(dst, dst, before, ALU.add))
                    place = dst
                    step(dve.tensor_scalar(pq, by_tile(src)[:, NT - 1, :], 1.0 / SUB, 1.0, ALU.mult, ALU.add))
                    below = tmp[:, 0:PT * 8].rearrange("p (e j) -> p e j", j=8)
                    step(dve.tensor_tensor(below, pq.unsqueeze(2).broadcast_to([P, PT, 8]), rank[:, :].unsqueeze(1).broadcast_to([P, PT, 8]), ALU.is_gt))
                    step(dve.tensor_reduce(pn, below, AXX, ALU.add))
                    src, dst, other, sh = pn, pa, pb, 1
                    while sh < NPAIR:
                        dve.tensor_copy(by_tree(dst, NPAIR)[:, :, 0:sh], by_tree(src, NPAIR)[:, :, 0:sh])
                        step(dve.tensor_tensor(by_tree(dst, NPAIR)[:, :, sh:], by_tree(src, NPAIR)[:, :, sh:], by_tree(src, NPAIR)[:, :, 0:NPAIR - sh], ALU.add))
                        src, dst, other, sh = dst, other, dst, 2 * sh
                    step(dve.tensor_tensor(pq, src, pn, ALU.subtract))
                    step(dve.tensor_scalar(pq, pq, float(SUB), None, ALU.mult))
                    step(dve.tensor_tensor(by_tile(place), by_tile(place), pq.unsqueeze(1).broadcast_to([P, NT, PT]), ALU.add))
                    step(dve.tensor_tensor(tmp, chosen, place, ALU.mult))
                    step(dve.tensor_reduce(flags[:, :, 0], by_tree(tmp, NPAIR), AXX, ALU.add))
                    step(dve.tensor_copy(rowt[:, :], flags[:, :, 0]))
                    assert count[0] == T_PLACED, count[0]
                    dve.wait_ge(cst, 3)
                    full = tmp[:, 0:TOTAL * NPAIR].rearrange("p (r s e) -> p r s e", r=TREES, e=NPAIR)
                    step(dve.tensor_tensor(full, by_tree(src, NPAIR).unsqueeze(2).broadcast_to([P, TREES, TSTEPS, NPAIR]),
                                           stepno.unsqueeze(1).unsqueeze(3).broadcast_to([P, TREES, TSTEPS, NPAIR]), ALU.is_le))
                    pair_of = s1[:, 0:TOTAL] if place is s2 else s2[:, 0:TOTAL]
                    step(dve.tensor_reduce(pair_of, tmp[:, 0:TOTAL * NPAIR].rearrange("p (s e) -> p s e", e=NPAIR), AXX, ALU.add))
                    for r in range(TREES):
                        e = slice(r * TSTEPS, (r + 1) * TSTEPS)
                        ins = dve.tensor_scalar(step_exp[:, e], pair_of[:, e], float(NPAIR - 1), float(r * NPAIR), ALU.min, ALU.add)
                    step(ins)
                    assert count[0] == T_STEPS, count[0]

                    def flags_in(g, v):
                        dve.wait_ge(g_full, g + 1)
                        dve.tensor_copy(flagT[v], ps[0:NFLAG, 7, 0:SUB])
                        dve.tensor_copy(flagTb[v], ps[0:NFLAG, 7, 0:SUB]).then_inc(f_in, 1)

                    def ring_step(r, g, v, k, last):
                        if not last:
                            flags_in(g + 1, after(v, k)[0])
                        dve.wait_ge(y_full[v], k + 1)
                        dve.wait_ge(y_st[v], k * 16)
                        dve.tensor_copy(y_sb[v], ps[:, 3 + v, :].rearrange("p (t d) -> p t d", t=2)).then_inc(y_out[v], 1)

                    flags_in(0, 0)
                    ring(dve, ring_step)
                    for blk in range(NB):
                        for u in range(2):
                            for qt in range(2):
                                dve.wait_ge(at.s_full, blk * 4 + (2 * u + qt + 1))
                                dve.tensor_reduce(negmax[:, u, qt, 0:1], ps[:, 2 * u + qt, 0:SEQ], AXX, ALU.max, negate=True).then_inc(at.maxed, 1)
                        for u in range(2):
                            dve.wait_ge(at.e_in, blk * 4 + (2 * u + 2))
                            dve.reciprocal(rinv[:, u, :, 0], rowsum[:, u, :, 0]).then_inc(rg, 1)
                            dve.wait_ge(rg, blk * 4 + (2 * u + 1))
                            dve.tensor_scalar(rinv[:, u, :, 1], rinv[:, u, :, 0], gate(4 + 2), None, ALU.mult).then_inc(rg, 1)
                            dve.wait_ge(rg, blk * 4 + (2 * u + 2))
                            dve.wait_ge(o_full, blk * 2 + (u + 1))
                            xp = x_pair(blk, u)
                            for t in range(2):
                                x = xp(t)[:, 0, :]
                                ins = dve.scalar_tensor_tensor(x, ps[:, 4 + u, t * D:(t + 1) * D], rinv[:, u, t, 1:2], x, ALU.mult, ALU.add)
                            ins.then_inc(o_in, 1)
                        dve.wait_ge(o_in, blk * 2 + 2)
                        xp = x_tile(blk)
                        nrm.statistics(dve, blk, 0, xp)
                        wait(dve, n_full, blk * 2)
                        nrm.result(dve, blk, 0, lambda t: xs4[:, t, :], xp)

                @block.sync
                def _(sp):
                    sp.dma_start(leafm_ld, a["leafm"]).then_inc(ld_leafm, 16)
                    sync_tail(sp)

                    def load_weights(r, s, v, k):
                        e = sp.value_load(step_exp[0:1, ds(s + r * TSTEPS, 1)], min_val=0, max_val=TREES * NPAIR - 1)
                        wait(sp, y_full[v], k)
                        sp.dma_start(rec[v], a["L2_rec"][ds(e, 1)].rearrange("e p c -> (e p) c")).then_inc(ld_r[v], 16)
                        sp.dma_start(b2r[v], a["L2_b2r"][ds(e, 1)].rearrange("e p d -> (e p) d")).then_inc(ld_r[v], 16)

                    def load_rows_of(r, s, v):
                        wait(sp, g_full, s + (r * TSTEPS - SLOTS + 1))
                        sp.dma_start(rows[v], a[f"xt{r}"][ds(s * SUB, SUB)].rearrange("(t p) d -> p t d", p=P)).then_inc(ld_g[v], 16)

                    def store(r, s, v, k):
                        sp.wait_ge(y_out[v], k + 1)
                        sp.dma_start(a[f"yt{r}"][ds(s * SUB, SUB)].rearrange("(t p) d -> p t d", p=P), y_sb[v]).then_inc(y_st[v], 16)

                    def rest(r, s, v, k):
                        if isinstance(s, int) and s < SLOTS:
                            store(r - 1, s + TSTEPS - SLOTS, v, k - 1)
                        else:
                            store(r, s - SLOTS, v, k - 1)
                        load_weights(r, s, v, k)
                        if isinstance(s, int) and s == TSTEPS - 1:
                            if r < TREES - 1:
                                sp.wait_ge(sent[r + 1], NT * 16)
                                load_rows_of(r + 1, 0, 0)
                        else:
                            load_rows_of(r, s + 1, (v + 1) % SLOTS)

                    sp.wait_ge(link, T_STEPS)
                    for v in range(SLOTS):
                        load_weights(0, v, v, 0)
                    sp.wait_ge(sent[0], NT * 16)
                    for s in range(SLOTS + 1):
                        load_rows_of(0, s, s % SLOTS)
                    for r in range(TREES):
                        if r:
                            for v in range(SLOTS):
                                rest(r, v, v, r * PER)
                        with sp.Fori(1, PER - 1) as i:
                            for v in range(SLOTS):
                                rest(r, i * SLOTS + v, v, i + r * PER)
                        for v in range(SLOTS):
                            rest(r, TSTEPS - SLOTS + v, v, r * PER + PER - 1)
                    for v in range(SLOTS):
                        store(TREES - 1, TSTEPS - SLOTS + v, v, TREES * PER - 1)

                @block.gpsimd
                def _(pool):
                    pool.memset(ones, 1.0).then_inc(cst, 1)
                    pool.wait_ge(cst, 1)
                    pool.affine_select(out=upper, in_=ones, pattern=[[1, P]], compare_op=ALU.is_gt, fill=0.0,
                                       base=0, channel_multiplier=-1).then_inc(cst, 1)
                    pool.iota(stepno, pattern=[[1, TSTEPS]], base=0, channel_multiplier=0, allow_small_or_imprecise_dtypes=True).then_inc(cst, 1)
                    pool.wait_ge(link, T_PLACED)
                    pool.wait_ge(zeroed, 64)
                    for r in range(TREES):
                        for t in range(NT):
                            pool.indirect_dma_start(a[f"xt{r}"], bass.IndirectOffsetOnAxis(rowt[:, t * TREES + r:t * TREES + r + 1], 0),
                                                    x_row(t), None).then_inc(sent[r], 16)
                    for r in range(TREES):
                        pool.wait_ge(sent[r], NT * 16)
                    for r in range(TREES):
                        for v in range(SLOTS):
                            pool.wait_ge(y_st[v], PER * (r + 1) * 16)
                        for t in range(NT):
                            pool.indirect_dma_start(outs[r][:, t, :], None, a[f"yt{r}"],
                                                    bass.IndirectOffsetOnAxis(rowt[:, t * TREES + r:t * TREES + r + 1], 0)).then_inc(got[r] if r < 2 else got_v[t // 4], 16)
                    for blk in range(NB):
                        nrm.power(pool, blk, 0)

                @block.scalar
                def _(act):
                    for j in range(NT // 2):
                        act.wait_ge(r_full, j + 1)
                        for t in range(2):
                            ins = act.activation(x_row(2 * j + t)[:, 0:D], ps[:, j % 4, t * D:(t + 1) * D], ACT.Identity)
                        ins.then_inc(r_in, 1)
                    act.wait_ge(ld_leafm, 16)
                    act.activation(leafm.rearrange("p r c -> p (r c)"), leafm_ld, ACT.Identity).then_inc(leafm_in, 1)

                    def rows_in(g):
                        act.wait_ge(g_full, g + 1)
                        act.activation(xT, ps[:, 6, :].rearrange("p (k t) -> p k t", k=KD), ACT.Identity).then_inc(g_in, 1)

                    def ring_step(r, g, v, k, last):
                        act.wait_ge(ld_r[v], k * 32 + 32)
                        act.wait_ge(h_full, g + 1)
                        act.activation(hid, ps[:, v, 0:SUB], ACT.Relu, bias=rec[v][:, REC - 1:REC]).then_inc(h_in, 1)
                        if not last:
                            rows_in(g + 1)

                    def norm_T(blk):
                        for u in range(2):
                            act.wait_ge(n_full, blk * 2 + (u + 1))
                            store_T(act, xnT, 6 + u, blk, u).then_inc(xT_in, 1)

                    rows_in(0)
                    ring(act, ring_step)
                    for v in range(SLOTS):
                        act.wait_ge(y_st[v], TREES * PER * 16)
                    for blk in range(NB):
                        for i, dst in enumerate((qT, kT)):
                            for u in range(2):
                                act.wait_ge(t_full, blk * 4 + (2 * i + u + 1))
                                act.activation(dst[:, :, u * SEQ:(u + 1) * SEQ], ps[:, 2 * i + u, :].rearrange("p (k t) -> p k t", k=KD),
                                               ACT.Identity, scale=(1.0 if i else D ** -0.5)).then_inc(t_in, 1)
                        at.exps(act, blk, True)
                        at.turned(act, blk)
                        if blk:
                            norm_T(blk - 1)
                    norm_T(NB - 1)

                @block.tensor
                def _(pe):
                    go = E0 - 1 + E1
                    for t in range(NT):
                        q = t % (NT // 2) * TREES * NODES
                        for k in range(KD):
                            ins = pe.matmul(ps[:, 4 + t // (NT // 2), q:q + TREES * NODES], xnT[:, k, t * P:(t + 1) * P],
                                            gatew[:, k, go:go + TREES * NODES], start=(k == 0), stop=(k == KD - 1))
                    ins.then_inc(nodes, 1)
                    for j in range(NT // 2):
                        wait(pe, r_in, max(0, j - 3))
                        for t in range(2):
                            for k in range(KD):
                                o = t * D + k * P
                                ins = pe.transpose(ps[:, j % 4, o:o + P], xnT[:, k, (2 * j + t) * P:(2 * j + t + 1) * P], ident[:, :])
                        ins.then_inc(r_full, 1)
                    pe.wait_ge(link, T_CHOSEN)
                    pe.wait_ge(cst, 2)
                    pe.matmul(ps[:, 6, 0:LT * NPAIR], upper, chosen, start=True, stop=True)
                    pe.matmul(ps[:, 7, 0:LT * NPAIR], ones, chosen, start=True, stop=True).then_inc(counted, 1)

                    def rows_T(v, k):
                        pe.wait_ge(ld_g[v], k * 16 + 16)
                        transpose_pair(pe, 6, rows[v])
                        for t in range(2):
                            ins = pe.transpose(ps[0:NFLAG, 7, t * P:(t + 1) * P], rows[v][:, t, D:ROW], ident[:, :])
                        ins.then_inc(g_full, 1)

                    def ring_step(r, g, v, k, last):
                        pe.wait_ge(g_in, g + 1)
                        pe.wait_ge(f_in, g + 1)
                        pe.wait_ge(ld_r[v], k * 32 + 32)
                        w1r, w2r = rec[v][:, 0:D], rec[v][:, D:2 * D]
                        for kk in range(KD):
                            pe.matmul(ps[:, v, 0:SUB], w1r[:, kk * P:(kk + 1) * P], xT[:, kk, :], start=(kk == 0), stop=False)
                        pe.matmul(ps[:, v, 0:SUB], leafm[:, r, :], flagTb[v], start=False, stop=True).then_inc(h_full, 1)
                        if not last:
                            rows_T(*after(v, k))
                        wait(pe, y_out[v], k)
                        pe.wait_ge(h_in, g + 1)
                        for t in range(2):
                            o = ps[:, 3 + v, t * D:(t + 1) * D]
                            pe.matmul(o, hid[:, t * P:(t + 1) * P], w2r, start=True, stop=False)
                            ins = pe.matmul(o, flagT[v][:, t * P:(t + 1) * P], b2r[v], start=False, stop=True)
                        ins.then_inc(y_full[v], 1)

                    def norm_T(blk):
                        pe.wait_ge(nrm.link, nrm.done(blk, 0))
                        wait(pe, xT_in, blk * 2)
                        for u in range(2):
                            transpose_pair(pe, 6 + u, xs4[:, 2 * u:2 * u + 2, :]).then_inc(n_full, 1)

                    pe.wait_ge(leafm_in, 1)
                    rows_T(0, 0)
                    ring(pe, ring_step)
                    for v in range(SLOTS):
                        pe.wait_ge(y_out[v], TREES * PER)
                    for blk in range(NB):
                        wait(pe, at.e_in, blk * 4)
                        for i in range(2):
                            pe.wait_ge(got[i], NT * 16)
                            for u in range(2):
                                transpose_pair(pe, 2 * i + u, outs[i][:, blk * 4 + 2 * u:blk * 4 + 2 * u + 2, :]).then_inc(t_full, 1)
                        pe.wait_ge(t_in, blk * 4 + 4)
                        at.scores(pe, blk)
                        wait(pe, xT_in, max(0, blk - 1) * 2)
                        at.turn(pe, blk)
                        pe.wait_ge(got_v[blk], 64)
                        wait(pe, o_in, blk * 2)
                        for u in range(2):
                            pe.wait_ge(at.p_in, blk * 2 + (u + 1))
                            for t in range(2):
                                for kt in range(2):
                                    ins = pe.matmul(ps[:, 4 + u, t * D:(t + 1) * D], probT[:, u, kt, t * P:(t + 1) * P],
                                                    outs[2][:, blk * 4 + 2 * u + kt, :], start=(kt == 0), stop=(kt == 1))
                            ins.then_inc(o_full, 1)
                        if blk:
                            norm_T(blk - 1)
                    norm_T(NB - 1)

        def phase_padded(sync_tail):
            n = "L3a_"
            wq, wk, wv, wo = (attw[:, 1, i] for i in range(4))
            padm, pada = wbuf[:, 2, 0:T], wbuf[:, 2, T:2 * T]
            padi = hbuf[:, 0:T].bitcast(I32)
            staged = psem(n + "staged")
            q_full = psem(n + "q_full")
            q_in = psem(n + "q_in")
            v_full = psem(n + "v_full")
            v_in = psem(n + "v_in")
            mskd = psem(n + "masked")
            c_full = psem(n + "c_full")
            c_in = psem(n + "c_in")
            o_full = psem(n + "o_full")
            o_in = psem(n + "o_in")
            inv = psem(n + "inv")
            n_full = psem(n + "n_full")
            xT_in = psem(n + "xT_in")
            copied = psem(n + "copied")
            pads = psem(n + "pads")
            w_hi = psem(n + "w_hi")
            w_lo = psem(n + "w_lo")
            scaled = psem(n + "scaled")
            pre = psem(n + "pre")
            post, nrm = Norm(n + "post", 1, 4), Norm(n + "norm", 1, 4)
            ts4, xs4 = (hbuf[:, i * 1024:(i + 1) * 1024].rearrange("p (t d) -> p t d", t=4) for i in (2, 3))
            at = Single(n)

            with nc.Block() as block:
                @block.sync
                def _(sp):
                    sp.dma_start(padi, a["pad"].unsqueeze(0).broadcast_to([P, T])).then_inc(ld_pad, 16)
                    sync_tail(sp)

                @block.gpsimd
                def _(pool):
                    def body(blk, last):
                        x4 = x_tok[:, ds(blk * 4, 4), :]
                        pool.tensor_tensor(x4, x4, rowsA[:, 3, :].unsqueeze(1).broadcast_to([P, 4, D]), ALU.add).then_inc(pre, 1)
                        if not last:
                            pool.wait_ge(v_full, blk * 2 + 2)
                            pool.tensor_copy(stage[:, :, :], ctxT[:, :, ds(blk * BLK + BLK, BLK)]).then_inc(staged, 1)
                        post.power(pool, blk, 0)
                        nrm.power(pool, blk, 0)
                        pool.wait_ge(nrm.link, nrm.done(blk, 0))
                        pool.tensor_copy(xn_tok[:, ds(blk * 4, 4), :], xs4).then_inc(copied, 1)

                    pool.tensor_copy(stage[:, :, :], ctxT[:, :, 0:BLK]).then_inc(staged, 1)
                    pool.wait_ge(scaled, 1)
                    with pool.Fori(0, NB - 1) as blk:
                        body(blk, False)
                    body(NB - 1, True)

                @block.scalar
                def _(act):
                    def norm_T(blk):
                        for u in range(2):
                            act.wait_ge(n_full, blk * 2 + (u + 1))
                            store_T(act, xnT, 6 + u, blk, u).then_inc(xT_in, 1)

                    def body(blk, first):
                        for j in range(4):
                            m = j % 2
                            act.wait_ge(q_full, blk * 4 + (j + 1))
                            if j < 2:
                                act.activation(qT[:, m, :], ps[:, j, :], ACT.Identity, bias=qbias[:, 2 + m:3 + m], scale=D ** -0.5).then_inc(q_in, 1)
                            else:
                                act.activation(kT[:, m, :], ps[:, j, :], ACT.Identity, bias=col("L3_bk", m)).then_inc(q_in, 1)
                        if not first:
                            norm_T(blk - 1)
                        at.exps(act, blk, False)
                        at.turned(act, blk)
                        for u in range(2):
                            act.wait_ge(c_full, blk * 2 + (u + 1))
                            act.activation(probT[:, 2 + u].rearrange("p a b -> p (a b)"), ps[:, 4 + u, :], ACT.Identity).then_inc(c_in, 1)

                    def tail(blk):
                        act.wait_ge(ld_w[LAST_LOAD[0]], 32 * LAST_LOAD[1])
                        for j in range(4):
                            q = slice(j * 1024, (j + 1) * 1024)
                            act.activation(wbuf_r[1][:, q], wbuf[:, LAST_LOAD[0], q], ACT.Identity).then_inc(w_hi, 1)
                        norm_T(blk)

                    blocks(act, body, tail)

                @block.vector
                def _(dve):
                    dve.wait_ge(ld_pad, 16)
                    dve.tensor_scalar(pada, padi, 0.0, NEG, ALU.is_equal, ALU.mult)
                    dve.tensor_scalar(padm, padi, 0.0, None, ALU.not_equal).then_inc(pads, 1)
                    dve.wait_ge(pads, 1)
                    dve.wait_ge(ld_rowsA, 64)
                    dve.tensor_scalar(rowsA[:, 2:4, :], rowsA[:, 2:4, :], gate(3), None, ALU.mult).then_inc(scaled, 1)
                    dve.wait_ge(scaled, 1)
                    with dve.Fori(0, NB) as blk:
                        def value_bias(u):
                            dve.wait_ge(v_full, blk * 2 + (u + 1))
                            dve.tensor_tensor(vtok[:, 2 * u:2 * u + 2, :], ps[:, 4 + u, :].rearrange("p (t d) -> p t d", t=2),
                                              rowsA[:, 0, :].unsqueeze(1).broadcast_to([P, 2, D]), ALU.add).then_inc(v_in, 1)

                        value_bias(0)
                        for u in range(2):
                            sc = prob[:, u, :, 1, :]
                            pm, pa = (x[:, ds(blk * BLK + u * SEQ, SEQ)].unsqueeze(1).broadcast_to([P, 2, SEQ]) for x in (padm, pada))
                            dve.wait_ge(at.s_full, blk * 4 + (2 * u + 2))
                            dve.tensor_tensor(sc, ps[:, 2 * u:2 * u + 2, 0:SEQ], pm, ALU.mult).then_inc(mskd, 1)
                            dve.wait_ge(mskd, blk * 4 + (2 * u + 1))
                            dve.tensor_tensor(sc, sc, pa, ALU.add).then_inc(mskd, 1)
                            dve.wait_ge(mskd, blk * 4 + (2 * u + 2))
                            dve.tensor_reduce(negmax[:, u, :, 0], sc, AXX, ALU.max, negate=True).then_inc(at.maxed, 2)
                        value_bias(1)
                        for u in range(2):
                            dve.wait_ge(at.e_in, blk * 4 + (2 * u + 2))
                            dve.reciprocal(rinv[:, u, :, 0], rowsum[:, u, :, 0]).then_inc(inv, 1)
                            dve.wait_ge(inv, blk * 2 + (u + 1))
                            dve.wait_ge(o_full, blk * 2 + (u + 1))
                            for t in range(2):
                                ins = dve.scalar_tensor_tensor(ts4[:, 2 * u + t, :], ps[:, 6 + u, t * D:(t + 1) * D], rinv[:, u, t, 0:1],
                                                               rowsA[:, 1, :], ALU.mult, ALU.add)
                            ins.then_inc(o_in, 1)
                        dve.wait_ge(o_in, blk * 2 + 2)
                        tp = lambda t: ts4[:, t, :]
                        post.statistics(dve, blk, 0, tp)
                        dve.wait_ge(pre, blk + 1)
                        xp = x_tile(blk)
                        post.add_scaled(dve, blk, 0, tp, rowsA[:, 2, :], xp)
                        dve.wait_ge(post.link, post.done(blk, 0))
                        nrm.statistics(dve, blk, 0, xp)
                        wait(dve, n_full, blk * 2)
                        wait(dve, copied, blk)
                        nrm.result(dve, blk, 0, lambda t: xs4[:, t, :], xp)
                    for j in range(4):
                        q = slice(j * 1024, (j + 1) * 1024)
                        dve.wait_ge(w_hi, j + 1)
                        dve.tensor_tensor(wbuf_r[LAST_LOAD[0]][:, q], wbuf[:, LAST_LOAD[0], q], wbuf_r[1][:, q], ALU.subtract).then_inc(w_lo, 1)
                    dve.wait_ge(w_lo, 4)

                @block.tensor
                def _(pe):
                    def norm_T(blk):
                        pe.wait_ge(nrm.link, nrm.done(blk, 0))
                        for u in range(2):
                            transpose_pair(pe, 6 + u, xs4[:, 2 * u:2 * u + 2, :]).then_inc(n_full, 1)

                    def body(blk, first):
                        for j in range(4):
                            m = j % 2
                            w, src = (wq, xnT) if j < 2 else (wk, ctxT)
                            for k in range(KD):
                                ins = pe.matmul(ps[:, j, :], w[:, k, m * P:(m + 1) * P], src[:, k, ds(blk * BLK, BLK)],
                                                start=(k == 0), stop=(k == KD - 1))
                            ins.then_inc(q_full, 1)
                        pe.wait_ge(staged, blk + 1)
                        wait(pe, c_in, blk * 2)
                        def values(u):
                            for t in range(2):
                                for k in range(KD):
                                    ins = pe.matmul(ps[:, 4 + u, t * D:(t + 1) * D], stage[:, k, (2 * u + t) * P:(2 * u + t + 1) * P], wv[:, k, :],
                                                    start=(k == 0), stop=(k == KD - 1))
                            ins.then_inc(v_full, 1)

                        values(0)
                        pe.wait_ge(q_in, blk * 4 + 4)
                        at.scores(pe, blk)
                        values(1)
                        if not first:
                            norm_T(blk - 1)
                            pe.wait_ge(xT_in, blk * 2)
                        at.turn(pe, blk)
                        pe.wait_ge(v_in, blk * 2 + 2)
                        for u in range(2):
                            pe.wait_ge(at.p_in, blk * 2 + (u + 1))
                            for m in range(KD):
                                for kt in range(2):
                                    ins = pe.matmul(ps[:, 4 + u, m * SEQ:(m + 1) * SEQ], vtok[:, 2 * u + kt, m * P:(m + 1) * P],
                                                    probT[:, u, kt, :], start=(kt == 0), stop=(kt == 1))
                            ins.then_inc(c_full, 1)
                        for u in range(2):
                            pe.wait_ge(c_in, blk * 2 + (u + 1))
                            for t in range(2):
                                for m in range(KD):
                                    ins = pe.matmul(ps[:, 6 + u, t * D:(t + 1) * D], probT[:, 2 + u, m, t * P:(t + 1) * P], wo[:, m, :],
                                                    start=(m == 0), stop=(m == 1))
                            ins.then_inc(o_full, 1)

                    pe.wait_ge(ld_att[1], 32)
                    blocks(pe, body, norm_T)

        def phase_last():
            n = "L3f_"
            sl, _ = LAST_LOAD
            x_hi = psem(n + "x_hi")
            x_lo = psem(n + "x_lo")
            hid_hi, hid_lo = psem(n + "hid_hi"), psem(n + "hid_lo")
            w_part = [[wbuf_r[i][:, j * 2048:(j + 1) * 2048] for j in range(2)] for i in (1, sl)]
            (hi1, lo1) = (x[0].rearrange("p (k f) -> p k f", k=KD) for x in w_part)
            (hi2, lo2) = (x[1].rearrange("p (f d) -> p f d", f=NF) for x in w_part)
            hh, hl = (x.rearrange("p (f t) -> p f t", f=NF) for x in (wbuf_r[2], hbuf_r))
            h_full, h_in = psem(n + "h_full"), psem(n + "h_in")
            y_full, y_in = psem(n + "y_full"), psem(n + "y_in")
            scaled = psem(n + "scaled")
            pre = psem(n + "pre")
            post = Norm(n + "post", 2)

            with nc.Block() as block:
                @block.sync
                def _(sp):
                    rows_out = out.rearrange("(t p) d -> p t d", p=P)
                    with sp.Fori(0, NB) as blk:
                        for u in range(2):
                            sp.wait_ge(post.link, post.done(blk, u))
                            sp.dma_start(rows_out[:, ds(blk * 4 + 2 * u, 2), :], x_tok[:, ds(blk * 4 + 2 * u, 2), :]).then_inc(stored, 16)
                    sp.wait_ge(stored, 2 * NB * 16)

                @block.gpsimd
                def _(pool):
                    def add_rows(blk):
                        for x, row in ((xn_tok, 0), (x_tok, 2)):
                            x4 = x[:, ds(blk * 4, 4), :]
                            pool.tensor_tensor(x4, x4, rowsF[:, row, :].unsqueeze(1).broadcast_to([P, 4, D]), ALU.add).then_inc(pre, 1)

                    def body(blk, last):
                        if not last:
                            add_rows(blk + 1)
                        for u in range(2):
                            post.power(pool, blk, u)

                    pool.wait_ge(scaled, 1)
                    add_rows(0)
                    with pool.Fori(0, NB - 1) as blk:
                        body(blk, False)
                    body(NB - 1, True)

                @block.scalar
                def _(act):
                    def high(blk):
                        b = ds(blk * BLK, BLK)
                        act.activation(ctxT_r[:, :, b], xnT[:, :, b], ACT.Identity).then_inc(x_hi, 1)

                    def body(blk, last):
                        for f in range(NF):
                            act.wait_ge(h_full, blk * NF + (f + 1))
                            act.activation(hT[:, f, :], ps[:, f % 4, :], ACT.Relu, bias=col("L3_b1", f)).then_inc(h_in, 1)
                            act.wait_ge(h_in, blk * NF + (f + 1))
                            act.activation(hh[:, f, :], hT[:, f, :], ACT.Identity).then_inc(hid_hi, 1)
                        if not last:
                            high(blk + 1)

                    high(0)
                    with act.Fori(0, NB - 1) as blk:
                        body(blk, False)
                    body(NB - 1, True)

                @block.vector
                def _(dve):
                    dve.wait_ge(ld_rowsF, 32)
                    dve.tensor_scalar(rowsF[:, 1:3, :], rowsF[:, 1:3, :], gate(4 + 3), None, ALU.mult).then_inc(scaled, 1)
                    dve.wait_ge(scaled, 1)
                    def low(blk):
                        b = ds(blk * BLK, BLK)
                        dve.wait_ge(x_hi, blk + 1)
                        dve.tensor_tensor(xnT_r[:, :, b], xnT[:, :, b], ctxT_r[:, :, b], ALU.subtract).then_inc(x_lo, 1)

                    def body(blk, last):
                        for f in range(NF):
                            dve.wait_ge(hid_hi, blk * NF + (f + 1))
                            dve.tensor_tensor(hl[:, f, :], hT[:, f, :], hh[:, f, :], ALU.subtract).then_inc(hid_lo, 1)
                        if not last:
                            low(blk + 1)
                        dve.wait_ge(pre, blk * 2 + 2)
                        for u in range(2):
                            dve.wait_ge(y_full, blk * 2 + (u + 1))
                            dve.tensor_tensor(ts[:, :, :], ps[:, 4 + u, :].rearrange("p (t d) -> p t d", t=2),
                                              xn_tok[:, ds(blk * 4 + 2 * u, 2), :], ALU.add).then_inc(y_in, 1)
                            dve.wait_ge(y_in, blk * 2 + (u + 1))
                            tp = lambda t: ts[:, t, :]
                            post.statistics(dve, blk, u, tp)
                            xp = x_pair(blk, u)
                            post.add_scaled(dve, blk, u, tp, rowsF[:, 1, :], lambda t: xp(t)[:, 0, :])
                            dve.wait_ge(post.link, post.done(blk, u))

                    low(0)
                    with dve.Fori(0, NB - 1) as blk:
                        body(blk, False)
                    body(NB - 1, True)

                @block.tensor
                def _(pe):
                    with pe.Fori(0, NB) as blk:
                        b = ds(blk * BLK, BLK)
                        pe.wait_ge(x_lo, blk + 1)
                        for f in range(NF):
                            if f >= 4:
                                pe.wait_ge(h_in, blk * NF + (f - 3))
                            for k in range(KD):
                                for i, (m, x) in enumerate(((hi1, ctxT_r), (hi1, xnT_r), (lo1, ctxT_r))):
                                    ins = pe.matmul(ps[:, f % 4, :], m[:, k, f * P:(f + 1) * P], x[:, k, b],
                                                    start=(k == 0 and i == 0), stop=(k == KD - 1 and i == 2))
                            ins.then_inc(h_full, 1)
                        for u in range(2):
                            wait(pe, y_in, blk * 2)
                            for t in range(2):
                                for f in range(NF):
                                    if u == 0 and t == 0:
                                        pe.wait_ge(hid_lo, blk * NF + (f + 1))
                                    for i, (h, m) in enumerate(((hh, hi2), (hh, lo2), (hl, hi2))):
                                        ins = pe.matmul(ps[:, 4 + u, t * D:(t + 1) * D], h[:, f, (2 * u + t) * P:(2 * u + t + 1) * P],
                                                        m[:, f, :], start=(f == 0 and i == 0), stop=(f == NF - 1 and i == 2))
                            ins.then_inc(y_full, 1)

        LAST_LOAD = (0, 2)

        def during_ffn0(sp):
            sp.dma_start(attw[:, 1, 3], a["L1_wo"].rearrange("(k p) n -> p k n", p=P)).then_inc(ld_att[1], 16)
            load_rows(sp, rowsA, "attn1", ld_rowsA)

        def during_ffn1(sp):
            load_rows(sp, rowsA, "attn2", ld_rowsA)
            load_att(sp, 0, 1)
            load_att(sp, 1, 2)
            sp.dma_start(mask8, a["mask"].rearrange("(t p) k -> p t k", p=P)).then_inc(ld_mask, 16)

        def during_ffn2(sp):
            load_rows(sp, rowsA, "attn3", ld_rowsA)
            load_rows(sp, rowsF, "ffn3", ld_rowsF)

        def during_attn3(sp):
            load_expert(sp, LAST_LOAD[0], a["L3_w1"], a["L3_w2"])

        phase_setup()
        end_phase()
        phase_heads(0, lambda sp: None)
        end_phase()
        phase_experts(0, ACT.Relu, 4, False, during_ffn0)
        end_phase()
        phase_heads(1, lambda sp: None)
        end_phase()
        phase_experts(1, ACT.Gelu, 5, True, during_ffn1)
        end_phase()
        phase_linear(lambda sp: None)
        end_phase()
        phase_trees(during_ffn2)
        end_phase()
        phase_padded(during_attn3)
        end_phase()
        phase_last()


def tree_records(v):
    import numpy as np
    out = []
    for t in "qkv":
        w1 = v[f"L2_ffn_{t}_w1"].reshape(NPAIR, 2, KD, P, LEAFW).transpose(0, 3, 2, 1, 4).reshape(NPAIR, P, D)
        out.append(np.concatenate([w1, v[f"L2_ffn_{t}_w2"].reshape(NPAIR, P, D), v[f"L2_ffn_{t}_b1"].reshape(NPAIR, P, 1)], axis=2))
    return np.concatenate(out)


def tree_biases(v):
    import numpy as np
    out = np.zeros((TREES, NPAIR, NFLAG, D), np.float32)
    for r, t in enumerate("qkv"):
        out[r, :, 2 * r:2 * r + 2] = v[f"L2_ffn_{t}_b2"].reshape(NPAIR, 2, D)
    return out.reshape(TREES * NPAIR, NFLAG, D)


def leaf_masks():
    import numpy as np
    out = np.zeros((NFLAG, TREES, 2, LEAFW), np.float32)
    for r in range(TREES):
        for leaf in range(2):
            out[2 * r + leaf, r, 1 - leaf] = -BIG
    return out.reshape(NFLAG, TREES * P)


def kernel(**inputs):
    import numpy as np
    import concourse.bacc as bacc
    from concourse.bass_utils import run_bass_kernel_spmd

    v = {k: np.asarray(x) for k, x in inputs.items()}

    def colsof(x, n):
        return x.reshape(n, P).T

    arrays = {
        "x": v["x"].reshape(T, D), "ctx": v["ctx_1024"].reshape(T, D),
        "mask": v["mask_Bx1xSxS2_bf0"].reshape(T, SEQ), "pad": v["mask_Bx1xS2_ik1"].reshape(T),
        "g": np.concatenate([v["g_xattn"], v["g_ffn"]]),
        "attw": np.stack([np.stack([v[f"L0_xattn_{w}"] for w in ("Wq", "Wk", "Wv", "Wo")]),
                          np.stack([v[f"L2_xattn_{w}"].T for w in ("wq_w", "wk_w", "wv_w", "wo_w")]),
                          np.stack([v[f"L3_xattn_{w}"] for w in ("Wq", "Wk", "Wv", "Wo")])]),
        "L1_wo": v["L1_xattn_Wo"].T,
        "rep": np.stack([np.tile(v[f"L1_xattn_{w}"].T, (GH, 1)) for w in ("Wq", "Wk", "Wv")], axis=1),
        "L0_w1": np.concatenate([v["L0_ffn_W1"], v["L0_ffn_Ws1"][None]]),
        "L0_w2": np.concatenate([v["L0_ffn_W2"], v["L0_ffn_Ws2"][None]]),
        "L1_w1": v["L1_ffn_W1"], "L1_w2": v["L1_ffn_W2"],
        "L0_b1r": v["L0_ffn_b1"].reshape(E0 - 1, NF, P).transpose(0, 2, 1), "L0_b2": v["L0_ffn_b2"],
        "L1_b1r": v["L1_ffn_b1"].reshape(E1, NF, P).transpose(0, 2, 1), "L1_b2": v["L1_ffn_b2"],
        "L2_rec": tree_records(v), "L2_b2r": tree_biases(v), "leafm": leaf_masks(),
        "L3_w1": v["L3_ffn_w1"][0], "L3_w2": v["L3_ffn_w2"][0],
    }
    columns = {
        "L0_bq": v["L0_xattn_bq"], "L0_bk": v["L0_xattn_bk"],
        "L0_bs1": v["L0_ffn_bs1"],
        "L2_bq": v["L2_xattn_wq_b"],
        "L3_bq": v["L3_xattn_bq"], "L3_bk": v["L3_xattn_bk"], "L3_b1": v["L3_ffn_b1"][0],
    }
    arrays["cols"] = np.concatenate([colsof(columns[k], n) for k, (_, n) in COLS.items()], axis=1)
    arrays["rows"] = np.stack([
        v["L0_xattn_bv"], v["L0_xattn_bo"], v["L0_ffn_bs2"], v["L1_xattn_bo"],
        v["L2_xattn_wk_b"], v["L2_xattn_wv_b"], v["L2_xattn_wo_b"], v["L2_xattn_ln_g"], v["L2_xattn_ln_b"],
        v["L3_xattn_bv"], v["L3_xattn_bo"], v["L3_xattn_g0"], v["L3_xattn_beta0"],
        v["L3_ffn_b2"][0], v["L3_ffn_gamma"], v["L3_ffn_beta"]])
    gatew = np.concatenate([v["L0_ffn_Wg"], v["L1_ffn_Wg"], *[v[f"L2_ffn_{t}_node_w"].T for t in "qkv"]], axis=1)
    arrays["gatew"] = gatew.reshape(KD, P, NGATEW).transpose(1, 0, 2)
    arrays["small"] = np.concatenate([v["L1_ffn_bg"], *[v[f"L2_ffn_{t}_node_b"] for t in "qkv"]])

    nc = bacc.Bacc("TRN2", target_bir_lowering=False, num_devices=1)
    a, feed = {}, {}
    for name, x in arrays.items():
        feed["in_" + name] = np.ascontiguousarray(x)
        a[name] = nc.dram_tensor("in_" + name, x.shape, mybir.dt.from_np(x.dtype), kind="ExternalInput").ap()
    out = nc.dram_tensor("out_x", (T, D), F32, kind="ExternalOutput").ap()
    a["xg"] = nc.dram_tensor("expert_rows", (XROWS, D), F32).ap()
    for r in range(TREES):
        a[f"xt{r}"] = nc.dram_tensor(f"tree{r}_rows", (TSTEPS * SUB, ROW), F32).ap()
        a[f"yt{r}"] = nc.dram_tensor(f"tree{r}_outputs", (TSTEPS * SUB, D), F32).ap()
    a["yg"] = nc.dram_tensor("expert_outputs", (XROWS, D), F32).ap()
    decoder_kernel(nc, a, out)
    r = run_bass_kernel_spmd(nc, [feed], core_ids=[0])
    return r.results[0]["out_x"].reshape(NBATCH, SEQ, D)
```
